# Optimizing a Trainium2 kernel written in Bass

```python
import numpy as np
import jax
import jax.numpy as jnp

def _softmax(x, axis=-1):
    return jax.nn.softmax(x, axis=axis)

def _gelu(x):
    return jax.nn.gelu(x, approximate=True)

def _silu(x):
    return jax.nn.silu(x)

def _sigmoid(x):
    return jax.nn.sigmoid(x)

def _layernorm(x, axis=-1, eps=1e-05):
    m = jnp.mean(x, axis=axis, keepdims=True)
    v = jnp.var(x, axis=axis, keepdims=True)
    return (x - m) / jnp.sqrt(v + eps)

def _scatter_add(tgt, idx, src, axis=0):
    return tgt.at[idx].add(src)

def _segment_sum(src, seg, n):
    return jax.ops.segment_sum(src, seg, n)
kernel_name = 'mk_gnn_preln_d4_gnn_r16_bba598'

def setup_inputs(seed: int=0):
    np.random.seed(seed)
    _w = jnp.asarray

    def _rec_inputs():
        import jax
        import jax.numpy as jnp
        _gk = jax.random.key(seed)
        x = -0.0005121 + 1.001 * jax.random.normal(jax.random.fold_in(_gk, 1), (6250, 64), jnp.float32)
        src = jax.random.randint(jax.random.fold_in(_gk, 2), (200000,), 0, 6250, jnp.int32)
        dst = jnp.minimum((6250 * jax.random.uniform(jax.random.fold_in(_gk, 3), (200000,)) ** 2.0).astype(jnp.int32), 99999)
        _o = jnp.argsort(dst, stable=True)
        src = src[_o]
        dst = dst[_o]
        edge_attr_32 = -5.16925e-05 + 1.00005 * jax.random.normal(jax.random.fold_in(_gk, 13), (200000, 32), jnp.float32)
        edge_type_4 = jax.random.randint(jax.random.fold_in(_gk, 15), (200000,), 0, 4, jnp.int32)
        return (x, src, dst, edge_attr_32, edge_type_4)
    x, src, dst, edge_attr_32, edge_type_4 = _rec_inputs()

    def _L0_gnn_setup():
        import jax, jax.numpy as jnp
        import numpy as np
        N = 3125
        E = 50000
        H = 64
        K = 4
        STEPS = 4

        def _gru_cell(a, feat, w_ih, w_hh, b_ih, b_hh):
            gi = a @ w_ih.T + b_ih
            gh = feat @ w_hh.T + b_hh
            i_r, i_z, i_n = jnp.split(gi, 3, axis=-1)
            h_r, h_z, h_n = jnp.split(gh, 3, axis=-1)
            r = jax.nn.sigmoid(i_r + h_r)
            z = jax.nn.sigmoid(i_z + h_z)
            n = jnp.tanh(i_n + r * h_n)
            return (1.0 - z) * n + z * feat
        key = jax.random.key(seed)
        ks = jax.random.split(key, 10)
        s = 0.05
        return {'h': jax.random.normal(ks[0], (N, H), jnp.float32), 'W': jax.random.normal(ks[1], (K, H, H), jnp.float32) * s, 'b': jax.random.normal(ks[2], (K, H), jnp.float32) * s, 'w_ih': jax.random.normal(ks[3], (3 * H, H), jnp.float32) * s, 'w_hh': jax.random.normal(ks[4], (3 * H, H), jnp.float32) * s, 'b_ih': jax.random.normal(ks[5], (3 * H,), jnp.float32) * s, 'b_hh': jax.random.normal(ks[6], (3 * H,), jnp.float32) * s, 'src': jax.random.randint(ks[7], (E,), 0, N, dtype=jnp.int32), 'dst': jax.random.randint(ks[8], (E,), 0, N, dtype=jnp.int32), 'etypes': jax.random.randint(ks[9], (E,), 0, K, dtype=jnp.int32)}
    _L0_gnn_all = _L0_gnn_setup()
    _L0_gnn_in = {k: v for k, v in _L0_gnn_all.items() if k in ('W', 'b', 'w_ih', 'w_hh', 'b_ih', 'b_hh')}
    del _L0_gnn_all

    def _L1_gnn_setup():
        import jax, jax.numpy as jnp
        import numpy as np
        N_NODES = 3125
        N_EDGES = 50000
        IN_DIM = 64
        OUT_DIM = 64
        ALPHA = 0.2
        key = jax.random.key(seed)
        k1, k2, k3, k4 = jax.random.split(key, 4)
        x = jax.random.normal(k1, (N_NODES, IN_DIM), dtype=jnp.float32)
        edge_index = jax.random.randint(k2, (2, N_EDGES), 0, N_NODES, dtype=jnp.int64)
        W = jax.random.normal(k3, (OUT_DIM, IN_DIM), dtype=jnp.float32) * (1.0 / np.sqrt(IN_DIM))
        a = jax.random.normal(k4, (1, 2 * OUT_DIM), dtype=jnp.float32) * (1.0 / np.sqrt(2 * OUT_DIM))
        return {'x': x, 'edge_index': edge_index, 'W': W, 'a': a}
    _L1_gnn_all = _L1_gnn_setup()
    _L1_gnn_in = {k: v for k, v in _L1_gnn_all.items() if k in ('W', 'a')}
    del _L1_gnn_all

    def _L2_gnn_setup():
        import jax, jax.numpy as jnp
        import numpy as np
        N_SRC = 6250
        N_DST = 6250
        N_EDGES = 62500
        D = 64
        key = jax.random.key(seed)
        k1, k2, k3 = jax.random.split(key, 3)
        src_emb = jax.random.normal(k1, (N_SRC, D), dtype=jnp.float32)
        edge_src = jax.random.randint(k2, (N_EDGES,), 0, N_SRC, dtype=jnp.int64)
        edge_dst = jax.random.randint(k3, (N_EDGES,), 0, N_DST, dtype=jnp.int64)
        return {'src_emb': src_emb, 'edge_src': edge_src, 'edge_dst': edge_dst, 'num_dst': N_DST}
    _L2_gnn_all = _L2_gnn_setup()
    _L2_gnn_in = {k: v for k, v in _L2_gnn_all.items() if k in ()}
    del _L2_gnn_all

    def _L3_gnn_setup():
        import jax, jax.numpy as jnp
        import numpy as np
        N_NODES = 6250
        N_EDGES = 200000
        EDGE_OUT = 32
        HID = 128
        NODE_OUT = 64
        N_GRAPHS = 16
        key = jax.random.key(seed)
        ks = jax.random.split(key, 9)
        x = jax.random.normal(ks[0], (N_NODES, 64), dtype=jnp.float32)
        edge_index = jax.random.randint(ks[1], (2, N_EDGES), 0, N_NODES, dtype=jnp.int64)
        edge_attr = jax.random.normal(ks[2], (N_EDGES, EDGE_OUT), dtype=jnp.float32)
        u = jax.random.normal(ks[3], (N_GRAPHS, 1), dtype=jnp.float32)
        batch = jnp.sort(jax.random.randint(ks[4], (N_NODES,), 0, N_GRAPHS, dtype=jnp.int64))
        d_in = 3 * EDGE_OUT + 1
        W1 = jax.random.normal(ks[5], (d_in, HID), dtype=jnp.float32) / np.sqrt(d_in)
        b1 = jnp.zeros((HID,), dtype=jnp.float32)
        W2 = jax.random.normal(ks[6], (HID, NODE_OUT), dtype=jnp.float32) / np.sqrt(HID)
        b2 = jnp.zeros((NODE_OUT,), dtype=jnp.float32)
        return {'x': x, 'edge_index': edge_index, 'edge_attr': edge_attr, 'u': u, 'batch': batch, 'W1': W1, 'b1': b1, 'W2': W2, 'b2': b2}
    _L3_gnn_all = _L3_gnn_setup()
    _L3_gnn_in = {k: v for k, v in _L3_gnn_all.items() if k in ('u', 'W1', 'b1', 'W2', 'b2')}
    del _L3_gnn_all
    return {'x': x, 'src': src, 'dst': dst, 'edge_attr_32': edge_attr_32, 'edge_type_4': edge_type_4, 'L0_gnn_W': _L0_gnn_in['W'], 'L0_gnn_b': _L0_gnn_in['b'], 'L0_gnn_w_ih': _L0_gnn_in['w_ih'], 'L0_gnn_w_hh': _L0_gnn_in['w_hh'], 'L0_gnn_b_ih': _L0_gnn_in['b_ih'], 'L0_gnn_b_hh': _L0_gnn_in['b_hh'], 'L1_gnn_W': _L1_gnn_in['W'], 'L1_gnn_a': _L1_gnn_in['a'], 'L3_gnn_u': _L3_gnn_in['u'], 'L3_gnn_W1': _L3_gnn_in['W1'], 'L3_gnn_b1': _L3_gnn_in['b1'], 'L3_gnn_W2': _L3_gnn_in['W2'], 'L3_gnn_b2': _L3_gnn_in['b2']}

def reference(x, src, dst, edge_attr_32, edge_type_4, L0_gnn_W, L0_gnn_b, L0_gnn_w_ih, L0_gnn_w_hh, L0_gnn_b_ih, L0_gnn_b_hh, L1_gnn_W, L1_gnn_a, L3_gnn_u, L3_gnn_W1, L3_gnn_b1, L3_gnn_W2, L3_gnn_b2):
    import jax
    import jax.numpy as jnp

    def _L0_gnn_ref(h, W, b, w_ih, w_hh, b_ih, b_hh, src, dst, etypes):
        import jax, jax.numpy as jnp
        import numpy as np
        N = 3125
        E = 50000
        H = 64
        K = 4
        STEPS = 4

        def _gru_cell(a, feat, w_ih, w_hh, b_ih, b_hh):
            gi = a @ w_ih.T + b_ih
            gh = feat @ w_hh.T + b_hh
            i_r, i_z, i_n = jnp.split(gi, 3, axis=-1)
            h_r, h_z, h_n = jnp.split(gh, 3, axis=-1)
            r = jax.nn.sigmoid(i_r + h_r)
            z = jax.nn.sigmoid(i_z + h_z)
            n = jnp.tanh(i_n + r * h_n)
            return (1.0 - z) * n + z * feat
        num_nodes = h.shape[0]

        def step(feat, _):
            transformed = jnp.einsum('nd,khd->knh', feat, W) + b[:, None, :]
            msgs = transformed[etypes, src]
            a = jax.ops.segment_sum(msgs, dst, num_segments=num_nodes)
            feat = _gru_cell(a, feat, w_ih, w_hh, b_ih, b_hh)
            return (feat, None)
        feat, _ = jax.lax.scan(step, h, None, length=STEPS)
        return feat

    def _L1_gnn_ref(x, edge_index, W, a):
        import jax, jax.numpy as jnp
        import numpy as np
        N_NODES = 3125
        N_EDGES = 50000
        IN_DIM = 64
        OUT_DIM = 64
        ALPHA = 0.2
        num_nodes = x.shape[0]
        h = x @ W.T
        src, dst = (edge_index[0], edge_index[1])
        a_src = a[0, :OUT_DIM]
        a_dst = a[0, OUT_DIM:]
        e = jax.nn.leaky_relu(h[src] @ a_src + h[dst] @ a_dst, ALPHA)
        seg_max = jax.ops.segment_max(e, src, num_segments=num_nodes)
        exp_e = jnp.exp(e - seg_max[src])
        denom = jax.ops.segment_sum(exp_e, src, num_segments=num_nodes)
        attention = exp_e / denom[src]
        h_prime = jax.ops.segment_sum(attention[:, None] * h[src], dst, num_segments=num_nodes)
        return jax.nn.elu(h_prime)

    def _L2_gnn_ref(src_emb, edge_src, edge_dst, num_dst):
        import jax, jax.numpy as jnp
        import numpy as np
        N_SRC = 6250
        N_DST = 6250
        N_EDGES = 62500
        D = 64
        messages = src_emb[edge_src]
        dst_emb = jax.ops.segment_sum(messages, edge_dst, num_segments=num_dst)
        return dst_emb

    def _L3_gnn_ref(x, edge_index, edge_attr, u, batch, W1, b1, W2, b2):
        import jax, jax.numpy as jnp
        import numpy as np
        N_NODES = 6250
        N_EDGES = 200000
        EDGE_OUT = 32
        HID = 128
        NODE_OUT = 64
        N_GRAPHS = 16
        N = x.shape[0]
        row = edge_index[0]
        seg_sum = jax.ops.segment_sum(edge_attr, row, num_segments=N)
        seg_max = jax.ops.segment_max(edge_attr, row, num_segments=N)
        cnt = jax.ops.segment_sum(jnp.ones((edge_attr.shape[0], 1), edge_attr.dtype), row, num_segments=N)
        seg_mean = seg_sum / jnp.maximum(cnt, 1.0)
        seg_max = jnp.where(cnt > 0, seg_max, 0.0)
        h = jnp.concatenate([seg_sum, seg_max, seg_mean, u[batch]], axis=1)
        h = jax.nn.relu(h @ W1 + b1)
        return h @ W2 + b2
    edge_index = jnp.stack([src, dst])
    batch0 = jnp.zeros((6250,), jnp.int32)
    h = jnp.maximum(_layernorm(x, axis=-1), 0.0)
    x = x + _L0_gnn_ref(h, L0_gnn_W, L0_gnn_b, L0_gnn_w_ih, L0_gnn_w_hh, L0_gnn_b_ih, L0_gnn_b_hh, src, dst, edge_type_4)
    h = jnp.maximum(_layernorm(x, axis=-1), 0.0)
    x = x + _L1_gnn_ref(h, edge_index, L1_gnn_W, L1_gnn_a)
    h = jnp.maximum(_layernorm(x, axis=-1), 0.0)
    x = x + _L2_gnn_ref(h, src, dst, 6250)
    h = jnp.maximum(_layernorm(x, axis=-1), 0.0)
    x = x + _L3_gnn_ref(h, edge_index, edge_attr_32, L3_gnn_u, batch0, L3_gnn_W1, L3_gnn_b1, L3_gnn_W2, L3_gnn_b2)
    return x

_drawn_inputs = setup_inputs


def setup_inputs(seed=0):
    import zlib

    import numpy as np

    out = dict(_drawn_inputs(seed))
    spreads = {'L3_gnn_b1': (0.0, 2.0), 'L3_gnn_b2': (0.0, 2.0)}
    factors = {'L0_gnn_b_hh': 2.818, 'L1_gnn_a': 6.761, 'L3_gnn_u': 30.158}
    for name, (base, spread) in spreads.items():
        noise = np.random.default_rng([zlib.crc32(name.encode()), seed]).standard_normal(out[name].shape)
        drawn = base * np.exp(spread * noise) if base else spread * noise
        out[name] = jnp.asarray(drawn.astype(out[name].dtype))
    for name, factor in factors.items():
        out[name] = (out[name] * factor).astype(out[name].dtype)
    return out
```

```python
import concourse.bass as bass
from concourse import mybir
from contextlib import ExitStack
from itertools import count
from math import prod

F32 = mybir.dt.float32
I32 = mybir.dt.int32
ALU = mybir.AluOpType
ACT = mybir.ActivationFunctionType
AX = mybir.AxisListType

P = 128
N = 6250
NBR = -(-N // P)
NB = 50
NP = NB * P
D = 64
FA = 32
KT = 4
STEPS = 4
E = 200000
EP = 125
EC = E // EP
GK = 13
T = 1612
GI = T // (2 * GK)
SK = 10
SI = EC // (2 * SK)
LOT = 5
NL = NB // LOT
SLAB = 100
HID = 128
REC_W = 4
SRT_W = FA + 2
BIG = 3.4028234663852886e38
NO_NODE = 255.0
assert (E + NBR * (P - 1)) // P <= T and EP * EC == E and T % (2 * GK) == 0 and EC % (2 * SK) == 0


class Chain:

    def __init__(self, eng, sem):
        self.eng, self.sem, self.n, self.base = eng, sem, 0, 0

    def __call__(self, ins):
        self.n += 1
        ins.then_inc(self.sem, 1)
        self.eng.wait_ge(self.sem, self.base + self.n)

    def enter(self, i, per):
        self.base, self.n, self.per = self.base + self.n + i * per, 0, per
        self.after = None

    def leave(self, base0, turns):
        assert self.n == self.per, (self.n, self.per)
        self.base, self.n = base0 + turns * self.per, 0


def build(nc, x, src, dst, attr, etype, W0, b0, wih, whh, bih, bhh, W1g, a1, u3, W13, b13, W23, b23, out):
    top = ExitStack()

    class Phase(ExitStack):

        def __init__(self):
            super().__init__()
            self.held = []
            self.callback(self.tidy)

        def tidy(self):
            for s in self.held:
                nc.gpsimd.sem_clear(s)
            nc.all_engine_barrier()
            for s in self.held:
                nc.release_semaphore(s)

    def sems(st, *names):
        made_here = [nc.alloc_semaphore(n) for n in names]
        st.held += made_here
        return made_here

    def dma_sems(*names):
        return [nc.alloc_semaphore(n) for n in names]

    made = count()

    def sb(st, name, shape, dt=F32):
        return st.enter_context(nc.sbuf_tensor(f"{name}_{next(made)}", shape, dt))

    ps_all = top.enter_context(nc.psum_tensor("ps_all", [P, 8 * 512], F32))
    bank = [0]

    def pb(st, shape):
        size = prod(shape[1:])
        at = bank[0]
        bank[0] += -(-size // 512)
        assert bank[0] <= 8
        st.callback(bank.__setitem__, 0, at)
        view = ps_all[0:shape[0], at * 512:at * 512 + size]
        return view.rearrange("p (a b) -> p a b", a=shape[1]) if len(shape) == 3 else view

    def along(ap, n):
        p, k = ap.shape
        return ap.rearrange("p (k a) -> p k a", a=1).broadcast_to((p, k, n))

    def across(ap, k):
        p, n = ap.shape
        return ap.rearrange("p (a n) -> p a n", a=1).broadcast_to((p, k, n))

    with top:
        rec_d = nc.dram_tensor("rec_d", (P, T * REC_W), I32).ap()
        msg_d = nc.dram_tensor("msg_d", (NP * KT, D), F32).ap()
        row_d = nc.dram_tensor("row_d", (NP, D), F32).ap()
        srt_d = nc.dram_tensor("srt_d", (E, SRT_W), F32).ap()
        seg_d = nc.dram_tensor("seg_d", (E, 2 * FA), F32).ap()
        mxd_d = nc.dram_tensor("mxd_d", (E, 1), F32).ap()

        iota = sb(top, "iota", [P, P])
        ident = sb(top, "ident", [P, P])
        tri = sb(top, "tri", [P, P])
        ones = sb(top, "ones", [P, P])
        zero = sb(top, "zero", [P, 512])
        src4 = sb(top, "src4", [P, T], I32)
        srcr = sb(top, "srcr", [P, T], I32)
        dlo = sb(top, "dlo", [P, T])
        dful = sb(top, "dful", [P, T])
        wgt = sb(top, "wgt", [P, T])
        blk64 = sb(top, "blk64", [1, T], I32)
        st_src = sb(top, "st_src", [P, NB])
        cn_src = sb(top, "cn_src", [P, NB])

        with Phase() as ph:
            (s_c, s_tri, s_ld, s_cnt, s_cs, s_base, s_bt, s_ge, s_br, s_df, s_v, s_z) = sems(
                ph, "a_const", "a_tri", "a_load", "a_counts", "a_sums", "a_starts", "a_startsT", "a_reached",
                "a_blocks", "a_defaults", "a_dve", "a_zero")
            (s_def,) = sems(ph, "a_stored")
            dstI = sb(ph, "dstI", [EP, EC], I32)
            srcI = sb(ph, "srcI", [EP, EC], I32)
            etI = sb(ph, "etI", [EP, EC], I32)
            tmpI = sb(ph, "tmpI", [EP, EC], I32)
            posI = sb(ph, "posI", [EP, EC], I32)
            pay = sb(ph, "pay", [EP, EC, REC_W], I32)
            cnt = sb(ph, "cnt", [EP, NB])
            pre = sb(ph, "pre", [EP, NB])
            tot = sb(ph, "tot", [P, NB])
            totI = sb(ph, "totI", [P, NB], I32)
            nch = sb(ph, "nch", [P, NB])
            cs = sb(ph, "cs", [P, NB])
            base = sb(ph, "base", [P, NB])
            csT = sb(ph, "csT", [NBR, 1])
            posF2 = sb(ph, "posF2", [EP, T])
            posI2 = sb(ph, "posI2", [EP, EC], I32)
            ends = sb(ph, "ends", [EP, EC, 2])
            with Phase() as p0:
                hiF = sb(p0, "hiF", [EP, EC])
                m = sb(p0, "m", [EP, EC])
                c = sb(p0, "c", [EP, EC])
                q = sb(p0, "q", [EP, EC])
                zr = sb(p0, "zr", [EP, EC])
                posF = sb(p0, "posF", [EP, EC])
                dflt = sb(p0, "dflt", [P, T, REC_W], I32)
                ioT = sb(p0, "ioT", [NBR, T])
                reach = sb(p0, "reach", [NBR, T])
                ps = pb(p0, [P, 2, 512])
                psb = pb(p0, [1, 4, 512])
                block = p0.enter_context(nc.Block())

                @block.gpsimd
                def _(pool):
                    pool.iota(iota[:, :], [[1, P]], base=0, channel_multiplier=0,
                              allow_small_or_imprecise_dtypes=True).then_inc(s_c, 1)
                    pool.iota(ioT[:, :], [[1, T]], base=0, channel_multiplier=0,
                              allow_small_or_imprecise_dtypes=True).then_inc(s_c, 1)
                    pool.memset(ident[:, :], 0.0).then_inc(s_tri, 1)
                    pool.memset(ones[:, :], 1.0).then_inc(s_tri, 1)
                    pool.wait_ge(s_tri, 2)
                    pool.affine_select(out=ident[:, :], in_=ident[:, :], compare_op=ALU.not_equal, fill=1.0, base=0,
                                       pattern=[[-1, P]], channel_multiplier=1).then_inc(s_c, 1)
                    pool.affine_select(out=tri[:, :], in_=ones[:, :], compare_op=ALU.is_gt, fill=0.0, base=0,
                                       pattern=[[1, P]], channel_multiplier=-1).then_inc(s_c, 1)

                @block.sync
                def _(sp):
                    for tile, a in ((dstI, dst), (srcI, src), (etI, etype)):
                        sp.dma_start(tile[:, :], a.rearrange("(p c) -> p c", p=EP)).then_inc(s_ld, 16)
                    sp.wait_ge(s_df, 2)
                    sp.dma_start(rec_d, dflt[:, :, :].rearrange("p t w -> p (t w)")).then_inc(s_def, 16)
                    sp.wait_ge(s_def, 16)

                @block.vector
                def _(dve):
                    link = Chain(dve, s_v)
                    dve.memset(zero[:, :], 0.0).then_inc(s_z, 1)
                    link(dve.memset(dflt[:, :, :], 0))
                    dve.memset(dflt[:, :, 2], int(NO_NODE)).then_inc(s_df, 2)
                    dve.memset(zr[:, :], 0.0)
                    dve.memset(posF[:, :], 0.0)
                    link(dve.memset(cnt[:, :], 0.0))
                    dve.wait_ge(s_ld, 48)
                    dve.wait_ge(s_c, 4)
                    dve.tensor_scalar(pay[:, :, 2], dstI[:, :], P - 1, None, ALU.bitwise_and)
                    dve.tensor_copy(pay[:, :, 3], dstI[:, :])
                    dve.tensor_copy(pay[:, :, 1], srcI[:, :])
                    dve.scalar_tensor_tensor(pay[:, :, 0], srcI[:, :], float(KT), etI[:, :], ALU.mult, ALU.add)
                    link(dve.tensor_scalar(tmpI[:, :], dstI[:, :], 7, None, ALU.arith_shift_right))
                    link(dve.tensor_copy(hiF[:, :], tmpI[:, :]))
                    with dve.Fori(0, NBR) as b:
                        dve.tensor_scalar(m[:, :], hiF[:, :], iota[0:EP, bass.ds(b, 1)], None, ALU.is_equal, ALU.add,
                                          accum_out=cnt[:, bass.ds(b, 1)]).then_inc(s_cnt, 1)
                        dve.wait_ge(s_cnt, b + 1)
                    dve.wait_ge(s_cs, 1)
                    link(dve.tensor_scalar(totI[:, :], ps[:, 1, 0:NB], float(P - 1), None, ALU.add))
                    dve.tensor_copy(pre[:, :], ps[0:EP, 0, 0:NB])
                    link(dve.tensor_scalar(totI[:, :], totI[:, :], 7, None, ALU.arith_shift_right))
                    link(dve.tensor_copy(nch[:, :], totI[:, :]))
                    link(dve.tensor_tensor_scan(cs[:, :], nch[:, :], zero[:, 0:NB], 0.0, ALU.add, ALU.add))
                    dve.tensor_tensor(cs[:, :], cs[:, :], nch[:, :], ALU.subtract).then_inc(s_base, 1)
                    dve.wait_ge(s_base, 1)
                    link(dve.scalar_tensor_tensor(base[0:EP, :], cs[0:EP, :], float(P), pre[:, :], ALU.mult, ALU.add))
                    link(dve.tensor_scalar(base[0:EP, :], base[0:EP, :], 1.0, None, ALU.subtract))
                    dve.wait_ge(s_bt, 1)
                    link(dve.tensor_copy(csT[:, :], ps[0:NBR, 0, 0:1]))
                    dve.tensor_scalar(reach[:, :], ioT[:, :], csT[:, 0:1], None, ALU.is_ge).then_inc(s_ge, 1)
                    n0 = link.base + link.n
                    with dve.Fori(0, NBR) as b:
                        link.enter(b, 4)
                        link(dve.tensor_scalar(m[:, :], hiF[:, :], iota[0:EP, bass.ds(b, 1)], None, ALU.is_equal))
                        link(dve.tensor_tensor_scan(c[:, :], m[:, :], zr[:, :], 0.0, ALU.add, ALU.add))
                        link(dve.scalar_tensor_tensor(q[:, :], c[:, :], base[0:EP, bass.ds(b, 1)], m[:, :],
                                                      ALU.add, ALU.mult))
                        link(dve.tensor_tensor(posF[:, :], posF[:, :], q[:, :], ALU.add))
                    link.leave(n0, NBR)
                    link(dve.tensor_copy(posI[:, :], posF[:, :]))
                    dve.tensor_scalar(tmpI[:, :], posI[:, :], P - 1, None, ALU.bitwise_and)
                    link(dve.tensor_scalar(posI[:, :], posI[:, :], 7, None, ALU.arith_shift_right))
                    dve.tensor_copy(c[:, :], tmpI[:, :])
                    link(dve.tensor_copy(q[:, :], posI[:, :]))
                    link(dve.scalar_tensor_tensor(posI[:, :], c[:, :], float(T), q[:, :], ALU.mult, ALU.add))
                    dve.wait_ge(s_br, 1)
                    link(dve.tensor_scalar(blk64[:, :].rearrange("a (k n) -> a k n", k=4), psb[:, :, 0:T // 4],
                                           1.0, float(D), ALU.subtract, ALU.mult))

                @block.tensor
                def _(pe):
                    pe.wait_ge(s_cnt, NBR)
                    pe.wait_ge(s_c, 4)
                    pe.matmul(ps[0:EP, 0, 0:NB], tri[0:EP, 0:EP], cnt[:, :], start=True, stop=True)
                    pe.matmul(ps[:, 1, 0:NB], ones[0:EP, :], cnt[:, :], start=True, stop=True).then_inc(s_cs, 1)
                    pe.wait_ge(s_base, 1)
                    pe.matmul(ps[0:NBR, 0, 0:1], cs[0:1, 0:NBR], ones[0:1, 0:1], start=True, stop=True).then_inc(s_bt, 1)
                    pe.wait_ge(s_ge, 1)
                    for k in range(4):
                        last = pe.matmul(psb[:, k, 0:T // 4], ones[0:NBR, 0:1], reach[:, k * (T // 4):(k + 1) * (T // 4)],
                                         start=True, stop=True)
                    last.then_inc(s_br, 1)

            with Phase() as p1:
                s_st = sems(p1, "b_staged0", "b_staged1")
                s_sc = dma_sems("b_scattered0", "b_scattered1")
                s_hm = sems(p1, "b_hmarks0", "b_hmarks1")
                s_hu = sems(p1, "b_hused0", "b_hused1")
                s_rm = sems(p1, "b_rmarks0", "b_rmarks1")
                (s_tick, s_v, s_key, s_sum, s_hst, s_tot, s_first, s_T, s_cT, s_E, s_M, s_U, s_cH, s_L, s_R) = sems(
                    p1, *("b_" + n for n in ("tick", "dve", "keys", "sums", "histogram", "totals", "first", "turned",
                                             "turnedsb", "equal", "earlier", "counted", "countsb", "looked", "ranked")))
                posS = [sb(p1, f"posS{h}", [EP, SK], I32) for h in range(2)]
                payS = [sb(p1, f"payS{h}", [EP, SK, REC_W], I32) for h in range(2)]
                slo = sb(p1, "slo", [EP, T])
                shi = sb(p1, "shi", [EP, T])
                lo = [sb(p1, f"lo{h}", [EP, GK, P]) for h in range(2)]
                hi = [sb(p1, f"hi{h}", [EP, GK, NB]) for h in range(2)]
                lT = [sb(p1, f"lT{k}", [P, EP]) for k in range(2)]
                eq = [sb(p1, f"eq{k}", [EP, EP]) for k in range(2)]
                hs = sb(p1, "hs", [P, NB])
                off = sb(p1, "off", [P, NB])
                junk = sb(p1, "junk", [EP, NB])
                ptt = [pb(p1, [P, 512]) for k in range(2)]
                peq = [pb(p1, [P, 512]) for k in range(2)]
                plk = [pb(p1, [P, 512]) for k in range(2)]
                pcn = pb(p1, [P, 512])
                ptm = pb(p1, [P, 512])
                block = p1.enter_context(nc.Block())

                @block.sync
                def _(sp):
                    def stage(h, at):
                        sp.dma_start(posS[h][:, :], posI[:, bass.ds(at, SK)]).then_inc(s_st[h], 16)
                        sp.dma_start(payS[h][:, :, :], pay[:, bass.ds(at, SK), :]).then_inc(s_st[h], 16)
                    for h in range(2):
                        stage(h, h * SK)
                    with sp.Fori(1, SI) as i:
                        for h in range(2):
                            sp.wait_ge(s_sc[h], i * (16 * SK))
                            stage(h, i * (2 * SK) + h * SK)

                @block.gpsimd
                def _(pool):
                    with pool.Fori(0, SI) as i:
                        for h in range(2):
                            pool.wait_ge(s_st[h], (i + 1) * 32)
                            pool.sem_inc(s_tick, 1)
                            for j in range(SK):
                                pool.indirect_dma_start(
                                    rec_d.rearrange("p (t w) -> (p t) w", w=REC_W),
                                    bass.IndirectOffsetOnAxis(posS[h][:, j:j + 1], 0),
                                    payS[h][:, j, :], None).then_inc(s_sc[h], 16)
                    for h in range(2):
                        pool.wait_ge(s_sc[h], 16 * SK * SI)

                @block.vector
                def _(dve):
                    link = Chain(dve, s_v)
                    dve.memset(slo[:, :], NO_NODE)
                    dve.memset(shi[:, :], NO_NODE)
                    link(dve.tensor_scalar(tmpI[:, :], srcI[:, :], P - 1, None, ALU.bitwise_and))
                    link(dve.tensor_copy(slo[:, 0:EC], tmpI[:, :]))
                    link(dve.tensor_scalar(tmpI[:, :], srcI[:, :], 7, None, ALU.arith_shift_right))
                    link(dve.tensor_copy(shi[:, 0:EC], tmpI[:, :]))

                    def marks(h, at, ready):
                        dve.tensor_tensor(lo[h][:, :, :], across(iota[0:EP, :], GK),
                                          along(slo[:, bass.ds(at, GK)], P), ALU.is_equal).then_inc(ready[h], 1)
                        dve.tensor_tensor(hi[h][:, :, :], across(iota[0:EP, 0:NB], GK),
                                          along(shi[:, bass.ds(at, GK)], NB), ALU.is_equal).then_inc(ready[h], 1)
                    for h in range(2):
                        marks(h, h * GK, s_hm)
                    with dve.Fori(1, GI) as i:
                        for h in range(2):
                            dve.wait_ge(s_hu[h], i)
                            marks(h, i * (2 * GK) + h * GK, s_hm)
                    dve.wait_ge(s_hu[0], GI)
                    dve.wait_ge(s_hu[1], GI)
                    dve.tensor_copy(cn_src[:, :], pcn[:, 0:NB]).then_inc(s_hst, 1)
                    dve.wait_ge(s_tot, 1)
                    link(dve.tensor_copy(hs[:, :], ptm[:, 0:NB]))
                    link(dve.tensor_tensor_scan(off[:, :], hs[:, :], zero[:, 0:NB], 0.0, ALU.add, ALU.add))
                    link(dve.tensor_tensor(off[:, :], off[:, :], hs[:, :], ALU.subtract))
                    dve.tensor_tensor(st_src[:, :], off[:, :], ptm[:, 64:64 + NB], ALU.add).then_inc(s_first, 1)
                    marks(0, 0, s_rm)

                    def masked(k, n):
                        dve.wait_ge(s_E, n + 1)
                        dve.tensor_tensor(eq[k % 2][:, :], peq[k % 2][0:EP, 0:EP], tri[0:EP, 0:EP],
                                          ALU.mult).then_inc(s_M, 1)

                    def ranked(h, j, k, n):
                        dve.wait_ge(s_L, n + 1)
                        if not (isinstance(n, int) and n == 0):
                            dve.wait_ge(s_R, n)
                        dve.scalar_tensor_tensor(junk[:, :], plk[k % 2][0:EP, 0:NB], 1.0, hi[h][:, j, :], ALU.mult,
                                                 ALU.mult, accum_out=posF2[:, bass.ds(n, 1)]).then_inc(s_R, 1)

                    def half(i, h, first, more):
                        for j in range(GK):
                            k = h * GK + j
                            n = i * (2 * GK) + k
                            masked(k, n)
                            if not (first and k == 0):
                                if j == 0:
                                    ranked(1 - h, GK - 1, k + 1, n - 1)
                                    if more:
                                        dve.wait_ge(s_R, n)
                                        marks(1 - h, i * (2 * GK) + (h + 1) * GK, s_rm)
                                else:
                                    ranked(h, j - 1, k - 1, n - 1)
                            elif more:
                                marks(1, GK, s_rm)
                    half(0, 0, True, True)
                    half(0, 1, False, True)
                    with dve.Fori(1, GI - 1) as i:
                        half(i, 0, False, True)
                        half(i, 1, False, True)
                    half(GI - 1, 0, False, True)
                    half(GI - 1, 1, False, False)
                    ranked(1, GK - 1, 1, T - 1)
                    dve.wait_ge(s_R, T)
                    link(dve.tensor_copy(posI2[:, :], posF2[:, 0:EC]))
                    dve.tensor_copy(ends[:, :, 0], dstI[:, :])
                    dve.tensor_copy(ends[:, :, 1], srcI[:, :])

                @block.tensor
                def _(pe):
                    pe.matmul(pcn[:, :], zero[:, 0:P], zero[:, :], start=True, stop=True)
                    with pe.Fori(0, GI) as i:
                        for h in range(2):
                            pe.wait_ge(s_hm[h], (i + 1) * 2)
                            for j in range(GK):
                                last = pe.matmul(pcn[:, 0:NB], lo[h][:, j, :], hi[h][:, j, :], start=False, stop=True,
                                                 skip_group_check=True)
                            last.then_inc(s_hu[h], 1)
                    pe.wait_ge(s_hst, 1)
                    pe.matmul(ptm[:, 0:NB], ones[:, :], cn_src[:, :], start=True, stop=True)
                    pe.matmul(ptm[:, 64:64 + NB], tri[:, :], cn_src[:, :], start=True, stop=True).then_inc(s_tot, 1)
                    pe.wait_ge(s_first, 1)
                    pe.matmul(pcn[:, 0:NB], ident[:, :], st_src[:, :], start=True, stop=True).then_inc(s_U, 1)
                    pe.wait_ge(s_rm[0], 2)
                    pe.transpose(ptt[0][:, 0:EP], lo[0][:, 0, :], ident[0:EP, 0:EP]).then_inc(s_T, 1)

                    def column(i, h, j, last):
                        k = h * GK + j
                        n = i * (2 * GK) + k
                        if not last:
                            if j == GK - 1:
                                pe.wait_ge(s_rm[1 - h], (i + 1 + h) * 2)
                            nh, nj = (h, j + 1) if j < GK - 1 else (1 - h, 0)
                            pe.transpose(ptt[(k + 1) % 2][:, 0:EP], lo[nh][:, nj, :], ident[0:EP, 0:EP]).then_inc(s_T, 1)
                        pe.wait_ge(s_cT, n + 1)
                        pe.matmul(peq[k % 2][0:EP, 0:EP], lT[k % 2][:, :], lT[k % 2][:, :], start=True,
                                  stop=True).then_inc(s_E, 1)
                        pe.wait_ge(s_cH, n + 1)
                        if not (isinstance(i, int) and i * (2 * GK) + k < 2):
                            pe.wait_ge(s_R, n - 1)
                        pe.matmul(plk[k % 2][0:EP, 0:NB], lT[k % 2][:, :], hs[:, :], start=True, stop=False)
                        pe.matmul(pcn[:, 0:NB], lo[h][:, j, :], hi[h][:, j, :], start=False, stop=True,
                                  skip_group_check=True).then_inc(s_U, 1)
                        pe.wait_ge(s_M, n + 1)
                        pe.matmul(plk[k % 2][0:EP, 0:NB], eq[k % 2][:, :], hi[h][:, j, :], start=False,
                                  stop=True).then_inc(s_L, 1)
                    for k in range(2 * GK):
                        column(0, k // GK, k % GK, False)
                    with pe.Fori(1, GI - 1) as i:
                        for k in range(2 * GK):
                            column(i, k // GK, k % GK, False)
                    for k in range(2 * GK):
                        column(GI - 1, k // GK, k % GK, k == 2 * GK - 1)

                @block.scalar
                def _(act):
                    with act.Fori(0, GI) as i:
                        for k in range(2 * GK):
                            n = i * (2 * GK) + k
                            act.wait_ge(s_T, n + 1)
                            act.activation(lT[k % 2][:, :], ptt[k % 2][:, 0:EP], ACT.Copy).then_inc(s_cT, 1)
                            act.wait_ge(s_U, n + 1)
                            act.activation(hs[:, :], pcn[:, 0:NB], ACT.Copy).then_inc(s_cH, 1)

            with Phase() as p2:
                s_st = sems(p2, "h_staged0", "h_staged1")
                s_en = sems(p2, "h_ends0", "h_ends1")
                s_sc = dma_sems("h_scattered0", "h_scattered1")
                (s_tick,) = sems(p2, "h_tick")
                posS = [sb(p2, f"posS{h}", [EP, SK], I32) for h in range(2)]
                rowS = [sb(p2, f"rowS{h}", [EP, SK, SRT_W]) for h in range(2)]
                block = p2.enter_context(nc.Block())
                av = attr.rearrange("(p c) f -> p c f", p=EP)

                @block.sync
                def _(sp):
                    def stage(h, at):
                        sp.dma_start(posS[h][:, :], posI2[:, bass.ds(at, SK)]).then_inc(s_st[h], 16)
                        sp.dma_start(rowS[h][:, :, 0:FA], av[:, bass.ds(at, SK), :]).then_inc(s_st[h], 16)
                    for h in range(2):
                        stage(h, h * SK)
                    with sp.Fori(1, SI) as i:
                        for h in range(2):
                            sp.wait_ge(s_sc[h], i * (16 * SK))
                            stage(h, i * (2 * SK) + h * SK)

                @block.scalar
                def _(act):
                    for h in range(2):
                        act.activation(rowS[h][:, :, FA:SRT_W], ends[:, h * SK:(h + 1) * SK, :],
                                       ACT.Copy).then_inc(s_en[h], 1)
                    with act.Fori(1, SI) as i:
                        for h in range(2):
                            act.wait_ge(s_sc[h], i * (16 * SK))
                            act.activation(rowS[h][:, :, FA:SRT_W], ends[:, bass.ds(i * (2 * SK) + h * SK, SK), :],
                                           ACT.Copy).then_inc(s_en[h], 1)

                @block.gpsimd
                def _(pool):
                    with pool.Fori(0, SI) as i:
                        for h in range(2):
                            pool.wait_ge(s_st[h], (i + 1) * 32)
                            pool.sem_inc(s_tick, 1)
                            pool.wait_ge(s_en[h], i + 1)
                            pool.sem_inc(s_tick, 1)
                            for j in range(SK):
                                pool.indirect_dma_start(
                                    srt_d, bass.IndirectOffsetOnAxis(posS[h][:, j:j + 1], 0),
                                    rowS[h][:, j, :], None).then_inc(s_sc[h], 16)
                    for h in range(2):
                        pool.wait_ge(s_sc[h], 16 * SK * SI)

        X = sb(top, "X", [P, NB, D])
        S = sb(top, "S", [P, NB, 2 * D])

        with Phase() as ph:
            (s_ld, s_v) = sems(ph, "c_load", "c_dve")
            rec = sb(ph, "rec", [P, T, REC_W], I32)
            block = ph.enter_context(nc.Block())

            @block.sync
            def _(sp):
                sp.dma_start(rec[:, :, :].rearrange("p t w -> p (t w)"), rec_d).then_inc(s_ld, 16)

            @block.vector
            def _(dve):
                dve.wait_ge(s_ld, 16)
                dve.tensor_copy(src4[:, :], rec[:, :, 0])
                dve.tensor_copy(srcr[:, :], rec[:, :, 1])
                dve.tensor_copy(dlo[:, :], rec[:, :, 2])
                dve.tensor_copy(dful[:, :], rec[:, :, 3])

        def gather_pass(tag, table, idx, wgt=None):
            with Phase() as ph:
                s_st = sems(ph, tag + "staged0", tag + "staged1")
                s_got = dma_sems(tag + "rows0", tag + "rows1")
                s_oh = sems(ph, tag + "marks0", tag + "marks1")
                s_use = sems(ph, tag + "used0", tag + "used1")
                (s_tick, s_v) = sems(ph, tag + "tick", tag + "dve")
                idS = [sb(ph, f"idS{h}", [P, GK], I32) for h in range(2)]
                rows = [sb(ph, f"rows{h}", [P, GK, D]) for h in range(2)]
                mark = [sb(ph, f"mark{h}", [P, GK, P]) for h in range(2)]
                acc = pb(ph, [P, 7 * 512])
                block = ph.enter_context(nc.Block())

                @block.scalar
                def _(act):
                    for h in range(2):
                        act.activation(idS[h][:, :], idx[:, h * GK:(h + 1) * GK], ACT.Copy).then_inc(s_st[h], 1)
                    with act.Fori(1, GI) as i:
                        for h in range(2):
                            act.wait_ge(s_use[h], i)
                            act.activation(idS[h][:, :], idx[:, bass.ds(i * (2 * GK) + h * GK, GK)],
                                           ACT.Copy).then_inc(s_st[h], 1)
                    for h in range(2):
                        act.wait_ge(s_use[h], GI)
                    act.activation(S[:, 0:32, 0:D], acc[:, 0:32 * D].rearrange("p (b f) -> p b f", f=D), ACT.Copy)

                @block.gpsimd
                def _(pool):
                    with pool.Fori(0, GI) as i:
                        for h in range(2):
                            pool.wait_ge(s_st[h], i + 1)
                            pool.sem_inc(s_tick, 1)
                            for j in range(GK):
                                pool.indirect_dma_start(rows[h][:, j, :], None, table,
                                                        bass.IndirectOffsetOnAxis(idS[h][:, j:j + 1], 0)
                                                        ).then_inc(s_got[h], 16)

                @block.vector
                def _(dve):
                    link = Chain(dve, s_v)

                    def make(h, at):
                        ins = dve.tensor_tensor(mark[h][:, :, :], across(iota[:, :], GK),
                                                along(dlo[:, bass.ds(at, GK)], P), ALU.is_equal)
                        if wgt is not None:
                            link(ins)
                            ins = dve.tensor_tensor(mark[h][:, :, :], mark[h][:, :, :],
                                                    along(wgt[:, bass.ds(at, GK)], P), ALU.mult)
                        ins.then_inc(s_oh[h], 1)
                    for h in range(2):
                        make(h, h * GK)
                    n0 = link.base + link.n
                    with dve.Fori(0, GI - 1) as i:
                        link.enter(i, 2 if wgt is not None else 0)
                        for h in range(2):
                            dve.wait_ge(s_use[h], i + 1)
                            make(h, i * (2 * GK) + (2 + h) * GK)
                    link.leave(n0, GI - 1)
                    for h in range(2):
                        dve.wait_ge(s_use[h], GI)
                    dve.tensor_copy(S[:, 32:NB, 0:D], acc[:, 32 * D:NB * D].rearrange("p (b f) -> p b f", f=D))

                @block.tensor
                def _(pe):
                    for b in range(7):
                        pe.matmul(acc[:, b * 512:(b + 1) * 512], zero[:, 0:P], zero[:, :], start=True, stop=True)
                    with pe.Fori(0, GI) as i:
                        for h in range(2):
                            pe.wait_ge(s_oh[h], i + 1)
                            pe.wait_ge(s_got[h], (i + 1) * (16 * GK))
                            for j in range(GK):
                                at = pe.value_load(blk64[0:1, bass.ds(i * (2 * GK) + (h * GK + j), 1)],
                                                   min_val=0, max_val=(NBR - 1) * D)
                                last = pe.matmul(acc[:, bass.ds(at, D)], mark[h][:, j, :], rows[h][:, j, :],
                                                 start=False, stop=True, skip_group_check=True)
                            last.then_inc(s_use[h], 1)

        def norm_tiles(st, tag):
            return [sb(st, tag + n, s) for n, s in (("t3", [P, NB, D]), ("m1", [P, NB]), ("v1", [P, NB]), ("sd", [P, NB]))]

        def norm_dve(dve, link, tiles, s_var, s_dev):
            t3, m1, v1, sd = tiles
            feat = S[:, :, D:2 * D]
            link(dve.tensor_reduce(m1[:, :], X[:, :, :], AX.X, ALU.add))
            link(dve.tensor_scalar(m1[:, :], m1[:, :], 1.0 / D, None, ALU.mult))
            link(dve.tensor_tensor(feat, X[:, :, :], along(m1[:, :], D), ALU.subtract))
            link(dve.tensor_tensor(t3[:, :, :], feat, feat, ALU.mult))
            link(dve.tensor_reduce(v1[:, :], t3[:, :, :], AX.X, ALU.add))
            dve.tensor_scalar(v1[:, :], v1[:, :], 1.0 / D, 1e-5, ALU.mult, ALU.add).then_inc(s_var, 1)
            dve.wait_ge(s_dev, 1)
            link(dve.reciprocal(sd[:, :], sd[:, :]))
            link(dve.tensor_scalar(feat, feat, 0.0, None, ALU.max))
            link(dve.tensor_tensor(feat, feat, along(sd[:, :], D), ALU.mult))

        def norm_act(act, tiles, s_var, s_dev):
            act.wait_ge(s_var, 1)
            act.activation(tiles[3][:, :], tiles[2][:, :], ACT.Sqrt).then_inc(s_dev, 1)

        l0 = ExitStack()
        with l0:
            Wg = sb(l0, "Wg", [P, 4 * D])
            Wt = sb(l0, "Wt", [P, KT * D])
            bg = sb(l0, "bg", [P, 4 * D])
            bt = sb(l0, "bt", [P, KT * D])
            with Phase() as ph:
                (s_ld, s_v, s_var, s_dev, s_z, s_tp, s_g) = sems(
                    ph, "d_load", "d_dve", "d_var", "d_dev", "d_zero", "d_transposed", "d_pool")
                raw = sb(ph, "raw", [P, 4, 2 * D])
                brow = sb(ph, "brow", [1, 3, 4 * D])
                tiles = norm_tiles(ph, "d_")
                psw = pb(ph, [P, 4, P])
                psr = pb(ph, [P, 2, 4 * D])
                block = ph.enter_context(nc.Block())

                @block.gpsimd
                def _(pool):
                    pool.memset(raw[:, :, :], 0.0).then_inc(s_z, 1)
                    pool.memset(brow[:, :, :], 0.0).then_inc(s_z, 1)
                    pool.memset(S[:, :, 0:D], 0.0)

                @block.sync
                def _(sp):
                    sp.wait_ge(s_g, 1)
                    sp.dma_start(X[:, 0:NBR - 1, :], x[0:(NBR - 1) * P, :].rearrange("(b p) f -> p b f", p=P)).then_inc(s_ld, 16)
                    sp.dma_start(X[0:N - (NBR - 1) * P, NBR - 1, :], x[(NBR - 1) * P:N, :]).then_inc(s_ld, 16)
                    sp.wait_ge(s_z, 2)
                    W0v = W0.rearrange("k h d -> (k h) d")
                    for dst_ap, src_ap in (
                            (raw[:, 0, 0:D], wih[0:2 * D, :]), (raw[:, 0, D:2 * D], whh[0:2 * D, :]),
                            (raw[0:D, 1, 0:D], wih[2 * D:3 * D, :]), (raw[D:2 * D, 1, D:2 * D], whh[2 * D:3 * D, :]),
                            (raw[:, 2, D:2 * D], W0v[0:P, :]), (raw[:, 3, D:2 * D], W0v[P:2 * P, :]),
                            (brow[:, 0, 0:3 * D], bih.rearrange("(a n) -> a n", a=1)),
                            (brow[:, 1, 0:2 * D], bhh[0:2 * D].rearrange("(a n) -> a n", a=1)),
                            (brow[:, 1, 3 * D:4 * D], bhh[2 * D:3 * D].rearrange("(a n) -> a n", a=1)),
                            (brow[:, 2, :], b0.rearrange("k h -> (k h)").rearrange("(a n) -> a n", a=1))):
                        sp.dma_start(dst_ap, src_ap).then_inc(s_ld, 16)

                @block.tensor
                def _(pe):
                    pe.wait_ge(s_ld, 12 * 16)
                    for k in range(4):
                        pe.transpose(psw[:, k, :], raw[:, k, :], ident[:, :])
                    pe.matmul(psr[:, 0, :], ones[0:1, :], brow[:, 0, :], start=True, stop=False)
                    pe.matmul(psr[:, 0, :], ones[0:1, :], brow[:, 1, :], start=False, stop=True)
                    pe.matmul(psr[:, 1, :], ones[0:1, :], brow[:, 2, :], start=True, stop=True).then_inc(s_tp, 1)

                @block.scalar
                def _(act):
                    norm_act(act, tiles, s_var, s_dev)

                @block.vector
                def _(dve):
                    link = Chain(dve, s_v)
                    dve.memset(X[:, NBR - 1:NB, :], 0.0).then_inc(s_g, 1)
                    dve.wait_ge(s_ld, 12 * 16)
                    norm_dve(dve, link, tiles, s_var, s_dev)
                    dve.wait_ge(s_tp, 1)
                    dve.tensor_copy(Wg[:, :].rearrange("p (k m) -> p k m", k=2), psw[:, 0:2, :])
                    dve.tensor_copy(Wt[:, :].rearrange("p (k m) -> p k m", k=2), psw[:, 2:4, :])
                    dve.tensor_copy(bg[:, :], psr[:, 0, :])
                    dve.tensor_copy(bt[:, :], psr[:, 1, :])

            def unit(tag, gated, messages):
                with Phase() as ph:
                    (s_in, s_t1, s_c1, s_gt, s_sm, s_sig, s_pre, s_tan, s_new, s_t2, s_c2, s_ms, s_mo, s_out, s_v) = sems(
                        ph, *(tag + n for n in ("staged", "turned", "sbuf", "gates", "biased", "sigmoid", "pretanh", "tanh",
                                                "feat", "turned2", "sbuf2", "msgs", "msgsb", "stored", "dve")))
                    stg = sb(ph, "stg", [P, LOT, 2 * D])
                    stT = sb(ph, "stT", [P, LOT, P])
                    gb = sb(ph, "gb", [P, LOT, 4 * D])
                    nn = sb(ph, "nn", [P, LOT, D])
                    mo = [sb(ph, f"mo{k}", [P, LOT, KT * D]) for k in range(2)]
                    pst = pb(ph, [P, 8, P])
                    psg = pb(ph, [P, 6, 4 * D])
                    psm = pb(ph, [P, 6, 4 * D])
                    block = ph.enter_context(nc.Block())
                    mv = msg_d.rearrange("(b p k) f -> p b (k f)", p=P, k=KT)
                    per = (4 if gated else 0)

                    @block.vector
                    def _(dve):
                        link = Chain(dve, s_v)
                        with dve.Fori(0, NL) as i:
                            link.enter(i, per)
                            lot = bass.ds(i * LOT, LOT)
                            dve.tensor_copy(stg[:, :, :], S[:, lot, :]).then_inc(s_in, 1)
                            if gated:
                                dve.wait_ge(s_gt, i + 1)
                                dve.tensor_tensor(gb[:, :, :], psg[:, 0:LOT, :], across(bg[:, :], LOT),
                                                  ALU.add).then_inc(s_sm, 1)
                                dve.wait_ge(s_sig, i + 1)
                                link(dve.tensor_tensor(nn[:, :, :], gb[:, :, 0:D], gb[:, :, 3 * D:4 * D], ALU.mult))
                                dve.tensor_tensor(nn[:, :, :], nn[:, :, :], gb[:, :, 2 * D:3 * D],
                                                  ALU.add).then_inc(s_pre, 1)
                                dve.wait_ge(s_tan, i + 1)
                                link(dve.tensor_tensor(gb[:, :, 0:D], stg[:, :, D:2 * D], nn[:, :, :], ALU.subtract))
                                link(dve.tensor_tensor(gb[:, :, 0:D], gb[:, :, 0:D], gb[:, :, D:2 * D], ALU.mult))
                                link(dve.tensor_tensor(stg[:, :, D:2 * D], gb[:, :, 0:D], nn[:, :, :], ALU.add))
                                dve.tensor_copy(S[:, lot, D:2 * D], stg[:, :, D:2 * D]).then_inc(s_new, 1)
                                dve.wait_ge(s_new, i + 1)
                            if messages:
                                dve.wait_ge(s_ms, i + 1)
                                dve.tensor_tensor(mo[0][:, :, :], psm[:, 0:LOT, :], across(bt[:, :], LOT),
                                                  ALU.add).then_inc(s_mo, 1)
                                dve.wait_ge(s_out, (i + 1) * 16)
                        link.leave(0, NL)

                    @block.tensor
                    def _(pe):
                        with pe.Fori(0, NL) as i:
                            if gated:
                                pe.wait_ge(s_in, i + 1)
                                for k in range(LOT):
                                    last = pe.transpose(pst[:, k, :], stg[:, k, :], ident[:, :])
                                last.then_inc(s_t1, 1)
                                pe.wait_ge(s_c1, i + 1)
                                for k in range(LOT):
                                    last = pe.matmul(psg[:, k, :], stT[:, k, :], Wg[:, :], start=True, stop=True)
                                last.then_inc(s_gt, 1)
                                pe.wait_ge(s_new, i + 1)
                            else:
                                pe.wait_ge(s_in, i + 1)
                            if messages:
                                for k in range(LOT):
                                    last = pe.transpose(pst[:, k, :], stg[:, k, :], ident[:, :])
                                last.then_inc(s_t2, 1)
                                pe.wait_ge(s_c2, i + 1)
                                for k in range(LOT):
                                    last = pe.matmul(psm[:, k, :], stT[:, k, :], Wt[:, :], start=True, stop=True)
                                last.then_inc(s_ms, 1)

                    @block.scalar
                    def _(act):
                        with act.Fori(0, NL) as i:
                            if gated:
                                act.wait_ge(s_t1, i + 1)
                                act.activation(stT[:, :, :], pst[:, 0:LOT, :], ACT.Copy).then_inc(s_c1, 1)
                                act.wait_ge(s_sm, i + 1)
                                act.activation(gb[:, :, 0:2 * D], gb[:, :, 0:2 * D], ACT.Sigmoid).then_inc(s_sig, 1)
                                act.wait_ge(s_pre, i + 1)
                                act.activation(nn[:, :, :], nn[:, :, :], ACT.Tanh).then_inc(s_tan, 1)
                            if messages:
                                act.wait_ge(s_t2, i + 1)
                                act.activation(stT[:, :, :], pst[:, 0:LOT, :], ACT.Copy).then_inc(s_c2, 1)

                    @block.sync
                    def _(sp):
                        if messages:
                            with sp.Fori(0, NL) as i:
                                sp.wait_ge(s_mo, i + 1)
                                sp.dma_start(mv[:, bass.ds(i * LOT, LOT), :], mo[0][:, :, :]).then_inc(s_out, 16)

            unit("e_", False, True)
            for step in range(STEPS):
                gather_pass(f"f{step}_", msg_d, src4)
                unit(f"g{step}_", True, step < STEPS - 1)
        bysrc = ExitStack()
        with bysrc:
            dsrt = sb(bysrc, "dsrt", [EP, T])
            keep = sb(bysrc, "keep", [EP, EC])
            keepM = sb(bysrc, "keepM", [EP, EC])
            whole = sb(bysrc, "whole", [EP, 1])
            endI = sb(bysrc, "endI", [P, NB], I32)

            def carries(pe_bank, dve, link, tails, width, s_tail, s_turn, s_row, s_back, rowT, contT, carryR, out_ap, sums):
                dve.wait_ge(s_turn, 1)
                link(dve.tensor_copy(rowT[:, :], pe_bank[0:width, 0:EP]))
                link(dve.tensor_copy(contT[:, :], pe_bank[0:width, 128:128 + EP]))
                if sums < width:
                    link(dve.tensor_scalar(contT[sums:width, :], contT[sums:width, :], 2.0, 1.0, ALU.mult, ALU.subtract))
                    link(dve.tensor_scalar(contT[sums:width, :], contT[sums:width, :], BIG, None, ALU.mult))
                    link(dve.memset(carryR[sums:width, 0:1], -BIG))
                    link(dve.tensor_tensor_scan(carryR[sums:width, 1:EP + 1], contT[sums:width, :], rowT[sums:width, :],
                                                -BIG, ALU.min, ALU.max))
                if sums:
                    link(dve.memset(carryR[0:sums, 0:1], 0.0))
                    link(dve.tensor_tensor_scan(carryR[0:sums, 1:EP + 1], contT[0:sums, :], rowT[0:sums, :],
                                                0.0, ALU.mult, ALU.add))
                dve.sem_inc(s_row, 1)
                dve.wait_ge(s_back, 1)
                link(dve.tensor_copy(out_ap, pe_bank[0:EP, 256:256 + width]))

            def carries_pe(pe, pe_bank, tails, cont, carryR, width, s_tail, s_turn, s_row, s_back):
                pe.wait_ge(s_tail, 1)
                pe.transpose(pe_bank[0:width, 0:EP], tails, ident[0:EP, 0:EP])
                pe.transpose(pe_bank[0:width, 128:128 + EP], cont, ident[0:EP, 0:EP]).then_inc(s_turn, 1)
                pe.wait_ge(s_row, 1)
                pe.transpose(pe_bank[0:EP, 256:256 + width], carryR[:, 0:EP], ident[0:width, 0:width]).then_inc(s_back, 1)

            NSL = EC // SLAB
            with Phase() as ph:
                s_in = sems(ph, "k_slab0", "k_slab1")
                s_us = sems(ph, "k_used0", "k_used1")
                s_so = sems(ph, "k_out0", "k_out1")
                s_wr = sems(ph, "k_stored0", "k_stored1")
                (s_pv, s_v, s_tail, s_turn, s_row, s_back) = sems(
                    ph, "k_before", "k_dve", "k_tails", "k_turned", "k_rows", "k_back")
                slab = [sb(ph, f"slab{h}", [EP, SLAB, SRT_W]) for h in range(2)]
                res = [sb(ph, f"res{h}", [EP, SLAB, 2 * FA]) for h in range(2)]
                ssrt = sb(ph, "ssrt", [EP, EC + 1])
                contE = sb(ph, "contE", [EP, 2 * FA])
                carry = sb(ph, "carry", [EP, 2 * FA])
                rowT = sb(ph, "rowT", [2 * FA, EP])
                contT = sb(ph, "contT", [2 * FA, EP])
                carryR = sb(ph, "carryR", [2 * FA, EP + 1])
                fin = sb(ph, "fin", [P, NB])
                pc = pb(ph, [P, 512])
                block = ph.enter_context(nc.Block())
                sv = srt_d.rearrange("(p c) w -> p c w", p=EP)
                gv = seg_d.rearrange("(p c) w -> p (c w)", p=EP)

                @block.sync
                def _(sp):
                    sp.dma_start(ssrt[1:EP, 0:1], sv[0:EP - 1, EC - 1, FA + 1:FA + 2],
                                 allow_slow_non_contiguous=True).then_inc(s_pv, 16)
                    for rnd in range(2):
                        with sp.Fori(0, NSL // 2) as i:
                            for h in range(2):
                                sp.wait_ge(s_us[h], i + 1 + rnd * (NSL // 2))
                                sp.dma_start(slab[h][:, :, :], sv[:, bass.ds(i * (2 * SLAB) + h * SLAB, SLAB), :]
                                             ).then_inc(s_in[h], 16)
                                if rnd:
                                    sp.wait_ge(s_so[h], i + 1)
                                    sp.dma_start(gv[:, bass.ds(i * (2 * SLAB * 2 * FA) + h * SLAB * 2 * FA, SLAB * 2 * FA)],
                                                 res[h][:, :, :].rearrange("p c w -> p (c w)")).then_inc(s_wr[h], 16)
                    for h in range(2):
                        sp.wait_ge(s_wr[h], 16 * (NSL // 2))

                @block.vector
                def _(dve):
                    link = Chain(dve, s_v)
                    for h in range(2):
                        dve.sem_inc(s_us[h], 1)
                    link(dve.memset(dsrt[:, :], NO_NODE * P))
                    dve.memset(res[1][:, SLAB - 1, 0:FA], 0.0)
                    link(dve.memset(res[1][:, SLAB - 1, FA:2 * FA], -BIG))
                    link(dve.memset(ssrt[0:1, 0:1], -1.0))
                    dve.wait_ge(s_pv, 16)
                    def scans(i, h, rnd):
                        dve.wait_ge(s_in[h], 16 * (i + 1 + rnd * (NSL // 2)))
                        at = i * (2 * SLAB) + h * SLAB
                        now = bass.ds(at, SLAB)
                        if rnd == 0:
                            dve.tensor_copy(dsrt[:, now], slab[h][:, :, FA])
                            link(dve.tensor_copy(ssrt[:, bass.ds(at + 1, SLAB)], slab[h][:, :, FA + 1]))
                            link(dve.tensor_tensor(keep[:, now], ssrt[:, bass.ds(at + 1, SLAB)], ssrt[:, now],
                                                   ALU.is_equal))
                            link(dve.tensor_scalar(keepM[:, now], keep[:, now], 2.0, 1.0, ALU.mult, ALU.subtract))
                            link(dve.tensor_scalar(keepM[:, now], keepM[:, now], BIG, None, ALU.mult))
                        elif not isinstance(i, int):
                            dve.wait_ge(s_wr[h], 16 * i)
                        for f in range(FA):
                            dve.tensor_tensor_scan(res[h][:, :, f], keep[:, now], slab[h][:, :, f],
                                                   res[1 - h][:, SLAB - 1, f:f + 1], ALU.mult, ALU.add)
                            last = dve.tensor_tensor_scan(res[h][:, :, FA + f], keepM[:, now], slab[h][:, :, f],
                                                          res[1 - h][:, SLAB - 1, FA + f:FA + f + 1], ALU.min, ALU.max)
                        last.then_inc(s_us[h], 1)
                        dve.wait_ge(s_us[h], i + 2 + rnd * (NSL // 2))
                        if rnd:
                            dve.sem_inc(s_so[h], 1)
                    for rnd in range(2):
                        n0 = link.base + link.n
                        if rnd == 0:
                            with dve.Fori(0, NSL // 2) as i:
                                link.enter(i, 8)
                                for h in range(2):
                                    scans(i, h, 0)
                            link.leave(n0, NSL // 2)
                        else:
                            for h in range(2):
                                scans(0, h, 1)
                            with dve.Fori(1, NSL // 2) as i:
                                for h in range(2):
                                    scans(i, h, 1)
                        if rnd == 0:
                            link(dve.tensor_reduce(whole[:, :], keep[:, :], AX.X, ALU.min))
                            dve.tensor_copy(contE[:, :], whole[:, 0:1].broadcast_to((EP, 2 * FA))).then_inc(s_tail, 1)
                            carries(pc, dve, link, None, 2 * FA, s_tail, s_turn, s_row, s_back, rowT, contT, carryR,
                                    res[1][:, SLAB - 1, :], FA)
                    link(dve.tensor_tensor(fin[:, :], st_src[:, :], cn_src[:, :], ALU.add))
                    dve.tensor_scalar(endI[:, :], fin[:, :], 1.0, 0.0, ALU.subtract, ALU.max)

                @block.tensor
                def _(pe):
                    carries_pe(pe, pc, res[1][:, SLAB - 1, :], contE[:, :], carryR, 2 * FA, s_tail, s_turn, s_row, s_back)

            l1 = bysrc.enter_context(ExitStack())
            H = sb(l1, "H", [P, NB, D])
            a_s = sb(l1, "a_s", [P, 2, NB])
            sm = sb(l1, "sm", [P, 2, NB])
            with Phase() as ph:
                (s_ld, s_z, s_v, s_var, s_dev, s_tp, s_w, s_in, s_t, s_c, s_h, s_hc) = sems(
                    ph, *("l_" + n for n in ("load", "zero", "dve", "var", "dev", "turned", "weights", "staged", "turned2",
                                             "sbuf", "products", "copied")))
                raw = sb(ph, "raw", [P, 2 * D])
                ar = sb(ph, "ar", [1, 2 * D])
                ab = sb(ph, "ab", [P, 2 * D])
                Wh = sb(ph, "Wh", [P, D])
                stg = sb(ph, "stg", [P, LOT, 2 * D])
                stT = sb(ph, "stT", [P, LOT, P])
                tiles = norm_tiles(ph, "l_")
                psw = pb(ph, [P, 512])
                pst = pb(ph, [P, 8, P])
                psh = pb(ph, [P, LOT, D])
                block = ph.enter_context(nc.Block())

                @block.gpsimd
                def _(pool):
                    pool.memset(raw[:, :], 0.0).then_inc(s_z, 1)

                @block.sync
                def _(sp):
                    sp.wait_ge(s_z, 1)
                    sp.dma_start(raw[0:D, D:2 * D], W1g).then_inc(s_ld, 16)
                    sp.dma_start(ar[:, :], a1).then_inc(s_ld, 16)

                @block.tensor
                def _(pe):
                    pe.wait_ge(s_ld, 32)
                    pe.transpose(psw[:, 0:P], raw[:, :], ident[:, :])
                    pe.matmul(psw[:, 128:128 + 2 * D], ones[0:1, :], ar[:, :], start=True, stop=True).then_inc(s_tp, 1)
                    pe.wait_ge(s_w, 1)
                    with pe.Fori(0, NL) as i:
                        pe.wait_ge(s_in, i + 1)
                        for k in range(LOT):
                            last = pe.transpose(pst[:, k, :], stg[:, k, :], ident[:, :])
                        last.then_inc(s_t, 1)
                        pe.wait_ge(s_c, i + 1)
                        for k in range(LOT):
                            last = pe.matmul(psh[:, k, :], stT[:, k, :], Wh[:, :], start=True, stop=True)
                        last.then_inc(s_h, 1)

                @block.scalar
                def _(act):
                    norm_act(act, tiles, s_var, s_dev)
                    with act.Fori(0, NL) as i:
                        act.wait_ge(s_t, i + 1)
                        act.activation(stT[:, :, :], pst[:, 0:LOT, :], ACT.Copy).then_inc(s_c, 1)

                @block.vector
                def _(dve):
                    link = Chain(dve, s_v)
                    link(dve.tensor_tensor(X[:, :, :], X[:, :, :], S[:, :, D:2 * D], ALU.add))
                    norm_dve(dve, link, tiles, s_var, s_dev)
                    dve.wait_ge(s_tp, 1)
                    dve.tensor_copy(ab[:, :], psw[:, 128:128 + 2 * D])
                    dve.tensor_copy(Wh[:, :], psw[:, 0:D]).then_inc(s_w, 1)
                    with dve.Fori(0, NL) as i:
                        lot = bass.ds(i * LOT, LOT)
                        dve.tensor_copy(stg[:, :, :], S[:, lot, :]).then_inc(s_in, 1)
                        dve.wait_ge(s_h, i + 1)
                        dve.tensor_copy(H[:, lot, :], psh[:, :, :]).then_inc(s_hc, 1)
                    dve.wait_ge(s_hc, NL)
                    t3 = tiles[0]
                    for k in range(2):
                        link(dve.tensor_tensor(t3[:, :, :], H[:, :, :], across(ab[:, k * D:(k + 1) * D], NB), ALU.mult))
                        link(dve.tensor_reduce(a_s[:, k, :], t3[:, :, :], AX.X, ALU.add))
                    link(dve.tensor_copy(sm[:, 0, :], a_s[:, 0, :]))

            def look_up(tag, parts, key, table, outs):
                nv = len(outs)
                per_bank = 5
                with Phase() as ph:
                    s_mk = sems(ph, tag + "marks0", tag + "marks1")
                    (s_v, s_T, s_C, s_L, s_R) = sems(ph, *(tag + n for n in ("dve", "turned", "sbuf", "looked", "read")))
                    kI = sb(ph, "kI", [parts, T], I32)
                    kJ = sb(ph, "kJ", [parts, T], I32)
                    klo = sb(ph, "klo", [parts, T])
                    khi = sb(ph, "khi", [parts, T])
                    lo = [sb(ph, f"lo{h}", [parts, GK, P]) for h in range(2)]
                    hi = [sb(ph, f"hi{h}", [parts, GK, NB]) for h in range(2)]
                    lT = sb(ph, "lT", [P, GK, parts])
                    pr = sb(ph, "pr", [parts, GK, NB])
                    ptt = pb(ph, [P, 4, 512])
                    plk = pb(ph, [P, 3, 512])
                    block = ph.enter_context(nc.Block())
                    groups = [(g * 4, min(4, GK - g * 4)) for g in range(-(-GK // 4))]

                    @block.vector
                    def _(dve):
                        link = Chain(dve, s_v)
                        dve.sem_inc(s_R, 1)
                        link(dve.tensor_copy(kI[:, :], key))
                        dve.tensor_scalar(kJ[:, :], kI[:, :], 7, None, ALU.arith_shift_right)
                        link(dve.tensor_scalar(kI[:, :], kI[:, :], P - 1, None, ALU.bitwise_and))
                        dve.tensor_copy(klo[:, :], kI[:, :])
                        link(dve.tensor_copy(khi[:, :], kJ[:, :]))

                        def marks(h, at):
                            dve.tensor_tensor(lo[h][:, :, :], across(iota[0:parts, :], GK),
                                              along(klo[:, bass.ds(at, GK)], P), ALU.is_equal).then_inc(s_mk[h], 1)
                            dve.tensor_tensor(hi[h][:, :, :], across(iota[0:parts, 0:NB], GK),
                                              along(khi[:, bass.ds(at, GK)], NB), ALU.is_equal).then_inc(s_mk[h], 1)

                        def read(i, h):
                            n = i * 2 + h
                            dve.wait_ge(s_L, n + 1)
                            for v in range(nv):
                                for b0, nb, k in ((0, 2, 10), (2, 1, 3)):
                                    w = nv * NB
                                    src_ap = plk[0:parts, b0:b0 + nb, 0:(k // nb) * w].rearrange(
                                        "p b (k w) -> p b k w", w=w)[:, :, :, v * NB:(v + 1) * NB]
                                    o = pr[:, b0 * 5:b0 * 5 + k, :]
                                    m = hi[h][:, b0 * 5:b0 * 5 + k, :]
                                    if nb == 2:
                                        for bb in range(2):
                                            ins = dve.tensor_tensor(pr[:, bb * 5:bb * 5 + 5, :], src_ap[:, bb, :, :],
                                                                    hi[h][:, bb * 5:bb * 5 + 5, :], ALU.mult)
                                    else:
                                        ins = dve.tensor_tensor(o, src_ap[:, 0, :, :], m, ALU.mult)
                                link(ins)
                                ins = dve.tensor_reduce(outs[v][:, bass.ds(i * (2 * GK) + h * GK, GK)], pr[:, :, :],
                                                        AX.X, ALU.add)
                                link(ins)
                            dve.sem_inc(s_R, 1)
                        marks(0, 0)
                        n0 = link.base + link.n
                        with dve.Fori(0, GI - 1) as i:
                            link.enter(i, 4 * nv)
                            marks(1, i * (2 * GK) + GK)
                            read(i, 0)
                            marks(0, i * (2 * GK) + 2 * GK)
                            read(i, 1)
                        link.leave(n0, GI - 1)
                        marks(1, T - GK)
                        read(GI - 1, 0)
                        read(GI - 1, 1)

                    @block.tensor
                    def _(pe):
                        with pe.Fori(0, GI) as i:
                            for h in range(2):
                                n = i * 2 + h
                                pe.wait_ge(s_mk[h], (i + 1) * 2)
                                for j in range(GK):
                                    last = pe.transpose(ptt[:, j // 4, (j % 4) * P:(j % 4) * P + parts], lo[h][:, j, :],
                                                        ident[0:parts, 0:parts])
                                last.then_inc(s_T, 1)
                                pe.wait_ge(s_C, n + 1)
                                pe.wait_ge(s_R, n + 1)
                                for j in range(GK):
                                    w = nv * NB
                                    at = (j % per_bank) * w
                                    last = pe.matmul(plk[0:parts, j // per_bank, at:at + w], lT[:, j, :],
                                                     table, start=True, stop=True)
                                last.then_inc(s_L, 1)

                    @block.scalar
                    def _(act):
                        with act.Fori(0, GI) as i:
                            for h in range(2):
                                n = i * 2 + h
                                act.wait_ge(s_T, n + 1)
                                for g0, k in groups:
                                    ins = act.activation(
                                        lT[:, g0:g0 + k, :],
                                        ptt[:, g0 // 4, 0:k * P].rearrange("p (k e) -> p k e", e=P)[:, :, 0:parts],
                                        ACT.Copy)
                                ins.then_inc(s_C, 1)

            dval = sb(l1, "dval", [EP, T])
            look_up("m_", EP, dsrt[:, :], a_s[:, 1, :], [dval])

            with Phase() as ph:
                (s_v, s_tail, s_turn, s_row, s_back, s_mx, s_wr, s_mo) = sems(
                    ph, *("n_" + n for n in ("dve", "tails", "turned", "rows", "back", "maxima", "stored", "largest")))
                (s_g,) = dma_sems("n_gathered")
                mx = sb(ph, "mx", [EP, EC])
                carry = sb(ph, "carry", [EP, 1])
                rowT = sb(ph, "rowT", [1, EP])
                contT = sb(ph, "contT", [1, EP])
                carryR = sb(ph, "carryR", [1, EP + 1])
                md = sb(ph, "md", [P, NB])
                has = sb(ph, "has", [P, NB])
                e5 = sb(ph, "e5", [P, NB])
                pc = pb(ph, [P, 512])
                block = ph.enter_context(nc.Block())

                @block.vector
                def _(dve):
                    link = Chain(dve, s_v)
                    dve.tensor_tensor_scan(mx[:, :], keepM[:, :], dval[:, 0:EC], -BIG, ALU.min, ALU.max).then_inc(s_tail, 1)
                    carries(pc, dve, link, None, 1, s_tail, s_turn, s_row, s_back, rowT, contT, carryR, carry[:, 0:1], 0)
                    dve.tensor_tensor_scan(mx[:, :], keepM[:, :], dval[:, 0:EC], carry[:, 0:1], ALU.min,
                                           ALU.max).then_inc(s_mx, 1)
                    dve.wait_ge(s_g, 16 * NBR)
                    link(dve.tensor_scalar(has[:, :], cn_src[:, :], 1.0, None, ALU.min))
                    link(dve.tensor_tensor(md[:, 0:NBR], md[:, 0:NBR], a_s[:, 0, 0:NBR], ALU.add))
                    link(dve.scalar_tensor_tensor(e5[:, 0:NBR], md[:, 0:NBR], 0.2, md[:, 0:NBR], ALU.mult, ALU.max))
                    link(dve.memset(sm[:, 1, :], 0.0))
                    dve.tensor_tensor(sm[:, 1, 0:NBR], e5[:, 0:NBR], has[:, 0:NBR], ALU.mult)

                @block.tensor
                def _(pe):
                    carries_pe(pe, pc, mx[:, EC - 1:EC], whole[:, :], carryR, 1, s_tail, s_turn, s_row, s_back)

                @block.sync
                def _(sp):
                    sp.wait_ge(s_mx, 1)
                    sp.dma_start(mxd_d.rearrange("(p c) w -> p (c w)", p=EP), mx[:, :]).then_inc(s_wr, 16)

                @block.gpsimd
                def _(pool):
                    pool.wait_ge(s_wr, 16)
                    for b in range(NBR):
                        pool.indirect_dma_start(md[:, b:b + 1], None, mxd_d,
                                                bass.IndirectOffsetOnAxis(endI[:, b:b + 1], 0)).then_inc(s_g, 16)

            sv_ = sb(l1, "sval", [P, T])
            mv_ = sb(l1, "mval", [P, T])
            dv_ = sb(l1, "dvl2", [P, T])
            look_up("o_", P, srcr[:, :], sm[:, :, :].rearrange("p v b -> p (v b)"), [sv_, mv_])
            look_up("p_", P, dful[:, :], a_s[:, 1, :], [dv_])
            with Phase() as ph:
                (s_v, s_e, s_x, s_w) = sems(ph, *("q_" + n for n in ("dve", "scores", "exp", "rows")))
                s_mk = sems(ph, "q_marks0", "q_marks1")
                s_us = sems(ph, "q_used0", "q_used1")
                (s_wr,) = sems(ph, "q_stored")
                tv = sb(ph, "tv", [P, T])
                klo = sb(ph, "klo", [P, T])
                khi = sb(ph, "khi", [P, T])
                kI = sb(ph, "kI", [P, T], I32)
                kJ = sb(ph, "kJ", [P, T], I32)
                lo = [sb(ph, f"lo{h}", [P, GK, P]) for h in range(2)]
                hi = [sb(ph, f"hi{h}", [P, GK, NB]) for h in range(2)]
                den = sb(ph, "den", [P, NB])
                pd = pb(ph, [P, 512])
                block = ph.enter_context(nc.Block())

                @block.vector
                def _(dve):
                    link = Chain(dve, s_v)
                    link(dve.tensor_tensor(sv_[:, :], sv_[:, :], dv_[:, :], ALU.add))
                    link(dve.scalar_tensor_tensor(tv[:, :], sv_[:, :], 0.2, sv_[:, :], ALU.mult, ALU.max))
                    link(dve.tensor_tensor(tv[:, :], tv[:, :], mv_[:, :], ALU.subtract))
                    dve.tensor_scalar(tv[:, :], tv[:, :], 0.0, None, ALU.min).then_inc(s_e, 1)
                    dve.tensor_scalar(kJ[:, :], srcr[:, :], 7, None, ALU.arith_shift_right)
                    link(dve.tensor_scalar(kI[:, :], srcr[:, :], P - 1, None, ALU.bitwise_and))
                    dve.tensor_copy(klo[:, :], kI[:, :])
                    link(dve.tensor_copy(khi[:, :], kJ[:, :]))
                    link(dve.tensor_scalar(dv_[:, :], dlo[:, :], float(P), None, ALU.is_lt))
                    dve.wait_ge(s_x, 1)
                    link(dve.tensor_tensor(wgt[:, :], tv[:, :], dv_[:, :], ALU.mult))

                    def marks(h, at):
                        dve.tensor_tensor(lo[h][:, :, :], across(iota[:, :], GK), along(klo[:, bass.ds(at, GK)], P),
                                          ALU.is_equal).then_inc(s_mk[h], 1)
                        link(dve.tensor_tensor(hi[h][:, :, :], across(iota[:, 0:NB], GK),
                                               along(khi[:, bass.ds(at, GK)], NB), ALU.is_equal))
                        dve.tensor_tensor(hi[h][:, :, :], hi[h][:, :, :], along(wgt[:, bass.ds(at, GK)], NB),
                                          ALU.mult).then_inc(s_mk[h], 1)
                    for h in range(2):
                        marks(h, h * GK)
                    n0 = link.base + link.n
                    with dve.Fori(0, GI - 1) as i:
                        link.enter(i, 2)
                        for h in range(2):
                            dve.wait_ge(s_us[h], i + 1)
                            marks(h, i * (2 * GK) + (2 + h) * GK)
                    link.leave(n0, GI - 1)
                    dve.wait_ge(s_us[0], GI)
                    dve.wait_ge(s_us[1], GI)
                    link(dve.tensor_scalar(den[:, :], pd[:, 0:NB], 0.5, None, ALU.max))
                    link(dve.reciprocal(den[:, :], den[:, :]))
                    dve.tensor_tensor(H[:, :, :], H[:, :, :], along(den[:, :], D), ALU.mult).then_inc(s_w, 1)

                @block.scalar
                def _(act):
                    act.wait_ge(s_e, 1)
                    act.activation(tv[:, :], tv[:, :], ACT.Exp).then_inc(s_x, 1)

                @block.tensor
                def _(pe):
                    pe.matmul(pd[:, :], zero[:, 0:P], zero[:, :], start=True, stop=True)
                    with pe.Fori(0, GI) as i:
                        for h in range(2):
                            pe.wait_ge(s_mk[h], (i + 1) * 2)
                            for j in range(GK):
                                last = pe.matmul(pd[:, 0:NB], lo[h][:, j, :], hi[h][:, j, :], start=False, stop=True,
                                                 skip_group_check=True)
                            last.then_inc(s_us[h], 1)

                @block.sync
                def _(sp):
                    sp.wait_ge(s_w, 1)
                    sp.dma_start(row_d.rearrange("(b p) f -> p b f", p=P), H[:, :, :]).then_inc(s_wr, 16)
                    sp.wait_ge(s_wr, 16)
            gather_pass("r_", row_d, srcr, wgt)
            l1.close()

            with Phase() as ph:
                (s_v, s_var, s_dev, s_m, s_x, s_rows, s_wr) = sems(
                    ph, *("s_" + n for n in ("dve", "var", "dev", "below", "exp", "rows", "stored")))
                tiles = norm_tiles(ph, "s_")
                block = ph.enter_context(nc.Block())

                @block.vector
                def _(dve):
                    link = Chain(dve, s_v)
                    t3, left = tiles[0], S[:, :, 0:D]
                    dve.tensor_scalar(t3[:, :, :], left, 0.0, None, ALU.min).then_inc(s_m, 1)
                    link(dve.scalar_tensor_tensor(X[:, :, :], left, 0.0, X[:, :, :], ALU.max, ALU.add))
                    dve.wait_ge(s_x, 1)
                    link(dve.scalar_tensor_tensor(X[:, :, :], t3[:, :, :], -1.0, X[:, :, :], ALU.add, ALU.add))
                    norm_dve(dve, link, tiles, s_var, s_dev)
                    dve.sem_inc(s_rows, 1)

                @block.scalar
                def _(act):
                    act.wait_ge(s_m, 1)
                    act.activation(tiles[0][:, :, :], tiles[0][:, :, :], ACT.Exp).then_inc(s_x, 1)
                    norm_act(act, tiles, s_var, s_dev)

                @block.sync
                def _(sp):
                    sp.wait_ge(s_rows, 1)
                    sp.dma_start(row_d.rearrange("(b p) f -> p b f", p=P), S[:, :, D:2 * D]).then_inc(s_wr, 16)
                    sp.wait_ge(s_wr, 16)
            gather_pass("t_", row_d, srcr)

            with Phase() as ph:
                (s_ld, s_v, s_bt, s_f, s_t, s_c, s_h, s_r, s_o, s_g2, s_b) = sems(
                    ph, *("u_" + n for n in ("load", "dve", "bias", "features", "turned", "sbuf", "hidden", "relu", "out",
                                             "added", "biases")))
                (s_g,) = dma_sems("u_gathered")
                K3 = 3 * FA
                sg = sb(ph, "sg", [P, NB, 2 * FA])
                f3 = sb(ph, "f3", [P, NB, K3])
                has = sb(ph, "has", [P, NB])
                rc = sb(ph, "rc", [P, NB])
                w1 = sb(ph, "w1", [K3, HID])
                ur = sb(ph, "ur", [1, 1])
                wu = sb(ph, "wu", [1, HID])
                br = sb(ph, "br", [1, HID])
                w2 = sb(ph, "w2", [HID, D])
                b2r = sb(ph, "b2r", [1, D])
                b2b = sb(ph, "b2b", [P, D])
                b1c = sb(ph, "b1c", [HID, 1])
                stg = sb(ph, "stg", [P, LOT, K3])
                stT = sb(ph, "stT", [K3, LOT, P])
                hd = sb(ph, "hd", [P, LOT, P])
                psb = pb(ph, [P, 512])
                pst = pb(ph, [P, 8, P])
                psh = pb(ph, [P, 8, P])
                pso = pb(ph, [P, LOT, D])
                block = ph.enter_context(nc.Block())

                @block.gpsimd
                def _(pool):
                    for b in range(NBR):
                        pool.indirect_dma_start(sg[:, b, :], None, seg_d,
                                                bass.IndirectOffsetOnAxis(endI[:, b:b + 1], 0)).then_inc(s_g, 16)

                @block.sync
                def _(sp):
                    for dst_ap, src_ap in ((w1[:, :], W13[0:K3, :]), (wu[:, :], W13[K3:K3 + 1, :]), (w2[:, :], W23),
                                           (br[:, :], b13.rearrange("(a n) -> a n", a=1)), (ur[:, :], u3[0:1, :]),
                                           (b2r[:, :], b23.rearrange("(a n) -> a n", a=1))):
                        sp.dma_start(dst_ap, src_ap).then_inc(s_ld, 16)

                @block.vector
                def _(dve):
                    link = Chain(dve, s_v)
                    link(dve.tensor_tensor(X[:, :, :], X[:, :, :], S[:, :, 0:D], ALU.add))
                    dve.tensor_scalar(has[:, :], cn_src[:, :], 1.0, None, ALU.min)
                    link(dve.tensor_scalar(rc[:, :], cn_src[:, :], 1.0, None, ALU.max))
                    link(dve.reciprocal(rc[:, :], rc[:, :]))
                    link(dve.memset(f3[:, NBR:NB, :], 0.0))
                    dve.wait_ge(s_g, 16 * NBR)
                    link(dve.tensor_tensor(f3[:, 0:NBR, 0:2 * FA], sg[:, 0:NBR, :], along(has[:, 0:NBR], 2 * FA), ALU.mult))
                    link(dve.tensor_tensor(f3[:, 0:NBR, 2 * FA:K3], f3[:, 0:NBR, 0:FA], along(rc[:, 0:NBR], FA), ALU.mult))
                    dve.wait_ge(s_bt, 1)
                    dve.tensor_copy(b1c[:, :], psb[:, 0:1])
                    dve.tensor_copy(b2b[:, :], psb[:, 8:8 + D]).then_inc(s_b, 1)
                    dve.wait_ge(s_b, 1)
                    n0 = link.base + link.n
                    with dve.Fori(0, NL) as i:
                        link.enter(i, 1)
                        lot = bass.ds(i * LOT, LOT)
                        dve.tensor_copy(stg[:, :, :], f3[:, lot, :]).then_inc(s_f, 1)
                        link(dve.tensor_tensor(X[:, lot, :], X[:, lot, :], across(b2b[:, :], LOT), ALU.add))
                        dve.wait_ge(s_o, i + 1)
                        dve.tensor_tensor(X[:, lot, :], X[:, lot, :], pso[:, :, :], ALU.add).then_inc(s_g2, 1)
                    link.leave(n0, NL)

                @block.tensor
                def _(pe):
                    pe.wait_ge(s_ld, 6 * 16)
                    pe.matmul(psb[:, 0:1], br[:, :], ones[0:1, 0:1], start=True, stop=False)
                    pe.matmul(psb[:, 0:1], wu[:, :], ur[:, :], start=False, stop=True)
                    pe.matmul(psb[:, 8:8 + D], ones[0:1, :], b2r[:, :], start=True, stop=True).then_inc(s_bt, 1)
                    with pe.Fori(0, NL) as i:
                        pe.wait_ge(s_f, i + 1)
                        for k in range(LOT):
                            last = pe.transpose(pst[0:K3, k, :], stg[:, k, :], ident[:, :])
                        last.then_inc(s_t, 1)
                        pe.wait_ge(s_c, i + 1)
                        for k in range(LOT):
                            last = pe.matmul(psh[:, k, :], w1[:, :], stT[:, k, :], start=True, stop=True)
                        last.then_inc(s_h, 1)
                        pe.wait_ge(s_r, i + 1)
                        for k in range(LOT):
                            last = pe.matmul(pso[:, k, :], hd[:, k, :], w2[:, :], start=True, stop=True)
                        last.then_inc(s_o, 1)

                @block.scalar
                def _(act):
                    act.wait_ge(s_b, 1)
                    with act.Fori(0, NL) as i:
                        act.wait_ge(s_t, i + 1)
                        act.activation(stT[:, :, :], pst[0:K3, 0:LOT, :], ACT.Copy).then_inc(s_c, 1)
                        act.wait_ge(s_h, i + 1)
                        act.activation(hd[:, :, :], psh[:, 0:LOT, :], ACT.Relu, bias=b1c[:, 0:1]).then_inc(s_r, 1)

        with Phase() as ph:
            (s_out,) = sems(ph, "z_out")
            block = ph.enter_context(nc.Block())

            @block.sync
            def _(sp):
                sp.dma_start(out[0:(NBR - 1) * P, :].rearrange("(b p) f -> p b f", p=P), X[:, 0:NBR - 1, :]).then_inc(s_out, 16)
                sp.dma_start(out[(NBR - 1) * P:N, :], X[0:N - (NBR - 1) * P, NBR - 1, :]).then_inc(s_out, 16)
                sp.wait_ge(s_out, 32)


_INS = ["x", "src", "dst", "edge_attr_32", "edge_type_4", "L0_gnn_W", "L0_gnn_b", "L0_gnn_w_ih", "L0_gnn_w_hh",
        "L0_gnn_b_ih", "L0_gnn_b_hh", "L1_gnn_W", "L1_gnn_a", "L3_gnn_u", "L3_gnn_W1", "L3_gnn_b1", "L3_gnn_W2",
        "L3_gnn_b2"]


def kernel(**inputs):
    import numpy as np
    import concourse.bacc as bacc
    from concourse.bass_utils import run_bass_kernel_spmd

    nc = bacc.Bacc("TRN2", target_bir_lowering=False, num_devices=1)
    arrays, args = {}, []
    for name in _INS:
        a = np.ascontiguousarray(inputs[name])
        arrays[f"in_{name}"] = a
        args.append(nc.dram_tensor(f"in_{name}", a.shape, mybir.dt.from_np(a.dtype), kind="ExternalInput").ap())
    args.append(nc.dram_tensor("out_x", (N, D), F32, kind="ExternalOutput").ap())
    build(nc, *args)
    r = run_bass_kernel_spmd(nc, [arrays], core_ids=[0])
    return r.results[0]["out_x"]
```

```python
import concourse.bass as bass
from concourse import mybir
from contextlib import ExitStack
from itertools import count
from math import prod

F32 = mybir.dt.float32
BF16 = mybir.dt.bfloat16
I32 = mybir.dt.int32
ALU = mybir.AluOpType
ACT = mybir.ActivationFunctionType
AX = mybir.AxisListType

P = 128
N = 6250
NBR = -(-N // P)
NB = 50
NP = NB * P
D = 64
FA = 32
KT = 4
STEPS = 4
E = 200000
EP = 125
EC = E // EP
GK = 13
T = 1612
GI = T // (2 * GK)
SK = 10
SI = EC // (2 * SK)
LOT = 5
NL = NB // LOT
SLAB = 32
HID = 128
REC_W = 4
SRT_W = FA + 2
BIG = 3.4028234663852886e38
NO_NODE = 255.0
assert (E + NBR * (P - 1)) // P <= T and EP * EC == E and T % (2 * GK) == 0 and EC % (2 * SK) == 0


class Chain:

    def __init__(self, eng, sem):
        self.eng, self.sem, self.n, self.base = eng, sem, 0, 0

    def __call__(self, ins):
        self.n += 1
        ins.then_inc(self.sem, 1)
        self.eng.wait_ge(self.sem, self.base + self.n)

    def enter(self, i, per):
        self.base, self.n, self.per = self.base + self.n + i * per, 0, per
        self.after = None

    def leave(self, base0, turns):
        assert self.n == self.per, (self.n, self.per)
        self.base, self.n = base0 + turns * self.per, 0


def build(nc, x, src, dst, attr, etype, W0, b0, wih, whh, bih, bhh, W1g, a1, u3, W13, b13, W23, b23, out):
    top = ExitStack()

    class Phase(ExitStack):

        def __init__(self):
            super().__init__()
            self.held = []
            self.callback(self.tidy)

        def tidy(self):
            for s in self.held:
                nc.gpsimd.sem_clear(s)
            nc.all_engine_barrier()
            for s in self.held:
                nc.release_semaphore(s)

    def sems(st, *names):
        made_here = [nc.alloc_semaphore(n) for n in names]
        st.held += made_here
        return made_here

    def dma_sems(*names):
        return [nc.alloc_semaphore(n) for n in names]

    made = count()

    def sb(st, name, shape, dt=F32):
        return st.enter_context(nc.sbuf_tensor(f"{name}_{next(made)}", shape, dt))

    ps_all = top.enter_context(nc.psum_tensor("ps_all", [P, 8 * 512], F32))
    bank = [0]

    def pb(st, shape):
        size = prod(shape[1:])
        at = bank[0]
        bank[0] += -(-size // 512)
        assert bank[0] <= 8
        st.callback(bank.__setitem__, 0, at)
        view = ps_all[0:shape[0], at * 512:at * 512 + size]
        return view.rearrange("p (a b) -> p a b", a=shape[1]) if len(shape) == 3 else view

    def along(ap, n):
        p, k = ap.shape
        return ap.rearrange("p (k a) -> p k a", a=1).broadcast_to((p, k, n))

    def across(ap, k):
        p, n = ap.shape
        return ap.rearrange("p (a n) -> p a n", a=1).broadcast_to((p, k, n))

    with top:
        rec_d = nc.dram_tensor("rec_d", (P, T * REC_W), I32).ap()
        msg_d = nc.dram_tensor("msg_d", (NP * KT, D), F32).ap()
        row_d = nc.dram_tensor("row_d", (NP, D), F32).ap()
        srt_d = nc.dram_tensor("srt_d", (E, SRT_W), F32).ap()
        seg_d = nc.dram_tensor("seg_d", (E, 2 * FA), F32).ap()
        mxd_d = nc.dram_tensor("mxd_d", (E, 1), F32).ap()
        sum_d = nc.dram_tensor("sum_d", (E, 1), F32).ap()
        two_d = nc.dram_tensor("two_d", (E + NP, 2), F32).ap()
        dot_d = nc.dram_tensor("dot_d", (NP,), F32).ap()
        att_d = nc.dram_tensor("att_d", (NP, D + 2), F32).ap()

        iota = sb(top, "iota", [P, P])
        ident = sb(top, "ident", [P, P])
        tri = sb(top, "tri", [P, P])
        ones = sb(top, "ones", [P, P])
        zero = sb(top, "zero", [P, 512])
        src4 = sb(top, "src4", [P, T], I32)
        srcr = sb(top, "srcr", [P, T], I32)
        dlo = sb(top, "dlo", [P, T])
        blk64 = sb(top, "blk64", [1, T], I32)
        st_src = sb(top, "st_src", [P, NB])
        cn_src = sb(top, "cn_src", [P, NB])

        with Phase() as ph:
            (s_c, s_tri, s_ld, s_cnt, s_cs, s_base, s_bt, s_ge, s_br, s_df, s_v, s_z) = sems(
                ph, "a_const", "a_tri", "a_load", "a_counts", "a_sums", "a_starts", "a_startsT", "a_reached",
                "a_blocks", "a_defaults", "a_dve", "a_zero")
            (s_def,) = sems(ph, "a_stored")
            dstI = sb(ph, "dstI", [EP, EC], I32)
            srcI = sb(ph, "srcI", [EP, EC], I32)
            etI = sb(ph, "etI", [EP, EC], I32)
            tmpI = sb(ph, "tmpI", [EP, EC], I32)
            posI = sb(ph, "posI", [EP, EC], I32)
            pay = sb(ph, "pay", [EP, EC, REC_W], I32)
            cnt = sb(ph, "cnt", [EP, NB])
            pre = sb(ph, "pre", [EP, NB])
            tot = sb(ph, "tot", [P, NB])
            totI = sb(ph, "totI", [P, NB], I32)
            nch = sb(ph, "nch", [P, NB])
            cs = sb(ph, "cs", [P, NB])
            base = sb(ph, "base", [P, NB])
            csT = sb(ph, "csT", [NBR, 1])
            with Phase() as p0:
                hiF = sb(p0, "hiF", [EP, EC])
                m = sb(p0, "m", [EP, EC])
                c = sb(p0, "c", [EP, EC])
                q = sb(p0, "q", [EP, EC])
                zr = sb(p0, "zr", [EP, EC])
                posF = sb(p0, "posF", [EP, EC])
                dflt = sb(p0, "dflt", [P, T, REC_W], I32)
                ioT = sb(p0, "ioT", [NBR, T])
                reach = sb(p0, "reach", [NBR, T])
                ps = pb(p0, [P, 2, 512])
                psb = pb(p0, [1, 4, 512])
                block = p0.enter_context(nc.Block())

                @block.gpsimd
                def _(pool):
                    pool.iota(iota[:, :], [[1, P]], base=0, channel_multiplier=0,
                              allow_small_or_imprecise_dtypes=True).then_inc(s_c, 1)
                    pool.iota(ioT[:, :], [[1, T]], base=0, channel_multiplier=0,
                              allow_small_or_imprecise_dtypes=True).then_inc(s_c, 1)
                    pool.memset(ident[:, :], 0.0).then_inc(s_tri, 1)
                    pool.memset(ones[:, :], 1.0).then_inc(s_tri, 1)
                    pool.wait_ge(s_tri, 2)
                    pool.affine_select(out=ident[:, :], in_=ident[:, :], compare_op=ALU.not_equal, fill=1.0, base=0,
                                       pattern=[[-1, P]], channel_multiplier=1).then_inc(s_c, 1)
                    pool.affine_select(out=tri[:, :], in_=ones[:, :], compare_op=ALU.is_gt, fill=0.0, base=0,
                                       pattern=[[1, P]], channel_multiplier=-1).then_inc(s_c, 1)

                @block.sync
                def _(sp):
                    for tile, a in ((dstI, dst), (srcI, src), (etI, etype)):
                        sp.dma_start(tile[:, :], a.rearrange("(p c) -> p c", p=EP)).then_inc(s_ld, 16)
                    sp.wait_ge(s_df, 2)
                    sp.dma_start(rec_d, dflt[:, :, :].rearrange("p t w -> p (t w)")).then_inc(s_def, 16)
                    sp.wait_ge(s_def, 16)

                @block.vector
                def _(dve):
                    link = Chain(dve, s_v)
                    dve.memset(zero[:, :], 0.0).then_inc(s_z, 1)
                    link(dve.memset(dflt[:, :, :], 0))
                    dve.memset(dflt[:, :, 2], int(NO_NODE)).then_inc(s_df, 2)
                    dve.memset(zr[:, :], 0.0)
                    dve.memset(posF[:, :], 0.0)
                    link(dve.memset(cnt[:, :], 0.0))
                    dve.wait_ge(s_ld, 48)
                    dve.wait_ge(s_c, 4)
                    dve.tensor_scalar(pay[:, :, 2], dstI[:, :], P - 1, None, ALU.bitwise_and)
                    dve.tensor_copy(pay[:, :, 3], dstI[:, :])
                    dve.tensor_copy(pay[:, :, 1], srcI[:, :])
                    dve.scalar_tensor_tensor(pay[:, :, 0], srcI[:, :], float(KT), etI[:, :], ALU.mult, ALU.add)
                    link(dve.tensor_scalar(tmpI[:, :], dstI[:, :], 7, None, ALU.arith_shift_right))
                    link(dve.tensor_copy(hiF[:, :], tmpI[:, :]))
                    with dve.Fori(0, NBR) as b:
                        dve.tensor_scalar(m[:, :], hiF[:, :], iota[0:EP, bass.ds(b, 1)], None, ALU.is_equal, ALU.add,
                                          accum_out=cnt[:, bass.ds(b, 1)]).then_inc(s_cnt, 1)
                        dve.wait_ge(s_cnt, b + 1)
                    dve.wait_ge(s_cs, 1)
                    link(dve.tensor_scalar(totI[:, :], ps[:, 1, 0:NB], float(P - 1), None, ALU.add))
                    dve.tensor_copy(pre[:, :], ps[0:EP, 0, 0:NB])
                    link(dve.tensor_scalar(totI[:, :], totI[:, :], 7, None, ALU.arith_shift_right))
                    link(dve.tensor_copy(nch[:, :], totI[:, :]))
                    link(dve.tensor_tensor_scan(cs[:, :], nch[:, :], zero[:, 0:NB], 0.0, ALU.add, ALU.add))
                    dve.tensor_tensor(cs[:, :], cs[:, :], nch[:, :], ALU.subtract).then_inc(s_base, 1)
                    dve.wait_ge(s_base, 1)
                    link(dve.scalar_tensor_tensor(base[0:EP, :], cs[0:EP, :], float(P), pre[:, :], ALU.mult, ALU.add))
                    link(dve.tensor_scalar(base[0:EP, :], base[0:EP, :], 1.0, None, ALU.subtract))
                    dve.wait_ge(s_bt, 1)
                    link(dve.tensor_copy(csT[:, :], ps[0:NBR, 0, 0:1]))
                    dve.tensor_scalar(reach[:, :], ioT[:, :], csT[:, 0:1], None, ALU.is_ge).then_inc(s_ge, 1)
                    n0 = link.base + link.n
                    with dve.Fori(0, NBR) as b:
                        link.enter(b, 4)
                        link(dve.tensor_scalar(m[:, :], hiF[:, :], iota[0:EP, bass.ds(b, 1)], None, ALU.is_equal))
                        link(dve.tensor_tensor_scan(c[:, :], m[:, :], zr[:, :], 0.0, ALU.add, ALU.add))
                        link(dve.scalar_tensor_tensor(q[:, :], c[:, :], base[0:EP, bass.ds(b, 1)], m[:, :],
                                                      ALU.add, ALU.mult))
                        link(dve.tensor_tensor(posF[:, :], posF[:, :], q[:, :], ALU.add))
                    link.leave(n0, NBR)
                    link(dve.tensor_copy(posI[:, :], posF[:, :]))
                    dve.tensor_scalar(tmpI[:, :], posI[:, :], P - 1, None, ALU.bitwise_and)
                    link(dve.tensor_scalar(posI[:, :], posI[:, :], 7, None, ALU.arith_shift_right))
                    dve.tensor_copy(c[:, :], tmpI[:, :])
                    link(dve.tensor_copy(q[:, :], posI[:, :]))
                    link(dve.scalar_tensor_tensor(posI[:, :], c[:, :], float(T), q[:, :], ALU.mult, ALU.add))
                    dve.wait_ge(s_br, 1)
                    link(dve.tensor_scalar(blk64[:, :].rearrange("a (k n) -> a k n", k=4), psb[:, :, 0:T // 4],
                                           1.0, float(D), ALU.subtract, ALU.mult))

                @block.tensor
                def _(pe):
                    pe.wait_ge(s_cnt, NBR)
                    pe.wait_ge(s_c, 4)
                    pe.matmul(ps[0:EP, 0, 0:NB], tri[0:EP, 0:EP], cnt[:, :], start=True, stop=True)
                    pe.matmul(ps[:, 1, 0:NB], ones[0:EP, :], cnt[:, :], start=True, stop=True).then_inc(s_cs, 1)
                    pe.wait_ge(s_base, 1)
                    pe.matmul(ps[0:NBR, 0, 0:1], cs[0:1, 0:NBR], ones[0:1, 0:1], start=True, stop=True).then_inc(s_bt, 1)
                    pe.wait_ge(s_ge, 1)
                    for k in range(4):
                        last = pe.matmul(psb[:, k, 0:T // 4], ones[0:NBR, 0:1], reach[:, k * (T // 4):(k + 1) * (T // 4)],
                                         start=True, stop=True)
                    last.then_inc(s_br, 1)

            with Phase() as p1:
                s_st = sems(p1, "b_staged0", "b_staged1")
                s_ft = sems(p1, "b_features0", "b_features1")
                s_sc = dma_sems("b_scattered0", "b_scattered1")
                s_fs = dma_sems("b_placed0", "b_placed1")
                s_hm = sems(p1, "b_hmarks0", "b_hmarks1")
                s_hu = sems(p1, "b_hused0", "b_hused1")
                s_rm = sems(p1, "b_rmarks0", "b_rmarks1")
                (s_tick, s_v, s_hst, s_tot, s_first, s_T, s_cT, s_E, s_M, s_U, s_cH, s_L, s_R, s_pos, s_en) = sems(
                    p1, *("b_" + n for n in ("tick", "dve", "counts", "totals", "first", "turned", "turnedsb", "equal",
                                             "earlier", "counted", "countsb", "looked", "ranked", "positions", "ends")))
                posS = [sb(p1, f"posS{h}", [EP, SK], I32) for h in range(2)]
                payS = [sb(p1, f"payS{h}", [EP, SK, REC_W], I32) for h in range(2)]
                plS = [sb(p1, f"plS{h}", [EP, SK], I32) for h in range(2)]
                rowS = [sb(p1, f"rowS{h}", [EP, SK, SRT_W]) for h in range(2)]
                slo = sb(p1, "slo", [EP, EC])
                shi = sb(p1, "shi", [EP, EC])
                posF2 = sb(p1, "posF2", [EP, EC])
                posI2 = sb(p1, "posI2", [EP, EC], I32)
                ends = sb(p1, "ends", [EP, EC, 2])
                lo = [sb(p1, f"lo{h}", [EP, SK, P], BF16) for h in range(2)]
                hi = [sb(p1, f"hi{h}", [EP, SK, NB], BF16) for h in range(2)]
                identb = sb(p1, "identb", [P, P], BF16)
                lT = [sb(p1, f"lT{k}", [P, EP]) for k in range(2)]
                eq = [sb(p1, f"eq{k}", [EP, EP], BF16) for k in range(2)]
                hs = sb(p1, "hs", [P, NB])
                off = sb(p1, "off", [P, NB])
                junk = sb(p1, "junk", [EP, NB])
                ptt = [pb(p1, [P, 512]) for k in range(2)]
                peq = [pb(p1, [P, 512]) for k in range(2)]
                plk = [pb(p1, [P, 512]) for k in range(2)]
                pcn = pb(p1, [P, 512])
                ptm = pb(p1, [P, 512])
                block = p1.enter_context(nc.Block())
                av = attr.rearrange("(p c) f -> p c f", p=EP)

                @block.sync
                def _(sp):
                    def stage(h, at):
                        sp.dma_start(posS[h][:, :], posI[:, bass.ds(at, SK)]).then_inc(s_st[h], 16)
                        sp.dma_start(payS[h][:, :, :], pay[:, bass.ds(at, SK), :]).then_inc(s_st[h], 16)
                    for h in range(2):
                        stage(h, h * SK)
                    with sp.Fori(1, SI) as i:
                        for h in range(2):
                            sp.wait_ge(s_sc[h], i * (16 * SK))
                            stage(h, i * (2 * SK) + h * SK)

                    def features(h, i):
                        at = i * (2 * SK) + h * SK
                        sp.dma_start(rowS[h][:, :, 0:FA], av[:, bass.ds(at, SK), :]).then_inc(s_ft[h], 16)
                        sp.dma_start(rowS[h][:, :, FA:SRT_W], ends[:, bass.ds(at, SK), :]).then_inc(s_ft[h], 16)
                        sp.wait_ge(s_pos, i * 2 + h + 1)
                        sp.dma_start(plS[h][:, :], posI2[:, bass.ds(at, SK)]).then_inc(s_ft[h], 16)
                    sp.wait_ge(s_en, 2)
                    for h in range(2):
                        features(h, 0)
                    with sp.Fori(1, SI) as i:
                        for h in range(2):
                            sp.wait_ge(s_fs[h], i * (16 * SK))
                            features(h, i)

                @block.gpsimd
                def _(pool):
                    with pool.Fori(0, SI) as i:
                        for h in range(2):
                            pool.wait_ge(s_st[h], (i + 1) * 32)
                            pool.sem_inc(s_tick, 1)
                            for j in range(SK):
                                pool.indirect_dma_start(
                                    rec_d.rearrange("p (t w) -> (p t) w", w=REC_W),
                                    bass.IndirectOffsetOnAxis(posS[h][:, j:j + 1], 0),
                                    payS[h][:, j, :], None).then_inc(s_sc[h], 16)
                    with pool.Fori(0, SI) as i:
                        for h in range(2):
                            pool.wait_ge(s_ft[h], (i + 1) * 48)
                            pool.sem_inc(s_tick, 1)
                            for j in range(SK):
                                pool.indirect_dma_start(
                                    srt_d, bass.IndirectOffsetOnAxis(plS[h][:, j:j + 1], 0),
                                    rowS[h][:, j, :], None).then_inc(s_fs[h], 16)
                    for h in range(2):
                        pool.wait_ge(s_sc[h], 16 * SK * SI)
                        pool.wait_ge(s_fs[h], 16 * SK * SI)

                @block.vector
                def _(dve):
                    link = Chain(dve, s_v)
                    dve.tensor_copy(ends[:, :, 0], dstI[:, :]).then_inc(s_en, 1)
                    dve.tensor_copy(ends[:, :, 1], srcI[:, :]).then_inc(s_en, 1)
                    dve.tensor_copy(identb[:, :], ident[:, :])
                    link(dve.tensor_scalar(tmpI[:, :], srcI[:, :], P - 1, None, ALU.bitwise_and))
                    link(dve.tensor_copy(slo[:, :], tmpI[:, :]))
                    link(dve.tensor_scalar(tmpI[:, :], srcI[:, :], 7, None, ALU.arith_shift_right))
                    link(dve.tensor_copy(shi[:, :], tmpI[:, :]))

                    def marks(h, at, ready):
                        dve.tensor_tensor(lo[h][:, :, :], across(iota[0:EP, :], SK),
                                          along(slo[:, bass.ds(at, SK)], P), ALU.is_equal).then_inc(ready[h], 1)
                        dve.tensor_tensor(hi[h][:, :, :], across(iota[0:EP, 0:NB], SK),
                                          along(shi[:, bass.ds(at, SK)], NB), ALU.is_equal).then_inc(ready[h], 1)
                    for h in range(2):
                        marks(h, h * SK, s_hm)
                    with dve.Fori(1, SI) as i:
                        for h in range(2):
                            dve.wait_ge(s_hu[h], i)
                            marks(h, i * (2 * SK) + h * SK, s_hm)
                    dve.wait_ge(s_hu[0], SI)
                    dve.wait_ge(s_hu[1], SI)
                    dve.tensor_copy(cn_src[:, :], pcn[:, 0:NB]).then_inc(s_hst, 1)
                    dve.wait_ge(s_tot, 1)
                    link(dve.tensor_copy(hs[:, :], ptm[:, 0:NB]))
                    link(dve.tensor_tensor_scan(off[:, :], hs[:, :], zero[:, 0:NB], 0.0, ALU.add, ALU.add))
                    link(dve.tensor_tensor(off[:, :], off[:, :], hs[:, :], ALU.subtract))
                    dve.tensor_tensor(st_src[:, :], off[:, :], ptm[:, 64:64 + NB], ALU.add).then_inc(s_first, 1)
                    marks(0, 0, s_rm)

                    def masked(k, n):
                        dve.wait_ge(s_E, n + 1)
                        dve.tensor_tensor(eq[k % 2][:, :], peq[k % 2][0:EP, 0:EP], tri[0:EP, 0:EP],
                                          ALU.mult).then_inc(s_M, 1)

                    def ranked(h, j, k, n):
                        dve.wait_ge(s_L, n + 1)
                        if not (isinstance(n, int) and n == 0):
                            dve.wait_ge(s_R, n)
                        dve.scalar_tensor_tensor(junk[:, :], plk[k % 2][0:EP, 0:NB], 1.0, hi[h][:, j, :], ALU.mult,
                                                 ALU.mult, accum_out=posF2[:, bass.ds(n, 1)]).then_inc(s_R, 1)

                    def placed(at):
                        dve.tensor_copy(posI2[:, bass.ds(at, SK)], posF2[:, bass.ds(at, SK)]).then_inc(s_pos, 1)

                    def half(i, h, first, more):
                        for j in range(SK):
                            k = h * SK + j
                            n = i * (2 * SK) + k
                            masked(k, n)
                            if not (first and k == 0):
                                if j == 0:
                                    ranked(1 - h, SK - 1, k + 1, n - 1)
                                    dve.wait_ge(s_R, n)
                                    if more:
                                        marks(1 - h, i * (2 * SK) + (h + 1) * SK, s_rm)
                                    placed(n - SK)
                                else:
                                    ranked(h, j - 1, k - 1, n - 1)
                            elif more:
                                marks(1, SK, s_rm)
                    half(0, 0, True, True)
                    half(0, 1, False, True)
                    with dve.Fori(1, SI - 1) as i:
                        half(i, 0, False, True)
                        half(i, 1, False, True)
                    half(SI - 1, 0, False, True)
                    half(SI - 1, 1, False, False)
                    ranked(1, SK - 1, 1, EC - 1)
                    dve.wait_ge(s_R, EC)
                    placed(EC - SK)

                @block.tensor
                def _(pe):
                    pe.matmul(pcn[:, :], zero[:, 0:P], zero[:, :], start=True, stop=True)
                    with pe.Fori(0, SI) as i:
                        for h in range(2):
                            pe.wait_ge(s_hm[h], (i + 1) * 2)
                            for j in range(SK):
                                last = pe.matmul(pcn[:, 0:NB], lo[h][:, j, :], hi[h][:, j, :], start=False, stop=True,
                                                 skip_group_check=True)
                            last.then_inc(s_hu[h], 1)
                    pe.wait_ge(s_hst, 1)
                    pe.matmul(ptm[:, 0:NB], ones[:, :], cn_src[:, :], start=True, stop=True)
                    pe.matmul(ptm[:, 64:64 + NB], tri[:, :], cn_src[:, :], start=True, stop=True).then_inc(s_tot, 1)
                    pe.wait_ge(s_first, 1)
                    pe.matmul(pcn[:, 0:NB], ident[:, :], st_src[:, :], start=True, stop=True).then_inc(s_U, 1)

                    def turned(k, h, j):
                        pe.transpose(ptt[k % 2].bitcast(BF16)[:, 0:EP], lo[h][:, j, :], identb[0:EP, 0:EP]).then_inc(s_T, 1)
                    pe.wait_ge(s_rm[0], 2)
                    turned(0, 0, 0)

                    def column(i, h, j, last):
                        k = h * SK + j
                        n = i * (2 * SK) + k
                        if not last:
                            if j == SK - 1:
                                pe.wait_ge(s_rm[1 - h], (i + 1 + h) * 2)
                            turned(k + 1, *((h, j + 1) if j < SK - 1 else (1 - h, 0)))
                        pe.wait_ge(s_cT, n + 1)
                        pe.matmul(peq[k % 2][0:EP, 0:EP], lT[k % 2][:, :], lT[k % 2][:, :], start=True,
                                  stop=True).then_inc(s_E, 1)
                        pe.wait_ge(s_cH, n + 1)
                        if not (isinstance(i, int) and i * (2 * SK) + k < 2):
                            pe.wait_ge(s_R, n - 1)
                        pe.matmul(plk[k % 2][0:EP, 0:NB], lT[k % 2][:, :], hs[:, :], start=True, stop=False)
                        pe.matmul(pcn[:, 0:NB], lo[h][:, j, :], hi[h][:, j, :], start=False, stop=True,
                                  skip_group_check=True).then_inc(s_U, 1)
                        pe.wait_ge(s_M, n + 1)
                        pe.matmul(plk[k % 2][0:EP, 0:NB], eq[k % 2][:, :], hi[h][:, j, :], start=False,
                                  stop=True).then_inc(s_L, 1)
                    for k in range(2 * SK):
                        column(0, k // SK, k % SK, False)
                    with pe.Fori(1, SI - 1) as i:
                        for k in range(2 * SK):
                            column(i, k // SK, k % SK, False)
                    for k in range(2 * SK):
                        column(SI - 1, k // SK, k % SK, k == 2 * SK - 1)

                @block.scalar
                def _(act):
                    with act.Fori(0, SI) as i:
                        for k in range(2 * SK):
                            n = i * (2 * SK) + k
                            act.wait_ge(s_T, n + 1)
                            act.activation(lT[k % 2][:, :], ptt[k % 2].bitcast(BF16)[:, 0:EP], ACT.Copy).then_inc(s_cT, 1)
                            act.wait_ge(s_U, n + 1)
                            act.activation(hs[:, :], pcn[:, 0:NB], ACT.Copy).then_inc(s_cH, 1)

        X = sb(top, "X", [P, NB, D])
        S = sb(top, "S", [P, NB, 2 * D])

        with Phase() as ph:
            (s_ld, s_v) = sems(ph, "c_load", "c_dve")
            rec = sb(ph, "rec", [P, T, REC_W], I32)
            block = ph.enter_context(nc.Block())

            @block.sync
            def _(sp):
                sp.dma_start(rec[:, :, :].rearrange("p t w -> p (t w)"), rec_d).then_inc(s_ld, 16)

            @block.vector
            def _(dve):
                dve.wait_ge(s_ld, 16)
                dve.tensor_copy(src4[:, :], rec[:, :, 0])
                dve.tensor_copy(srcr[:, :], rec[:, :, 1])
                dve.tensor_copy(dlo[:, :], rec[:, :, 2])

        def gather_pass(tag, table, idx, dots=None, side=None):
            width = D if dots is None else D + 2
            with Phase() as ph:
                s_st = sems(ph, tag + "staged0", tag + "staged1")
                s_got = dma_sems(tag + "rows0", tag + "rows1")
                s_oh = sems(ph, tag + "marks0", tag + "marks1")
                s_use = sems(ph, tag + "used0", tag + "used1")
                (s_tick, s_v, s_z, s_x) = sems(ph, tag + "tick", tag + "dve", tag + "scores", tag + "exp")
                idS = [sb(ph, f"idS{h}", [P, GK], I32) for h in range(2)]
                rows = [sb(ph, f"rows{h}", [P, GK, width]) for h in range(2)]
                mark = [sb(ph, f"mark{h}", [P, GK, P]) for h in range(2)]
                if dots is not None:
                    prod_ = sb(ph, "prod", [P, GK, P])
                    de = sb(ph, "de", [P, GK])
                    sc = sb(ph, "sc", [P, GK])
                acc = pb(ph, [P, 7 * 512])
                if side is not None:
                    side.bank = pb(ph, [P, 512])
                block = ph.enter_context(nc.Block())

                @block.scalar
                def _(act):
                    for h in range(2):
                        act.activation(idS[h][:, :], idx[:, h * GK:(h + 1) * GK], ACT.Copy).then_inc(s_st[h], 1)

                    def exps(i, h):
                        if dots is not None:
                            act.wait_ge(s_z, i * 2 + h + 1)
                            act.activation(sc[:, :], sc[:, :], ACT.Exp).then_inc(s_x, 1)
                    exps(0, 0)

                    def turn(i, beside):
                        for h in range(2):
                            act.wait_ge(s_use[h], i + 1)
                            act.activation(idS[h][:, :], idx[:, bass.ds(i * (2 * GK) + (2 + h) * GK, GK)],
                                           ACT.Copy).then_inc(s_st[h], 1)
                            exps(i + h, 1 - h)
                    first = 0
                    if side is not None:
                        first = side.turns
                        with act.Fori(0, first) as i:
                            turn(i, True)
                    with act.Fori(first, GI - 1) as i:
                        turn(i, False)
                    exps(GI - 1, 1)
                    for h in range(2):
                        act.wait_ge(s_use[h], GI)
                    act.activation(S[:, 0:32, 0:D], acc[:, 0:32 * D].rearrange("p (b f) -> p b f", f=D), ACT.Copy)

                @block.gpsimd
                def _(pool):
                    with pool.Fori(0, GI) as i:
                        for h in range(2):
                            pool.wait_ge(s_st[h], i + 1)
                            pool.sem_inc(s_tick, 1)
                            for j in range(GK):
                                pool.indirect_dma_start(rows[h][:, j, :], None, table,
                                                        bass.IndirectOffsetOnAxis(idS[h][:, j:j + 1], 0)
                                                        ).then_inc(s_got[h], 16)

                @block.vector
                def _(dve):
                    link = Chain(dve, s_v)

                    def make(i, h):
                        at = i * (2 * GK) + h * GK
                        ins = dve.tensor_tensor(mark[h][:, :, :], across(iota[:, :], GK),
                                                along(dlo[:, bass.ds(at, GK)], P), ALU.is_equal)
                        if dots is None:
                            ins.then_inc(s_oh[h], 1)
                            return
                        link(ins)
                        for j in range(GK):
                            blk = dve.value_load(blk64[0:1, bass.ds(at + j, 1)], min_val=0, max_val=(NBR - 1) * D)
                            last = dve.scalar_tensor_tensor(prod_[:, j, :], mark[h][:, j, :], 1.0,
                                                            dots[:, bass.ds(blk * 2, P)], ALU.mult, ALU.mult,
                                                            accum_out=de[:, j:j + 1])
                        link(last)
                        dve.wait_ge(s_got[h], (i + 1) * (16 * GK))
                        link(dve.tensor_tensor(de[:, :], de[:, :], rows[h][:, :, D], ALU.add))
                        link(dve.scalar_tensor_tensor(sc[:, :], de[:, :], 0.2, de[:, :], ALU.mult, ALU.max))
                        link(dve.tensor_tensor(sc[:, :], sc[:, :], rows[h][:, :, D + 1], ALU.subtract))
                        dve.tensor_scalar(sc[:, :], sc[:, :], 0.0, None, ALU.min).then_inc(s_z, 1)
                        dve.wait_ge(s_x, i * 2 + h + 1)
                        dve.tensor_tensor(mark[h][:, :, :], mark[h][:, :, :], along(sc[:, :], P),
                                          ALU.mult).then_inc(s_oh[h], 1)
                    per = 0 if dots is None else 5
                    for h in range(2):
                        make(0, h)

                    def turn(i, beside):
                        for h in range(2):
                            dve.wait_ge(s_use[h], i + 1)
                            make(i + 1, h)
                            if beside:
                                side.dve(dve, link, i, h)
                    first = 0
                    if side is not None:
                        side.before(dve, link)
                        turn(0, True)
                        n0 = link.base + link.n
                        with dve.Fori(1, side.turns) as i:
                            link.enter(i - 1, 2 * per + side.per)
                            turn(i, True)
                        link.leave(n0, side.turns - 1)
                        first = side.turns
                    n0 = link.base + link.n
                    with dve.Fori(first, GI - 1) as i:
                        link.enter(i - first, 2 * per)
                        turn(i, False)
                    link.leave(n0, GI - 1 - first)
                    if side is not None:
                        side.after(dve, link)
                    for h in range(2):
                        dve.wait_ge(s_use[h], GI)
                    dve.tensor_copy(S[:, 32:NB, 0:D], acc[:, 32 * D:NB * D].rearrange("p (b f) -> p b f", f=D))

                @block.sync
                def _(sp):
                    if side is not None:
                        side.sp(sp)

                @block.tensor
                def _(pe):
                    for b in range(7):
                        pe.matmul(acc[:, b * 512:(b + 1) * 512], zero[:, 0:P], zero[:, :], start=True, stop=True)

                    def turn(i, beside):
                        for h in range(2):
                            pe.wait_ge(s_oh[h], i + 1)
                            pe.wait_ge(s_got[h], (i + 1) * (16 * GK))
                            for j in range(GK):
                                at = pe.value_load(blk64[0:1, bass.ds(i * (2 * GK) + (h * GK + j), 1)],
                                                   min_val=0, max_val=(NBR - 1) * D)
                                last = pe.matmul(acc[:, bass.ds(at, D)], mark[h][:, j, :], rows[h][:, j, 0:D],
                                                 start=False, stop=True, skip_group_check=True)
                            last.then_inc(s_use[h], 1)
                    first = 0
                    if side is not None:
                        first = side.turns
                        side.before_pe(pe)
                        with pe.Fori(0, first) as i:
                            turn(i, True)
                    with pe.Fori(first, GI) as i:
                        turn(i, False)

        def norm_tiles(st, tag):
            return [sb(st, tag + n, s) for n, s in (("t3", [P, NB, D]), ("m1", [P, NB]), ("v1", [P, NB]), ("sd", [P, NB]))]

        def norm_dve(dve, link, tiles, s_var, s_dev):
            t3, m1, v1, sd = tiles
            feat = S[:, :, D:2 * D]
            link(dve.tensor_reduce(m1[:, :], X[:, :, :], AX.X, ALU.add))
            link(dve.tensor_scalar(m1[:, :], m1[:, :], 1.0 / D, None, ALU.mult))
            link(dve.tensor_tensor(feat, X[:, :, :], along(m1[:, :], D), ALU.subtract))
            link(dve.tensor_tensor(t3[:, :, :], feat, feat, ALU.mult))
            link(dve.tensor_reduce(v1[:, :], t3[:, :, :], AX.X, ALU.add))
            dve.tensor_scalar(v1[:, :], v1[:, :], 1.0 / D, 1e-5, ALU.mult, ALU.add).then_inc(s_var, 1)
            dve.wait_ge(s_dev, 1)
            link(dve.reciprocal(sd[:, :], sd[:, :]))
            link(dve.tensor_scalar(feat, feat, 0.0, None, ALU.max))
            link(dve.tensor_tensor(feat, feat, along(sd[:, :], D), ALU.mult))

        def norm_act(act, tiles, s_var, s_dev):
            act.wait_ge(s_var, 1)
            act.activation(tiles[3][:, :], tiles[2][:, :], ACT.Sqrt).then_inc(s_dev, 1)

        dsrt = sb(top, "dsrt", [EP, T])
        ssrt = sb(top, "ssrt", [EP, EC + 1])
        keep = sb(top, "keep", [EP, EC])
        keepM = sb(top, "keepM", [EP, EC])
        whole = sb(top, "whole", [EP, 1])
        endI = sb(top, "endI", [P, NB], I32)
        state = sb(top, "state", [EP, 2 * FA])

        def carries(bank_, dve, link, width, turned, rows_, back, rowT, contT, carryR, out_ap, sums):
            dve.wait_ge(*turned)
            link(dve.tensor_copy(rowT[:, :], bank_[0:width, 0:EP]))
            link(dve.tensor_copy(contT[:, :], bank_[0:width, 128:128 + EP]))
            if sums < width:
                link(dve.tensor_scalar(contT[sums:width, :], contT[sums:width, :], 2.0, 1.0, ALU.mult, ALU.subtract))
                link(dve.tensor_scalar(contT[sums:width, :], contT[sums:width, :], BIG, None, ALU.mult))
                link(dve.memset(carryR[sums:width, 0:1], -BIG))
                link(dve.tensor_tensor_scan(carryR[sums:width, 1:EP + 1], contT[sums:width, :], rowT[sums:width, :],
                                            -BIG, ALU.min, ALU.max))
            if sums:
                link(dve.memset(carryR[0:sums, 0:1], 0.0))
                link(dve.tensor_tensor_scan(carryR[0:sums, 1:EP + 1], contT[0:sums, :], rowT[0:sums, :],
                                            0.0, ALU.mult, ALU.add))
            dve.sem_inc(rows_[0], 1)
            dve.wait_ge(*back)
            link(dve.tensor_copy(out_ap, bank_[0:EP, 256:256 + width]))

        def carries_pe(pe, bank_, tails, cont, carryR, width, tail, turned, rows_, back):
            pe.wait_ge(*tail)
            pe.transpose(bank_[0:width, 0:EP], tails, ident[0:EP, 0:EP])
            pe.transpose(bank_[0:width, 128:128 + EP], cont, ident[0:EP, 0:EP]).then_inc(turned[0], 1)
            pe.wait_ge(*rows_)
            pe.transpose(bank_[0:EP, 256:256 + width], carryR[:, 0:EP], ident[0:width, 0:width]).then_inc(back[0], 1)

        class Side:

            per = 0

            def sp(self, sp): pass

            def before(self, dve, link): pass

            def before_pe(self, pe): pass

            def dve(self, dve, link, i, h): pass

            def pe(self, pe, i, h): pass

            def act(self, act, i, h): pass

            def after(self, dve, link): pass

        class Scans(Side):

            turns, per = EC // SLAB, 0

            def __init__(self, st, rnd):
                self.rnd, self.per = rnd, (7 if rnd == 0 else 2)
                (self.s_in, self.s_us, self.s_wr, self.s_pv) = sems(st, *(f"k{rnd}_" + n for n in (
                    "slab", "used", "stored", "before")))
                self.slab = sb(st, "slab", [EP, SLAB, SRT_W])
                self.res = sb(st, "res", [EP, SLAB, 2 * FA])

            def sp(self, sp):
                sv = srt_d.rearrange("(p c) w -> p c w", p=EP)
                gv = seg_d.rearrange("(p c) w -> p (c w)", p=EP)
                if self.rnd == 0:
                    sp.dma_start(ssrt[1:EP, 0:1], sv[0:EP - 1, EC - 1, FA + 1:FA + 2],
                                 allow_slow_non_contiguous=True).then_inc(self.s_pv, 16)
                with sp.Fori(0, self.turns) as i:
                    sp.wait_ge(self.s_us, i + 1)
                    sp.dma_start(self.slab[:, :, :], sv[:, bass.ds(i * SLAB, SLAB), :]).then_inc(self.s_in, 16)
                    if self.rnd:
                        sp.wait_ge(self.s_us, i + 2)
                        sp.dma_start(gv[:, bass.ds(i * (SLAB * 2 * FA), SLAB * 2 * FA)],
                                     self.res[:, :, :].rearrange("p c w -> p (c w)")).then_inc(self.s_wr, 16)
                if self.rnd:
                    sp.wait_ge(self.s_wr, 16 * self.turns)

            def before(self, dve, link):
                dve.sem_inc(self.s_us, 1)
                if self.rnd == 0:
                    link(dve.memset(dsrt[:, :], NO_NODE * P))
                    link(dve.memset(state[:, 0:FA], 0.0))
                    link(dve.memset(state[:, FA:2 * FA], -BIG))
                    link(dve.memset(ssrt[0:1, 0:1], -1.0))
                    dve.wait_ge(self.s_pv, 16)

            def dve(self, dve, link, i, h):
                if h:
                    return
                slab, res = self.slab, self.res
                dve.wait_ge(self.s_in, 16 * (i + 1))
                at = i * SLAB
                now = bass.ds(at, SLAB)
                if self.rnd == 0:
                    link(dve.tensor_copy(dsrt[:, now], slab[:, :, FA]))
                    link(dve.tensor_copy(ssrt[:, bass.ds(at + 1, SLAB)], slab[:, :, FA + 1]))
                    link(dve.tensor_tensor(keep[:, now], ssrt[:, bass.ds(at + 1, SLAB)], ssrt[:, now], ALU.is_equal))
                    link(dve.tensor_scalar(keepM[:, now], keep[:, now], 2.0, 1.0, ALU.mult, ALU.subtract))
                    link(dve.tensor_scalar(keepM[:, now], keepM[:, now], BIG, None, ALU.mult))
                elif not isinstance(i, int):
                    dve.wait_ge(self.s_wr, 16 * i)
                for f in range(FA):
                    dve.tensor_tensor_scan(res[:, :, f], keep[:, now], slab[:, :, f], state[:, f:f + 1],
                                           ALU.mult, ALU.add)
                    last = dve.tensor_tensor_scan(res[:, :, FA + f], keepM[:, now], slab[:, :, f],
                                                  state[:, FA + f:FA + f + 1], ALU.min, ALU.max)
                link(last)
                link(dve.tensor_copy(state[:, :], res[:, SLAB - 1, :]))
                dve.sem_inc(self.s_us, 1)

        def bridge():
            with Phase() as ph:
                (s_v, s_tail, s_turn, s_row, s_back) = sems(ph, "v_dve", "v_tails", "v_turned", "v_rows", "v_back")
                contE = sb(ph, "contE", [EP, 2 * FA])
                rowT = sb(ph, "rowT", [2 * FA, EP])
                contT = sb(ph, "contT", [2 * FA, EP])
                carryR = sb(ph, "carryR", [2 * FA, EP + 1])
                fin = sb(ph, "fin", [P, NB])
                pc = pb(ph, [P, 512])
                block = ph.enter_context(nc.Block())

                @block.vector
                def _(dve):
                    link = Chain(dve, s_v)
                    link(dve.tensor_reduce(whole[:, :], keep[:, :], AX.X, ALU.min))
                    dve.tensor_copy(contE[:, :], whole[:, 0:1].broadcast_to((EP, 2 * FA))).then_inc(s_tail, 1)
                    carries(pc, dve, link, 2 * FA, (s_turn, 1), (s_row, 1), (s_back, 1), rowT, contT, carryR,
                            state[:, :], FA)
                    link(dve.tensor_tensor(fin[:, :], st_src[:, :], cn_src[:, :], ALU.add))
                    dve.tensor_scalar(endI[:, :], fin[:, :], 1.0, 0.0, ALU.subtract, ALU.max)

                @block.tensor
                def _(pe):
                    carries_pe(pe, pc, state[:, :], contE[:, :], carryR, 2 * FA, (s_tail, 1), (s_turn, 1),
                               (s_row, 1), (s_back, 1))

        l0 = ExitStack()
        with l0:
            Wg = sb(l0, "Wg", [P, 4 * D])
            Wt = sb(l0, "Wt", [P, KT * D])
            bg = sb(l0, "bg", [P, 4 * D])
            bt = sb(l0, "bt", [P, KT * D])
            with Phase() as ph:
                (s_ld, s_v, s_var, s_dev, s_z, s_tp, s_g) = sems(
                    ph, "d_load", "d_dve", "d_var", "d_dev", "d_zero", "d_transposed", "d_pool")
                raw = sb(ph, "raw", [P, 4, 2 * D])
                brow = sb(ph, "brow", [1, 3, 4 * D])
                tiles = norm_tiles(ph, "d_")
                psw = pb(ph, [P, 4, P])
                psr = pb(ph, [P, 2, 4 * D])
                block = ph.enter_context(nc.Block())

                @block.gpsimd
                def _(pool):
                    pool.memset(raw[:, :, :], 0.0).then_inc(s_z, 1)
                    pool.memset(brow[:, :, :], 0.0).then_inc(s_z, 1)
                    pool.memset(S[:, :, 0:D], 0.0)

                @block.sync
                def _(sp):
                    sp.wait_ge(s_g, 1)
                    sp.dma_start(X[:, 0:NBR - 1, :], x[0:(NBR - 1) * P, :].rearrange("(b p) f -> p b f", p=P)).then_inc(s_ld, 16)
                    sp.dma_start(X[0:N - (NBR - 1) * P, NBR - 1, :], x[(NBR - 1) * P:N, :]).then_inc(s_ld, 16)
                    sp.wait_ge(s_z, 2)
                    W0v = W0.rearrange("k h d -> (k h) d")
                    for dst_ap, src_ap in (
                            (raw[:, 0, 0:D], wih[0:2 * D, :]), (raw[:, 0, D:2 * D], whh[0:2 * D, :]),
                            (raw[0:D, 1, 0:D], wih[2 * D:3 * D, :]), (raw[D:2 * D, 1, D:2 * D], whh[2 * D:3 * D, :]),
                            (raw[:, 2, D:2 * D], W0v[0:P, :]), (raw[:, 3, D:2 * D], W0v[P:2 * P, :]),
                            (brow[:, 0, 0:3 * D], bih.rearrange("(a n) -> a n", a=1)),
                            (brow[:, 1, 0:2 * D], bhh[0:2 * D].rearrange("(a n) -> a n", a=1)),
                            (brow[:, 1, 3 * D:4 * D], bhh[2 * D:3 * D].rearrange("(a n) -> a n", a=1)),
                            (brow[:, 2, :], b0.rearrange("k h -> (k h)").rearrange("(a n) -> a n", a=1))):
                        sp.dma_start(dst_ap, src_ap).then_inc(s_ld, 16)

                @block.tensor
                def _(pe):
                    pe.wait_ge(s_ld, 12 * 16)
                    for k in range(4):
                        pe.transpose(psw[:, k, :], raw[:, k, :], ident[:, :])
                    pe.matmul(psr[:, 0, :], ones[0:1, :], brow[:, 0, :], start=True, stop=False)
                    pe.matmul(psr[:, 0, :], ones[0:1, :], brow[:, 1, :], start=False, stop=True)
                    pe.matmul(psr[:, 1, :], ones[0:1, :], brow[:, 2, :], start=True, stop=True).then_inc(s_tp, 1)

                @block.scalar
                def _(act):
                    norm_act(act, tiles, s_var, s_dev)

                @block.vector
                def _(dve):
                    link = Chain(dve, s_v)
                    dve.memset(X[:, NBR - 1:NB, :], 0.0).then_inc(s_g, 1)
                    dve.wait_ge(s_ld, 12 * 16)
                    norm_dve(dve, link, tiles, s_var, s_dev)
                    dve.wait_ge(s_tp, 1)
                    dve.tensor_copy(Wg[:, :].rearrange("p (k m) -> p k m", k=2), psw[:, 0:2, :])
                    dve.tensor_copy(Wt[:, :].rearrange("p (k m) -> p k m", k=2), psw[:, 2:4, :])
                    dve.tensor_copy(bg[:, :], psr[:, 0, :])
                    dve.tensor_copy(bt[:, :], psr[:, 1, :])

            def unit(tag, gated, messages):
                with Phase() as ph:
                    (s_in, s_t1, s_c1, s_gt, s_sm, s_sig, s_pre, s_tan, s_new, s_t2, s_c2, s_ms, s_mo, s_out, s_v) = sems(
                        ph, *(tag + n for n in ("staged", "turned", "sbuf", "gates", "biased", "sigmoid", "pretanh", "tanh",
                                                "feat", "turned2", "sbuf2", "msgs", "msgsb", "stored", "dve")))
                    stg = sb(ph, "stg", [P, LOT, 2 * D])
                    stT = sb(ph, "stT", [P, LOT, P])
                    gb = sb(ph, "gb", [P, LOT, 4 * D])
                    nn = sb(ph, "nn", [P, LOT, D])
                    mo = [sb(ph, f"mo{k}", [P, LOT, KT * D]) for k in range(2)]
                    pst = pb(ph, [P, 8, P])
                    psg = pb(ph, [P, 6, 4 * D])
                    psm = pb(ph, [P, 6, 4 * D])
                    block = ph.enter_context(nc.Block())
                    mv = msg_d.rearrange("(b p k) f -> p b (k f)", p=P, k=KT)
                    per = (4 if gated else 0)

                    @block.vector
                    def _(dve):
                        link = Chain(dve, s_v)
                        with dve.Fori(0, NL) as i:
                            link.enter(i, per)
                            lot = bass.ds(i * LOT, LOT)
                            dve.tensor_copy(stg[:, :, :], S[:, lot, :]).then_inc(s_in, 1)
                            if gated:
                                dve.wait_ge(s_gt, i + 1)
                                dve.tensor_tensor(gb[:, :, :], psg[:, 0:LOT, :], across(bg[:, :], LOT),
                                                  ALU.add).then_inc(s_sm, 1)
                                dve.wait_ge(s_sig, i + 1)
                                link(dve.tensor_tensor(nn[:, :, :], gb[:, :, 0:D], gb[:, :, 3 * D:4 * D], ALU.mult))
                                dve.tensor_tensor(nn[:, :, :], nn[:, :, :], gb[:, :, 2 * D:3 * D],
                                                  ALU.add).then_inc(s_pre, 1)
                                dve.wait_ge(s_tan, i + 1)
                                link(dve.tensor_tensor(gb[:, :, 0:D], stg[:, :, D:2 * D], nn[:, :, :], ALU.subtract))
                                link(dve.tensor_tensor(gb[:, :, 0:D], gb[:, :, 0:D], gb[:, :, D:2 * D], ALU.mult))
                                link(dve.tensor_tensor(stg[:, :, D:2 * D], gb[:, :, 0:D], nn[:, :, :], ALU.add))
                                dve.tensor_copy(S[:, lot, D:2 * D], stg[:, :, D:2 * D]).then_inc(s_new, 1)
                                dve.wait_ge(s_new, i + 1)
                            if messages:
                                dve.wait_ge(s_ms, i + 1)
                                dve.tensor_tensor(mo[0][:, :, :], psm[:, 0:LOT, :], across(bt[:, :], LOT),
                                                  ALU.add).then_inc(s_mo, 1)
                                dve.wait_ge(s_out, (i + 1) * 16)
                        link.leave(0, NL)

                    @block.tensor
                    def _(pe):
                        with pe.Fori(0, NL) as i:
                            if gated:
                                pe.wait_ge(s_in, i + 1)
                                for k in range(LOT):
                                    last = pe.transpose(pst[:, k, :], stg[:, k, :], ident[:, :])
                                last.then_inc(s_t1, 1)
                                pe.wait_ge(s_c1, i + 1)
                                for k in range(LOT):
                                    last = pe.matmul(psg[:, k, :], stT[:, k, :], Wg[:, :], start=True, stop=True)
                                last.then_inc(s_gt, 1)
                                pe.wait_ge(s_new, i + 1)
                            else:
                                pe.wait_ge(s_in, i + 1)
                            if messages:
                                for k in range(LOT):
                                    last = pe.transpose(pst[:, k, :], stg[:, k, :], ident[:, :])
                                last.then_inc(s_t2, 1)
                                pe.wait_ge(s_c2, i + 1)
                                for k in range(LOT):
                                    last = pe.matmul(psm[:, k, :], stT[:, k, :], Wt[:, :], start=True, stop=True)
                                last.then_inc(s_ms, 1)

                    @block.scalar
                    def _(act):
                        with act.Fori(0, NL) as i:
                            if gated:
                                act.wait_ge(s_t1, i + 1)
                                act.activation(stT[:, :, :], pst[:, 0:LOT, :], ACT.Copy).then_inc(s_c1, 1)
                                act.wait_ge(s_sm, i + 1)
                                act.activation(gb[:, :, 0:2 * D], gb[:, :, 0:2 * D], ACT.Sigmoid).then_inc(s_sig, 1)
                                act.wait_ge(s_pre, i + 1)
                                act.activation(nn[:, :, :], nn[:, :, :], ACT.Tanh).then_inc(s_tan, 1)
                            if messages:
                                act.wait_ge(s_t2, i + 1)
                                act.activation(stT[:, :, :], pst[:, 0:LOT, :], ACT.Copy).then_inc(s_c2, 1)

                    @block.sync
                    def _(sp):
                        if messages:
                            with sp.Fori(0, NL) as i:
                                sp.wait_ge(s_mo, i + 1)
                                sp.dma_start(mv[:, bass.ds(i * LOT, LOT), :], mo[0][:, :, :]).then_inc(s_out, 16)

            unit("e_", False, True)
            for step in range(STEPS):
                with Phase() as ph:
                    gather_pass(f"f{step}_", msg_d, src4, side=Scans(ph, step) if step < 2 else None)
                if step == 0:
                    bridge()
                unit(f"g{step}_", True, step < STEPS - 1)
        with ExitStack() as late:
            l1 = late.enter_context(ExitStack())
            H = sb(l1, "H", [P, NB, D + 2])
            a_s = sb(l1, "a_s", [P, 2, NB])
            sm = sb(l1, "sm", [P, 2, NB])
            with Phase() as ph:
                (s_ld, s_z, s_v, s_var, s_dev, s_tp, s_w, s_in, s_t, s_c, s_h, s_hc) = sems(
                    ph, *("l_" + n for n in ("load", "zero", "dve", "var", "dev", "turned", "weights", "staged", "turned2",
                                             "sbuf", "products", "copied")))
                raw = sb(ph, "raw", [P, 2 * D])
                ar = sb(ph, "ar", [1, 2 * D])
                ab = sb(ph, "ab", [P, 2 * D])
                Wh = sb(ph, "Wh", [P, D])
                stg = sb(ph, "stg", [P, LOT, 2 * D])
                stT = sb(ph, "stT", [P, LOT, P])
                tiles = norm_tiles(ph, "l_")
                psw = pb(ph, [P, 512])
                pst = pb(ph, [P, 8, P])
                psh = pb(ph, [P, LOT, D])
                block = ph.enter_context(nc.Block())

                @block.gpsimd
                def _(pool):
                    pool.memset(raw[:, :], 0.0).then_inc(s_z, 1)

                @block.sync
                def _(sp):
                    sp.wait_ge(s_z, 1)
                    sp.dma_start(raw[0:D, D:2 * D], W1g).then_inc(s_ld, 16)
                    sp.dma_start(ar[:, :], a1).then_inc(s_ld, 16)

                @block.tensor
                def _(pe):
                    pe.wait_ge(s_ld, 32)
                    pe.transpose(psw[:, 0:P], raw[:, :], ident[:, :])
                    pe.matmul(psw[:, 128:128 + 2 * D], ones[0:1, :], ar[:, :], start=True, stop=True).then_inc(s_tp, 1)
                    pe.wait_ge(s_w, 1)
                    with pe.Fori(0, NL) as i:
                        pe.wait_ge(s_in, i + 1)
                        for k in range(LOT):
                            last = pe.transpose(pst[:, k, :], stg[:, k, :], ident[:, :])
                        last.then_inc(s_t, 1)
                        pe.wait_ge(s_c, i + 1)
                        for k in range(LOT):
                            last = pe.matmul(psh[:, k, :], stT[:, k, :], Wh[:, :], start=True, stop=True)
                        last.then_inc(s_h, 1)

                @block.scalar
                def _(act):
                    norm_act(act, tiles, s_var, s_dev)
                    with act.Fori(0, NL) as i:
                        act.wait_ge(s_t, i + 1)
                        act.activation(stT[:, :, :], pst[:, 0:LOT, :], ACT.Copy).then_inc(s_c, 1)

                @block.vector
                def _(dve):
                    link = Chain(dve, s_v)
                    link(dve.tensor_tensor(X[:, :, :], X[:, :, :], S[:, :, D:2 * D], ALU.add))
                    norm_dve(dve, link, tiles, s_var, s_dev)
                    dve.wait_ge(s_tp, 1)
                    dve.tensor_copy(ab[:, :], psw[:, 128:128 + 2 * D])
                    dve.tensor_copy(Wh[:, :], psw[:, 0:D]).then_inc(s_w, 1)
                    with dve.Fori(0, NL) as i:
                        lot = bass.ds(i * LOT, LOT)
                        dve.tensor_copy(stg[:, :, :], S[:, lot, :]).then_inc(s_in, 1)
                        dve.wait_ge(s_h, i + 1)
                        dve.tensor_copy(H[:, lot, 0:D], psh[:, :, :]).then_inc(s_hc, 1)
                    dve.wait_ge(s_hc, NL)
                    t3 = tiles[0]
                    for k in range(2):
                        link(dve.tensor_tensor(t3[:, :, :], H[:, :, 0:D], across(ab[:, k * D:(k + 1) * D], NB), ALU.mult))
                        link(dve.tensor_reduce(a_s[:, k, :], t3[:, :, :], AX.X, ALU.add))
                    link(dve.tensor_copy(sm[:, 0, :], a_s[:, 0, :]))

            def look_up(tag, parts, key, table, outs):
                nv = len(outs)
                per_bank = 5
                with Phase() as ph:
                    s_mk = sems(ph, tag + "marks0", tag + "marks1")
                    (s_v, s_T, s_C, s_L, s_R) = sems(ph, *(tag + n for n in ("dve", "turned", "sbuf", "looked", "read")))
                    kI = sb(ph, "kI", [parts, T], I32)
                    kJ = sb(ph, "kJ", [parts, T], I32)
                    klo = sb(ph, "klo", [parts, T])
                    khi = sb(ph, "khi", [parts, T])
                    lo = [sb(ph, f"lo{h}", [parts, GK, P]) for h in range(2)]
                    hi = [sb(ph, f"hi{h}", [parts, GK, NB]) for h in range(2)]
                    lT = sb(ph, "lT", [P, GK, parts])
                    pr = sb(ph, "pr", [parts, GK, NB])
                    ptt = pb(ph, [P, 4, 512])
                    plk = pb(ph, [P, 3, 512])
                    block = ph.enter_context(nc.Block())
                    groups = [(g * 4, min(4, GK - g * 4)) for g in range(-(-GK // 4))]

                    @block.vector
                    def _(dve):
                        link = Chain(dve, s_v)
                        dve.sem_inc(s_R, 1)
                        link(dve.tensor_copy(kI[:, :], key))
                        dve.tensor_scalar(kJ[:, :], kI[:, :], 7, None, ALU.arith_shift_right)
                        link(dve.tensor_scalar(kI[:, :], kI[:, :], P - 1, None, ALU.bitwise_and))
                        dve.tensor_copy(klo[:, :], kI[:, :])
                        link(dve.tensor_copy(khi[:, :], kJ[:, :]))

                        def marks(h, at):
                            dve.tensor_tensor(lo[h][:, :, :], across(iota[0:parts, :], GK),
                                              along(klo[:, bass.ds(at, GK)], P), ALU.is_equal).then_inc(s_mk[h], 1)
                            dve.tensor_tensor(hi[h][:, :, :], across(iota[0:parts, 0:NB], GK),
                                              along(khi[:, bass.ds(at, GK)], NB), ALU.is_equal).then_inc(s_mk[h], 1)

                        def read(i, h):
                            n = i * 2 + h
                            dve.wait_ge(s_L, n + 1)
                            for v in range(nv):
                                for b0, nb, k in ((0, 2, 10), (2, 1, 3)):
                                    w = nv * NB
                                    src_ap = plk[0:parts, b0:b0 + nb, 0:(k // nb) * w].rearrange(
                                        "p b (k w) -> p b k w", w=w)[:, :, :, v * NB:(v + 1) * NB]
                                    o = pr[:, b0 * 5:b0 * 5 + k, :]
                                    m = hi[h][:, b0 * 5:b0 * 5 + k, :]
                                    if nb == 2:
                                        for bb in range(2):
                                            ins = dve.tensor_tensor(pr[:, bb * 5:bb * 5 + 5, :], src_ap[:, bb, :, :],
                                                                    hi[h][:, bb * 5:bb * 5 + 5, :], ALU.mult)
                                    else:
                                        ins = dve.tensor_tensor(o, src_ap[:, 0, :, :], m, ALU.mult)
                                link(ins)
                                ins = dve.tensor_reduce(outs[v][:, bass.ds(i * (2 * GK) + h * GK, GK)], pr[:, :, :],
                                                        AX.X, ALU.add)
                                link(ins)
                            dve.sem_inc(s_R, 1)
                        marks(0, 0)
                        n0 = link.base + link.n
                        with dve.Fori(0, GI - 1) as i:
                            link.enter(i, 4 * nv)
                            marks(1, i * (2 * GK) + GK)
                            read(i, 0)
                            marks(0, i * (2 * GK) + 2 * GK)
                            read(i, 1)
                        link.leave(n0, GI - 1)
                        marks(1, T - GK)
                        read(GI - 1, 0)
                        read(GI - 1, 1)

                    @block.tensor
                    def _(pe):
                        with pe.Fori(0, GI) as i:
                            for h in range(2):
                                n = i * 2 + h
                                pe.wait_ge(s_mk[h], (i + 1) * 2)
                                for j in range(GK):
                                    last = pe.transpose(ptt[:, j // 4, (j % 4) * P:(j % 4) * P + parts], lo[h][:, j, :],
                                                        ident[0:parts, 0:parts])
                                last.then_inc(s_T, 1)
                                pe.wait_ge(s_C, n + 1)
                                pe.wait_ge(s_R, n + 1)
                                for j in range(GK):
                                    w = nv * NB
                                    at = (j % per_bank) * w
                                    last = pe.matmul(plk[0:parts, j // per_bank, at:at + w], lT[:, j, :],
                                                     table, start=True, stop=True)
                                last.then_inc(s_L, 1)

                    @block.scalar
                    def _(act):
                        with act.Fori(0, GI) as i:
                            for h in range(2):
                                n = i * 2 + h
                                act.wait_ge(s_T, n + 1)
                                for g0, k in groups:
                                    ins = act.activation(
                                        lT[:, g0:g0 + k, :],
                                        ptt[:, g0 // 4, 0:k * P].rearrange("p (k e) -> p k e", e=P)[:, :, 0:parts],
                                        ACT.Copy)
                                ins.then_inc(s_C, 1)

            dval = sb(l1, "dval", [EP, T])
            look_up("m_", EP, dsrt[:, :], a_s[:, 1, :], [dval])

            dots = sb(l1, "dots", [P, NBR * P])
            with Phase() as ph:
                (s_v, s_tail, s_turn, s_row, s_back, s_mx, s_wr, s_z, s_zw, s_pr, s_pl, s_sc, s_ex, s_sm, s_sw, s_rw, s_rs,
                 s_id) = sems(
                    ph, *("n_" + n for n in ("dve", "tails", "turned", "rows", "back", "maxima", "stored", "zero", "zeroed",
                                             "pairs", "loaded", "scores", "exp", "sums", "sumsstored", "table",
                                             "tablestored", "nodes")))
                (s_g, s_p, s_g2) = dma_sems("n_largest", "n_placed", "n_summed")
                mx = sb(ph, "mx", [EP, EC])
                two = sb(ph, "two", [EP, EC, 2])
                se = sb(ph, "se", [EP, EC])
                me = sb(ph, "me", [EP, EC])
                c1 = sb(ph, "c1", [EP, 1])
                rowT = sb(ph, "rowT", [1, EP])
                contT = sb(ph, "contT", [1, EP])
                carryR = sb(ph, "carryR", [1, EP + 1])
                md = sb(ph, "md", [P, NB])
                md2 = sb(ph, "md2", [P, NB])
                has = sb(ph, "has", [P, NB])
                e5 = sb(ph, "e5", [P, NB])
                node = sb(ph, "node", [P, NB])
                pidx = sb(ph, "pidx", [P, NB], I32)
                pair = sb(ph, "pair", [P, NB, 2])
                den = sb(ph, "den", [P, NB])
                pc = pb(ph, [P, 512])
                block = ph.enter_context(nc.Block())

                @block.vector
                def _(dve):
                    link = Chain(dve, s_v)
                    dve.memset(two[:, :, :], 0.0).then_inc(s_z, 1)
                    link(dve.tensor_scalar(has[:, :], cn_src[:, :], 1.0, None, ALU.min))
                    dve.wait_ge(s_id, 1)
                    link(dve.tensor_scalar(node[:, :], node[:, :], float(E), None, ALU.add))
                    link(dve.tensor_tensor(md[:, :], st_src[:, :], node[:, :], ALU.subtract))
                    link(dve.tensor_tensor(md[:, :], md[:, :], has[:, :], ALU.mult))
                    link(dve.tensor_tensor(pidx[:, :], md[:, :], node[:, :], ALU.add))

                    def carried(n, tail_at, sums):
                        carries(pc, dve, link, 1, (s_turn, n), (s_row, n), (s_back, n), rowT, contT, carryR, c1[:, 0:1],
                                sums)
                    dve.tensor_tensor_scan(mx[:, :], keepM[:, :], dval[:, 0:EC], -BIG, ALU.min, ALU.max).then_inc(s_tail, 1)
                    carried(1, mx, 0)
                    dve.tensor_tensor_scan(mx[:, :], keepM[:, :], dval[:, 0:EC], c1[:, 0:1], ALU.min,
                                           ALU.max).then_inc(s_mx, 1)
                    dve.wait_ge(s_g, 16 * NBR)
                    link(dve.tensor_tensor(e5[:, 0:NBR], md2[:, 0:NBR], a_s[:, 0, 0:NBR], ALU.add))
                    link(dve.scalar_tensor_tensor(e5[:, 0:NBR], e5[:, 0:NBR], 0.2, e5[:, 0:NBR], ALU.mult, ALU.max))
                    link(dve.memset(sm[:, 1, :], 0.0))
                    link(dve.tensor_tensor(sm[:, 1, 0:NBR], e5[:, 0:NBR], has[:, 0:NBR], ALU.mult))
                    link(dve.tensor_copy(pair[:, :, 0], sm[:, 0, :]))
                    dve.tensor_copy(pair[:, :, 1], sm[:, 1, :]).then_inc(s_pr, 1)
                    dve.wait_ge(s_pl, 16)
                    for n, (v, to) in enumerate(((0, se), (1, me))):
                        dve.tensor_tensor_scan(to[:, :], keep[:, :], two[:, :, v], 0.0, ALU.mult, ALU.add).then_inc(s_tail, 1)
                        carried(2 + n, to, 1)
                        link(dve.tensor_tensor_scan(to[:, :], keep[:, :], two[:, :, v], c1[:, 0:1], ALU.mult, ALU.add))
                    link(dve.tensor_tensor(se[:, :], se[:, :], dval[:, 0:EC], ALU.add))
                    link(dve.scalar_tensor_tensor(se[:, :], se[:, :], 0.2, se[:, :], ALU.mult, ALU.max))
                    dve.tensor_tensor(se[:, :], se[:, :], me[:, :], ALU.subtract).then_inc(s_sc, 1)
                    dve.wait_ge(s_ex, 1)
                    dve.tensor_tensor_scan(mx[:, :], keep[:, :], se[:, :], 0.0, ALU.mult, ALU.add).then_inc(s_tail, 1)
                    carried(4, mx, 1)
                    dve.tensor_tensor_scan(mx[:, :], keep[:, :], se[:, :], c1[:, 0:1], ALU.mult, ALU.add).then_inc(s_sm, 1)
                    dve.wait_ge(s_g2, 16 * NBR)
                    link(dve.tensor_scalar(den[:, 0:NBR], den[:, 0:NBR], 0.5, None, ALU.max))
                    link(dve.reciprocal(den[:, 0:NBR], den[:, 0:NBR]))
                    link(dve.memset(den[:, NBR:NB], 1.0))
                    dve.tensor_tensor(H[:, :, 0:D], H[:, :, 0:D], along(den[:, :], D), ALU.mult)
                    link(dve.tensor_copy(H[:, :, D], sm[:, 0, :]))
                    link(dve.tensor_copy(H[:, :, D + 1], sm[:, 1, :]))
                    dve.sem_inc(s_rw, 1)

                @block.scalar
                def _(act):
                    act.wait_ge(s_sc, 1)
                    act.activation(se[:, :], se[:, :], ACT.Exp).then_inc(s_ex, 1)

                @block.tensor
                def _(pe):
                    for n, tile in enumerate((mx, se, me, mx)):
                        k = n + 1
                        carries_pe(pe, pc, tile[:, EC - 1:EC], whole[:, :], carryR, 1, (s_tail, k), (s_turn, k), (s_row, k),
                                   (s_back, k))

                @block.sync
                def _(sp):
                    sp.dma_start(dot_d.rearrange("(b p) -> p b", p=P), a_s[:, 1, :],
                                 allow_slow_non_contiguous=True).then_inc(s_rs, 16)
                    sp.wait_ge(s_rs, 16)
                    sp.dma_start(dots[:, :], dot_d[0:NBR * P].rearrange("(a n) -> a n", a=1).broadcast_to((P, NBR * P))
                                 ).then_inc(s_rs, 16)
                    sp.wait_ge(s_z, 1)
                    sp.dma_start(two_d[0:E, :].rearrange("(p c) w -> p (c w)", p=EP),
                                 two[:, :, :].rearrange("p c w -> p (c w)")).then_inc(s_zw, 16)
                    sp.wait_ge(s_mx, 1)
                    sp.dma_start(mxd_d.rearrange("(p c) w -> p (c w)", p=EP), mx[:, :]).then_inc(s_wr, 16)
                    sp.wait_ge(s_p, 16 * NBR)
                    sp.dma_start(two[:, :, :].rearrange("p c w -> p (c w)"),
                                 two_d[0:E, :].rearrange("(p c) w -> p (c w)", p=EP)).then_inc(s_pl, 16)
                    sp.wait_ge(s_sm, 1)
                    sp.dma_start(sum_d.rearrange("(p c) w -> p (c w)", p=EP), mx[:, :]).then_inc(s_sw, 16)
                    sp.wait_ge(s_rw, 1)
                    sp.dma_start(att_d.rearrange("(b p) f -> p b f", p=P), H[:, :, :]).then_inc(s_rs, 16)
                    sp.wait_ge(s_rs, 48)

                @block.gpsimd
                def _(pool):
                    pool.iota(node[:, :], [[P, NB]], base=0, channel_multiplier=1,
                              allow_small_or_imprecise_dtypes=True).then_inc(s_id, 1)
                    pool.wait_ge(s_wr, 16)
                    for b in range(NBR):
                        pool.indirect_dma_start(md2[:, b:b + 1], None, mxd_d,
                                                bass.IndirectOffsetOnAxis(endI[:, b:b + 1], 0)).then_inc(s_g, 16)
                    pool.wait_ge(s_pr, 1)
                    pool.wait_ge(s_zw, 16)
                    for b in range(NBR):
                        pool.indirect_dma_start(two_d, bass.IndirectOffsetOnAxis(pidx[:, b:b + 1], 0),
                                                pair[:, b, :], None).then_inc(s_p, 16)
                    pool.wait_ge(s_sw, 16)
                    for b in range(NBR):
                        pool.indirect_dma_start(den[:, b:b + 1], None, sum_d,
                                                bass.IndirectOffsetOnAxis(endI[:, b:b + 1], 0)).then_inc(s_g2, 16)
            gather_pass("r_", att_d, srcr, dots)
            l1.close()

            with Phase() as ph:
                (s_v, s_var, s_dev, s_m, s_x, s_rows, s_wr) = sems(
                    ph, *("s_" + n for n in ("dve", "var", "dev", "below", "exp", "rows", "stored")))
                tiles = norm_tiles(ph, "s_")
                block = ph.enter_context(nc.Block())

                @block.vector
                def _(dve):
                    link = Chain(dve, s_v)
                    t3, left = tiles[0], S[:, :, 0:D]
                    dve.tensor_scalar(t3[:, :, :], left, 0.0, None, ALU.min).then_inc(s_m, 1)
                    link(dve.scalar_tensor_tensor(X[:, :, :], left, 0.0, X[:, :, :], ALU.max, ALU.add))
                    dve.wait_ge(s_x, 1)
                    link(dve.scalar_tensor_tensor(X[:, :, :], t3[:, :, :], -1.0, X[:, :, :], ALU.add, ALU.add))
                    norm_dve(dve, link, tiles, s_var, s_dev)
                    dve.sem_inc(s_rows, 1)

                @block.scalar
                def _(act):
                    act.wait_ge(s_m, 1)
                    act.activation(tiles[0][:, :, :], tiles[0][:, :, :], ACT.Exp).then_inc(s_x, 1)
                    norm_act(act, tiles, s_var, s_dev)

                @block.sync
                def _(sp):
                    sp.wait_ge(s_rows, 1)
                    sp.dma_start(row_d.rearrange("(b p) f -> p b f", p=P), S[:, :, D:2 * D]).then_inc(s_wr, 16)
                    sp.wait_ge(s_wr, 16)
            gather_pass("t_", row_d, srcr)

            with Phase() as ph:
                (s_ld, s_v, s_bt, s_f, s_t, s_c, s_h, s_r, s_o, s_g2, s_b) = sems(
                    ph, *("u_" + n for n in ("load", "dve", "bias", "features", "turned", "sbuf", "hidden", "relu", "out",
                                             "added", "biases")))
                (s_g,) = dma_sems("u_gathered")
                K3 = 3 * FA
                sg = sb(ph, "sg", [P, NB, 2 * FA])
                f3 = sb(ph, "f3", [P, NB, K3])
                has = sb(ph, "has", [P, NB])
                rc = sb(ph, "rc", [P, NB])
                w1 = sb(ph, "w1", [K3, HID])
                ur = sb(ph, "ur", [1, 1])
                wu = sb(ph, "wu", [1, HID])
                br = sb(ph, "br", [1, HID])
                w2 = sb(ph, "w2", [HID, D])
                b2r = sb(ph, "b2r", [1, D])
                b2b = sb(ph, "b2b", [P, D])
                b1c = sb(ph, "b1c", [HID, 1])
                stg = sb(ph, "stg", [P, LOT, K3])
                stT = sb(ph, "stT", [K3, LOT, P])
                hd = sb(ph, "hd", [P, LOT, P])
                psb = pb(ph, [P, 512])
                pst = pb(ph, [P, 8, P])
                psh = pb(ph, [P, 8, P])
                pso = pb(ph, [P, LOT, D])
                block = ph.enter_context(nc.Block())

                @block.gpsimd
                def _(pool):
                    for b in range(NBR):
                        pool.indirect_dma_start(sg[:, b, :], None, seg_d,
                                                bass.IndirectOffsetOnAxis(endI[:, b:b + 1], 0)).then_inc(s_g, 16)

                @block.sync
                def _(sp):
                    for dst_ap, src_ap in ((w1[:, :], W13[0:K3, :]), (wu[:, :], W13[K3:K3 + 1, :]), (w2[:, :], W23),
                                           (br[:, :], b13.rearrange("(a n) -> a n", a=1)), (ur[:, :], u3[0:1, :]),
                                           (b2r[:, :], b23.rearrange("(a n) -> a n", a=1))):
                        sp.dma_start(dst_ap, src_ap).then_inc(s_ld, 16)

                @block.vector
                def _(dve):
                    link = Chain(dve, s_v)
                    link(dve.tensor_tensor(X[:, :, :], X[:, :, :], S[:, :, 0:D], ALU.add))
                    dve.tensor_scalar(has[:, :], cn_src[:, :], 1.0, None, ALU.min)
                    link(dve.tensor_scalar(rc[:, :], cn_src[:, :], 1.0, None, ALU.max))
                    link(dve.reciprocal(rc[:, :], rc[:, :]))
                    link(dve.memset(f3[:, NBR:NB, :], 0.0))
                    dve.wait_ge(s_g, 16 * NBR)
                    link(dve.tensor_tensor(f3[:, 0:NBR, 0:2 * FA], sg[:, 0:NBR, :], along(has[:, 0:NBR], 2 * FA), ALU.mult))
                    link(dve.tensor_tensor(f3[:, 0:NBR, 2 * FA:K3], f3[:, 0:NBR, 0:FA], along(rc[:, 0:NBR], FA), ALU.mult))
                    dve.wait_ge(s_bt, 1)
                    dve.tensor_copy(b1c[:, :], psb[:, 0:1])
                    dve.tensor_copy(b2b[:, :], psb[:, 8:8 + D]).then_inc(s_b, 1)
                    dve.wait_ge(s_b, 1)
                    n0 = link.base + link.n
                    with dve.Fori(0, NL) as i:
                        link.enter(i, 1)
                        lot = bass.ds(i * LOT, LOT)
                        dve.tensor_copy(stg[:, :, :], f3[:, lot, :]).then_inc(s_f, 1)
                        link(dve.tensor_tensor(X[:, lot, :], X[:, lot, :], across(b2b[:, :], LOT), ALU.add))
                        dve.wait_ge(s_o, i + 1)
                        dve.tensor_tensor(X[:, lot, :], X[:, lot, :], pso[:, :, :], ALU.add).then_inc(s_g2, 1)
                    link.leave(n0, NL)

                @block.tensor
                def _(pe):
                    pe.wait_ge(s_ld, 6 * 16)
                    pe.matmul(psb[:, 0:1], br[:, :], ones[0:1, 0:1], start=True, stop=False)
                    pe.matmul(psb[:, 0:1], wu[:, :], ur[:, :], start=False, stop=True)
                    pe.matmul(psb[:, 8:8 + D], ones[0:1, :], b2r[:, :], start=True, stop=True).then_inc(s_bt, 1)
                    with pe.Fori(0, NL) as i:
                        pe.wait_ge(s_f, i + 1)
                        for k in range(LOT):
                            last = pe.transpose(pst[0:K3, k, :], stg[:, k, :], ident[:, :])
                        last.then_inc(s_t, 1)
                        pe.wait_ge(s_c, i + 1)
                        for k in range(LOT):
                            last = pe.matmul(psh[:, k, :], w1[:, :], stT[:, k, :], start=True, stop=True)
                        last.then_inc(s_h, 1)
                        pe.wait_ge(s_r, i + 1)
                        for k in range(LOT):
                            last = pe.matmul(pso[:, k, :], hd[:, k, :], w2[:, :], start=True, stop=True)
                        last.then_inc(s_o, 1)

                @block.scalar
                def _(act):
                    act.wait_ge(s_b, 1)
                    with act.Fori(0, NL) as i:
                        act.wait_ge(s_t, i + 1)
                        act.activation(stT[:, :, :], pst[0:K3, 0:LOT, :], ACT.Copy).then_inc(s_c, 1)
                        act.wait_ge(s_h, i + 1)
                        act.activation(hd[:, :, :], psh[:, 0:LOT, :], ACT.Relu, bias=b1c[:, 0:1]).then_inc(s_r, 1)

        with Phase() as ph:
            (s_out,) = sems(ph, "z_out")
            block = ph.enter_context(nc.Block())

            @block.sync
            def _(sp):
                sp.dma_start(out[0:(NBR - 1) * P, :].rearrange("(b p) f -> p b f", p=P), X[:, 0:NBR - 1, :]).then_inc(s_out, 16)
                sp.dma_start(out[(NBR - 1) * P:N, :], X[0:N - (NBR - 1) * P, NBR - 1, :]).then_inc(s_out, 16)
                sp.wait_ge(s_out, 32)


_INS = ["x", "src", "dst", "edge_attr_32", "edge_type_4", "L0_gnn_W", "L0_gnn_b", "L0_gnn_w_ih", "L0_gnn_w_hh",
        "L0_gnn_b_ih", "L0_gnn_b_hh", "L1_gnn_W", "L1_gnn_a", "L3_gnn_u", "L3_gnn_W1", "L3_gnn_b1", "L3_gnn_W2",
        "L3_gnn_b2"]


def kernel(**inputs):
    import numpy as np
    import concourse.bacc as bacc
    from concourse.bass_utils import run_bass_kernel_spmd

    nc = bacc.Bacc("TRN2", target_bir_lowering=False, num_devices=1)
    arrays, args = {}, []
    for name in _INS:
        a = np.ascontiguousarray(inputs[name])
        arrays[f"in_{name}"] = a
        args.append(nc.dram_tensor(f"in_{name}", a.shape, mybir.dt.from_np(a.dtype), kind="ExternalInput").ap())
    args.append(nc.dram_tensor("out_x", (N, D), F32, kind="ExternalOutput").ap())
    build(nc, *args)
    r = run_bass_kernel_spmd(nc, [arrays], core_ids=[0])
    return r.results[0]["out_x"]
```

```python
import concourse.bass as bass
from concourse import mybir
from contextlib import ExitStack
from itertools import count
from math import prod

F32 = mybir.dt.float32
BF16 = mybir.dt.bfloat16
I32 = mybir.dt.int32
ALU = mybir.AluOpType
ACT = mybir.ActivationFunctionType
AX = mybir.AxisListType

P = 128
N = 6250
NBR = -(-N // P)
NB = 50
NP = NB * P
D = 64
FA = 32
KT = 4
STEPS = 4
E = 200000
EP = 125
EC = E // EP
GK = 13
T = 1612
GI = T // (2 * GK)
SK = 10
SI = EC // (2 * SK)
SEGS = (120, 280, 400, 400, 400)
LK = 16
LI = 18
LP = EC - LI * 4 * LK
PK = 14
PI = LP // (2 * PK)
LOT = 5
NL = NB // LOT
SLAB = 32
HID = 128
REC_W = 4
SRT_W = FA + 2
BIG = 3.4028234663852886e38
NO_NODE = 255.0
assert sum(SEGS) == EC and PI * 2 * PK == LP and (E + NBR * (P - 1)) // P <= T and EP * EC == E and T % (2 * GK) == 0 and EC % (2 * SK) == 0


class Chain:

    def __init__(self, eng, sem):
        self.eng, self.sem, self.n, self.base = eng, sem, 0, 0

    def __call__(self, ins):
        self.n += 1
        ins.then_inc(self.sem, 1)
        self.eng.wait_ge(self.sem, self.base + self.n)

    def enter(self, i, per):
        self.base, self.n, self.per = self.base + self.n + i * per, 0, per
        self.after = None

    def leave(self, base0, turns):
        assert self.n == self.per, (self.n, self.per)
        self.base, self.n = base0 + turns * self.per, 0


def build(nc, x, src, dst, attr, etype, W0, b0, wih, whh, bih, bhh, W1g, a1, u3, W13, b13, W23, b23, out):
    top = ExitStack()

    class Phase(ExitStack):

        def __init__(self):
            super().__init__()
            self.held = []
            self.callback(self.tidy)

        def tidy(self):
            for s in self.held:
                nc.gpsimd.sem_clear(s)
            nc.all_engine_barrier()
            for s in self.held:
                nc.release_semaphore(s)

    def sems(st, *names):
        made_here = [nc.alloc_semaphore(n) for n in names]
        st.held += made_here
        return made_here

    def dma_sems(*names):
        return [nc.alloc_semaphore(n) for n in names]

    made = count()

    def sb(st, name, shape, dt=F32):
        return st.enter_context(nc.sbuf_tensor(f"{name}_{next(made)}", shape, dt))

    ps_all = top.enter_context(nc.psum_tensor("ps_all", [P, 8 * 512], F32))
    bank = [0]

    def pb(st, shape):
        size = prod(shape[1:])
        at = bank[0]
        bank[0] += -(-size // 512)
        assert bank[0] <= 8
        st.callback(bank.__setitem__, 0, at)
        view = ps_all[0:shape[0], at * 512:at * 512 + size]
        return view.rearrange("p (a b) -> p a b", a=shape[1]) if len(shape) == 3 else view

    def along(ap, n):
        p, k = ap.shape
        return ap.rearrange("p (k a) -> p k a", a=1).broadcast_to((p, k, n))

    def across(ap, k):
        p, n = ap.shape
        return ap.rearrange("p (a n) -> p a n", a=1).broadcast_to((p, k, n))

    with top:
        rec_d = nc.dram_tensor("rec_d", (P, T * REC_W), I32).ap()
        msg_d = nc.dram_tensor("msg_d", (NP * KT, D), F32).ap()
        row_d = nc.dram_tensor("row_d", (NP, D), F32).ap()
        srt_d = nc.dram_tensor("srt_d", (E, SRT_W), F32).ap()
        seg_d = nc.dram_tensor("seg_d", (E, 2 * FA), F32).ap()
        mxd_d = nc.dram_tensor("mxd_d", (E, 1), F32).ap()
        sum_d = nc.dram_tensor("sum_d", (E, 1), F32).ap()
        two_d = nc.dram_tensor("two_d", (E + NP, 2), F32).ap()
        dot_d = nc.dram_tensor("dot_d", (NP,), F32).ap()
        att_d = nc.dram_tensor("att_d", (NP, D + 2), F32).ap()

        iota = sb(top, "iota", [P, P])
        ident = sb(top, "ident", [P, P])
        tri = sb(top, "tri", [P, P])
        ones = sb(top, "ones", [P, P])
        zero = sb(top, "zero", [P, 512])
        src4 = sb(top, "src4", [P, T], I32)
        srcr = sb(top, "srcr", [P, T], I32)
        dlo = sb(top, "dlo", [P, T])
        blk64 = sb(top, "blk64", [1, T], I32)
        st_src = sb(top, "st_src", [P, NB])
        cn_src = sb(top, "cn_src", [P, NB])

        with Phase() as ph:
            (s_c, s_tri, s_ld, s_cnt, s_cs, s_base, s_bt, s_ge, s_br, s_df, s_v, s_z) = sems(
                ph, "a_const", "a_tri", "a_load", "a_counts", "a_sums", "a_starts", "a_startsT", "a_reached",
                "a_blocks", "a_defaults", "a_dve", "a_zero")
            (s_def,) = sems(ph, "a_stored")
            dstI = sb(ph, "dstI", [EP, EC], I32)
            srcI = sb(ph, "srcI", [EP, EC], I32)
            etI = sb(ph, "etI", [EP, EC], I32)
            tmpI = sb(ph, "tmpI", [EP, EC], I32)
            posI = sb(ph, "posI", [EP, EC], I32)
            pay = sb(ph, "pay", [EP, EC, REC_W], I32)
            cnt = sb(ph, "cnt", [EP, NB])
            pre = sb(ph, "pre", [EP, NB])
            tot = sb(ph, "tot", [P, NB])
            totI = sb(ph, "totI", [P, NB], I32)
            nch = sb(ph, "nch", [P, NB])
            cs = sb(ph, "cs", [P, NB])
            base = sb(ph, "base", [P, NB])
            hiF = sb(ph, "hiF", [EP, EC])
            csT = sb(ph, "csT", [NBR, 1])
            with Phase() as p0:
                m = [sb(p0, f"m{h}", [EP, EC]) for h in range(2)]
                dflt = sb(p0, "dflt", [P, T, REC_W], I32)
                ioT = sb(p0, "ioT", [NBR, T])
                reach = sb(p0, "reach", [NBR, T])
                ps = pb(p0, [P, 2, 512])
                psb = pb(p0, [1, 4, 512])
                block = p0.enter_context(nc.Block())

                @block.gpsimd
                def _(pool):
                    pool.iota(iota[:, :], [[1, P]], base=0, channel_multiplier=0,
                              allow_small_or_imprecise_dtypes=True).then_inc(s_c, 1)
                    pool.iota(ioT[:, :], [[1, T]], base=0, channel_multiplier=0,
                              allow_small_or_imprecise_dtypes=True).then_inc(s_c, 1)
                    pool.memset(ident[:, :], 0.0).then_inc(s_tri, 1)
                    pool.memset(ones[:, :], 1.0).then_inc(s_tri, 1)
                    pool.wait_ge(s_tri, 2)
                    pool.affine_select(out=ident[:, :], in_=ident[:, :], compare_op=ALU.not_equal, fill=1.0, base=0,
                                       pattern=[[-1, P]], channel_multiplier=1).then_inc(s_c, 1)
                    pool.affine_select(out=tri[:, :], in_=ones[:, :], compare_op=ALU.is_gt, fill=0.0, base=0,
                                       pattern=[[1, P]], channel_multiplier=-1).then_inc(s_c, 1)

                @block.sync
                def _(sp):
                    for tile, a in ((dstI, dst), (srcI, src), (etI, etype)):
                        sp.dma_start(tile[:, :], a.rearrange("(p c) -> p c", p=EP)).then_inc(s_ld, 16)
                    sp.wait_ge(s_df, 2)
                    sp.dma_start(rec_d, dflt[:, :, :].rearrange("p t w -> p (t w)")).then_inc(s_def, 16)
                    sp.wait_ge(s_def, 16)

                @block.vector
                def _(dve):
                    link = Chain(dve, s_v)
                    dve.memset(zero[:, :], 0.0).then_inc(s_z, 1)
                    link(dve.memset(dflt[:, :, :], 0))
                    dve.memset(dflt[:, :, 2], int(NO_NODE)).then_inc(s_df, 2)
                    dve.wait_ge(s_ld, 48)
                    dve.wait_ge(s_c, 4)
                    dve.tensor_scalar(pay[:, :, 2], dstI[:, :], P - 1, None, ALU.bitwise_and)
                    dve.tensor_copy(pay[:, :, 3], dstI[:, :])
                    dve.tensor_copy(pay[:, :, 1], srcI[:, :])
                    dve.scalar_tensor_tensor(pay[:, :, 0], srcI[:, :], float(KT), etI[:, :], ALU.mult, ALU.add)
                    link(dve.tensor_scalar(tmpI[:, :], dstI[:, :], 7, None, ALU.arith_shift_right))
                    link(dve.tensor_copy(hiF[:, :], tmpI[:, :]))
                    def counted(n, h):
                        dve.tensor_scalar(m[h][:, :], hiF[:, :], iota[0:EP, bass.ds(n, 1)], None, ALU.is_equal, ALU.add,
                                          accum_out=cnt[:, bass.ds(n, 1)]).then_inc(s_cnt, 1)
                    for h in range(2):
                        counted(h, h)
                    with dve.Fori(1, NB // 2) as b:
                        for h in range(2):
                            dve.wait_ge(s_cnt, b * 2 + (h - 1))
                            counted(b * 2 + h, h)
                    dve.wait_ge(s_cs, 1)
                    link(dve.tensor_scalar(totI[:, :], ps[:, 1, 0:NB], float(P - 1), None, ALU.add))
                    dve.tensor_copy(pre[:, :], ps[0:EP, 0, 0:NB])
                    link(dve.tensor_scalar(totI[:, :], totI[:, :], 7, None, ALU.arith_shift_right))
                    link(dve.tensor_copy(nch[:, :], totI[:, :]))
                    link(dve.tensor_tensor_scan(cs[:, :], nch[:, :], zero[:, 0:NB], 0.0, ALU.add, ALU.add))
                    dve.tensor_tensor(cs[:, :], cs[:, :], nch[:, :], ALU.subtract).then_inc(s_base, 1)
                    dve.wait_ge(s_base, 1)
                    link(dve.scalar_tensor_tensor(base[0:EP, :], cs[0:EP, :], float(P), pre[:, :], ALU.mult, ALU.add))
                    link(dve.tensor_scalar(base[0:EP, :], base[0:EP, :], 1.0, None, ALU.subtract))
                    dve.wait_ge(s_bt, 1)
                    link(dve.tensor_copy(csT[:, :], ps[0:NBR, 0, 0:1]))
                    dve.tensor_scalar(reach[:, :], ioT[:, :], csT[:, 0:1], None, ALU.is_ge).then_inc(s_ge, 1)
                    dve.wait_ge(s_br, 1)
                    link(dve.tensor_scalar(blk64[:, :].rearrange("a (k n) -> a k n", k=4), psb[:, :, 0:T // 4],
                                           1.0, float(D), ALU.subtract, ALU.mult))

                @block.tensor
                def _(pe):
                    pe.wait_ge(s_cnt, NB)
                    pe.wait_ge(s_c, 4)
                    pe.matmul(ps[0:EP, 0, 0:NB], tri[0:EP, 0:EP], cnt[:, :], start=True, stop=True)
                    pe.matmul(ps[:, 1, 0:NB], ones[0:EP, :], cnt[:, :], start=True, stop=True).then_inc(s_cs, 1)
                    pe.wait_ge(s_base, 1)
                    pe.matmul(ps[0:NBR, 0, 0:1], cs[0:1, 0:NBR], ones[0:1, 0:1], start=True, stop=True).then_inc(s_bt, 1)
                    pe.wait_ge(s_ge, 1)
                    for k in range(4):
                        last = pe.matmul(psb[:, k, 0:T // 4], ones[0:NBR, 0:1], reach[:, k * (T // 4):(k + 1) * (T // 4)],
                                         start=True, stop=True)
                    last.then_inc(s_br, 1)

            with Phase() as p1:
                s_st = sems(p1, "b_staged0", "b_staged1")
                s_ft = sems(p1, "b_features0", "b_features1")
                s_sc = dma_sems("b_scattered0", "b_scattered1")
                s_fs = dma_sems("b_placed0", "b_placed1")
                s_hm = sems(p1, "b_hmarks0", "b_hmarks1")
                s_hu = sems(p1, "b_hused0", "b_hused1")
                s_rm = sems(p1, "b_rmarks0", "b_rmarks1")
                (s_tick, s_v, s_hst, s_tot, s_first, s_T, s_cT, s_E, s_M, s_U, s_cH, s_L, s_R, s_pos, s_en, s_seg) = sems(
                    p1, *("b_" + n for n in ("tick", "dve", "counts", "totals", "first", "turned", "turnedsb", "equal",
                                             "earlier", "counted", "countsb", "looked", "ranked", "positions", "ends",
                                             "slots")))
                posS = [sb(p1, f"posS{h}", [EP, SK], I32) for h in range(2)]
                payS = [sb(p1, f"payS{h}", [EP, SK, REC_W], I32) for h in range(2)]
                plS = [sb(p1, f"plS{h}", [EP, SK], I32) for h in range(2)]
                rowS = [sb(p1, f"rowS{h}", [EP, SK, SRT_W]) for h in range(2)]
                m, c, q, zr, posF = (sb(p1, n, [EP, max(SEGS)]) for n in ("m", "c", "q", "zr", "posF"))
                slo = sb(p1, "slo", [EP, EC])
                shi = sb(p1, "shi", [EP, EC])
                posF2 = sb(p1, "posF2", [EP, EC])
                posI2 = sb(p1, "posI2", [EP, EC], I32)
                ends = sb(p1, "ends", [EP, EC, 2])
                lo = [sb(p1, f"lo{h}", [EP, SK, P], BF16) for h in range(2)]
                hi = [sb(p1, f"hi{h}", [EP, SK, NB], BF16) for h in range(2)]
                identb = sb(p1, "identb", [P, P], BF16)
                lT = [sb(p1, f"lT{k}", [P, EP]) for k in range(2)]
                eq = [sb(p1, f"eq{k}", [EP, EP], BF16) for k in range(2)]
                hs = sb(p1, "hs", [P, NB])
                off = sb(p1, "off", [P, NB])
                junk = sb(p1, "junk", [EP, NB])
                ptt = [pb(p1, [P, 512]) for k in range(2)]
                peq = [pb(p1, [P, 512]) for k in range(2)]
                plk = [pb(p1, [P, 512]) for k in range(2)]
                pcn = pb(p1, [P, 512])
                ptm = pb(p1, [P, 512])
                block = p1.enter_context(nc.Block())
                av = attr.rearrange("(p c) f -> p c f", p=EP)

                @block.sync
                def _(sp):
                    def stage(h, at):
                        sp.dma_start(posS[h][:, :], posI[:, bass.ds(at, SK)]).then_inc(s_st[h], 16)
                        sp.dma_start(payS[h][:, :, :], pay[:, bass.ds(at, SK), :]).then_inc(s_st[h], 16)
                    sp.wait_ge(s_seg, 1)
                    for h in range(2):
                        stage(h, h * SK)
                    for seg, size in enumerate(SEGS):
                        sp.wait_ge(s_seg, seg + 1)
                        first = sum(SEGS[:seg]) // (2 * SK)
                        with sp.Fori(max(1, first), first + size // (2 * SK)) as i:
                            for h in range(2):
                                sp.wait_ge(s_sc[h], i * (16 * SK))
                                stage(h, i * (2 * SK) + h * SK)

                    def features(h, i):
                        at = i * (2 * SK) + h * SK
                        sp.dma_start(rowS[h][:, :, 0:FA], av[:, bass.ds(at, SK), :]).then_inc(s_ft[h], 16)
                        sp.dma_start(rowS[h][:, :, FA:SRT_W], ends[:, bass.ds(at, SK), :]).then_inc(s_ft[h], 16)
                        sp.wait_ge(s_pos, i * 2 + h + 1)
                        sp.dma_start(plS[h][:, :], posI2[:, bass.ds(at, SK)]).then_inc(s_ft[h], 16)
                    sp.wait_ge(s_en, 2)
                    for h in range(2):
                        features(h, 0)
                    with sp.Fori(1, SI) as i:
                        for h in range(2):
                            sp.wait_ge(s_fs[h], i * (16 * SK))
                            features(h, i)

                @block.gpsimd
                def _(pool):
                    with pool.Fori(0, SI) as i:
                        for h in range(2):
                            pool.wait_ge(s_st[h], (i + 1) * 32)
                            pool.sem_inc(s_tick, 1)
                            for j in range(SK):
                                pool.indirect_dma_start(
                                    rec_d.rearrange("p (t w) -> (p t) w", w=REC_W),
                                    bass.IndirectOffsetOnAxis(posS[h][:, j:j + 1], 0),
                                    payS[h][:, j, :], None).then_inc(s_sc[h], 16)
                    with pool.Fori(0, SI) as i:
                        for h in range(2):
                            pool.wait_ge(s_ft[h], (i + 1) * 48)
                            pool.sem_inc(s_tick, 1)
                            for j in range(SK):
                                pool.indirect_dma_start(
                                    srt_d, bass.IndirectOffsetOnAxis(plS[h][:, j:j + 1], 0),
                                    rowS[h][:, j, :], None).then_inc(s_fs[h], 16)
                    for h in range(2):
                        pool.wait_ge(s_sc[h], 16 * SK * SI)
                        pool.wait_ge(s_fs[h], 16 * SK * SI)

                @block.vector
                def _(dve):
                    link = Chain(dve, s_v)
                    dve.memset(zr[:, :], 0.0)
                    for seg, size in enumerate(SEGS):
                        cols = slice(sum(SEGS[:seg]), sum(SEGS[:seg + 1]))
                        link(dve.memset(posF[:, 0:size], 0.0))
                        n0 = link.base + link.n
                        with dve.Fori(0, NBR) as b:
                            link.enter(b, 4)
                            link(dve.tensor_scalar(m[:, 0:size], hiF[:, cols], iota[0:EP, bass.ds(b, 1)], None, ALU.is_equal))
                            link(dve.tensor_tensor_scan(c[:, 0:size], m[:, 0:size], zr[:, 0:size], base[0:EP, bass.ds(b, 1)],
                                                        ALU.add, ALU.add))
                            dve.tensor_tensor(q[:, 0:size], c[:, 0:size], m[:, 0:size], ALU.mult)
                            link(dve.tensor_copy(base[0:EP, bass.ds(b, 1)], c[:, size - 1:size]))
                            link(dve.tensor_tensor(posF[:, 0:size], posF[:, 0:size], q[:, 0:size], ALU.add))
                        link.leave(n0, NBR)
                        link(dve.tensor_copy(posI[:, cols], posF[:, 0:size]))
                        dve.tensor_scalar(tmpI[:, cols], posI[:, cols], P - 1, None, ALU.bitwise_and)
                        link(dve.tensor_scalar(posI[:, cols], posI[:, cols], 7, None, ALU.arith_shift_right))
                        dve.tensor_copy(c[:, 0:size], tmpI[:, cols])
                        link(dve.tensor_copy(q[:, 0:size], posI[:, cols]))
                        link(dve.scalar_tensor_tensor(posI[:, cols], c[:, 0:size], float(T), q[:, 0:size], ALU.mult, ALU.add))
                        dve.sem_inc(s_seg, 1)
                    dve.tensor_copy(ends[:, :, 0], dstI[:, :]).then_inc(s_en, 1)
                    dve.tensor_copy(ends[:, :, 1], srcI[:, :]).then_inc(s_en, 1)
                    dve.tensor_copy(identb[:, :], ident[:, :])
                    link(dve.tensor_scalar(tmpI[:, :], srcI[:, :], P - 1, None, ALU.bitwise_and))
                    link(dve.tensor_copy(slo[:, :], tmpI[:, :]))
                    link(dve.tensor_scalar(tmpI[:, :], srcI[:, :], 7, None, ALU.arith_shift_right))
                    link(dve.tensor_copy(shi[:, :], tmpI[:, :]))

                    def marks(h, at, ready):
                        dve.tensor_tensor(lo[h][:, :, :], across(iota[0:EP, :], SK),
                                          along(slo[:, bass.ds(at, SK)], P), ALU.is_equal).then_inc(ready[h], 1)
                        dve.tensor_tensor(hi[h][:, :, :], across(iota[0:EP, 0:NB], SK),
                                          along(shi[:, bass.ds(at, SK)], NB), ALU.is_equal).then_inc(ready[h], 1)
                    for h in range(2):
                        marks(h, h * SK, s_hm)
                    with dve.Fori(1, SI) as i:
                        for h in range(2):
                            dve.wait_ge(s_hu[h], i)
                            marks(h, i * (2 * SK) + h * SK, s_hm)
                    dve.wait_ge(s_hu[0], SI)
                    dve.wait_ge(s_hu[1], SI)
                    dve.tensor_copy(cn_src[:, :], pcn[:, 0:NB]).then_inc(s_hst, 1)
                    dve.wait_ge(s_tot, 1)
                    link(dve.tensor_copy(hs[:, :], ptm[:, 0:NB]))
                    link(dve.tensor_tensor_scan(off[:, :], hs[:, :], zero[:, 0:NB], 0.0, ALU.add, ALU.add))
                    link(dve.tensor_tensor(off[:, :], off[:, :], hs[:, :], ALU.subtract))
                    dve.tensor_tensor(st_src[:, :], off[:, :], ptm[:, 64:64 + NB], ALU.add).then_inc(s_first, 1)
                    marks(0, 0, s_rm)

                    def masked(k, n):
                        dve.wait_ge(s_E, n + 1)
                        dve.tensor_tensor(eq[k % 2][:, :], peq[k % 2][0:EP, 0:EP], tri[0:EP, 0:EP],
                                          ALU.mult).then_inc(s_M, 1)

                    def ranked(h, j, k, n):
                        dve.wait_ge(s_L, n + 1)
                        if not (isinstance(n, int) and n == 0):
                            dve.wait_ge(s_R, n)
                        dve.scalar_tensor_tensor(junk[:, :], plk[k % 2][0:EP, 0:NB], 1.0, hi[h][:, j, :], ALU.mult,
                                                 ALU.mult, accum_out=posF2[:, bass.ds(n, 1)]).then_inc(s_R, 1)

                    def placed(at):
                        dve.tensor_copy(posI2[:, bass.ds(at, SK)], posF2[:, bass.ds(at, SK)]).then_inc(s_pos, 1)

                    def half(i, h, first, more):
                        for j in range(SK):
                            k = h * SK + j
                            n = i * (2 * SK) + k
                            masked(k, n)
                            if not (first and k == 0):
                                if j == 0:
                                    ranked(1 - h, SK - 1, k + 1, n - 1)
                                    dve.wait_ge(s_R, n)
                                    if more:
                                        marks(1 - h, i * (2 * SK) + (h + 1) * SK, s_rm)
                                    placed(n - SK)
                                else:
                                    ranked(h, j - 1, k - 1, n - 1)
                            elif more:
                                marks(1, SK, s_rm)
                    half(0, 0, True, True)
                    half(0, 1, False, True)
                    with dve.Fori(1, SI - 1) as i:
                        half(i, 0, False, True)
                        half(i, 1, False, True)
                    half(SI - 1, 0, False, True)
                    half(SI - 1, 1, False, False)
                    ranked(1, SK - 1, 1, EC - 1)
                    dve.wait_ge(s_R, EC)
                    placed(EC - SK)

                @block.tensor
                def _(pe):
                    pe.matmul(pcn[:, :], zero[:, 0:P], zero[:, :], start=True, stop=True)
                    with pe.Fori(0, SI) as i:
                        for h in range(2):
                            pe.wait_ge(s_hm[h], (i + 1) * 2)
                            for j in range(SK):
                                last = pe.matmul(pcn[:, 0:NB], lo[h][:, j, :], hi[h][:, j, :], start=False, stop=True,
                                                 skip_group_check=True)
                            last.then_inc(s_hu[h], 1)
                    pe.wait_ge(s_hst, 1)
                    pe.matmul(ptm[:, 0:NB], ones[:, :], cn_src[:, :], start=True, stop=True)
                    pe.matmul(ptm[:, 64:64 + NB], tri[:, :], cn_src[:, :], start=True, stop=True).then_inc(s_tot, 1)
                    pe.wait_ge(s_first, 1)
                    pe.matmul(pcn[:, 0:NB], ident[:, :], st_src[:, :], start=True, stop=True).then_inc(s_U, 1)

                    def turned(k, h, j):
                        pe.transpose(ptt[k % 2].bitcast(BF16)[:, 0:EP], lo[h][:, j, :], identb[0:EP, 0:EP]).then_inc(s_T, 1)
                    pe.wait_ge(s_rm[0], 2)
                    turned(0, 0, 0)

                    def column(i, h, j, last):
                        k = h * SK + j
                        n = i * (2 * SK) + k
                        if not last:
                            if j == SK - 1:
                                pe.wait_ge(s_rm[1 - h], (i + 1 + h) * 2)
                            turned(k + 1, *((h, j + 1) if j < SK - 1 else (1 - h, 0)))
                        pe.wait_ge(s_cT, n + 1)
                        pe.matmul(peq[k % 2][0:EP, 0:EP], lT[k % 2][:, :], lT[k % 2][:, :], start=True,
                                  stop=True).then_inc(s_E, 1)
                        pe.wait_ge(s_cH, n + 1)
                        if not (isinstance(i, int) and i * (2 * SK) + k < 2):
                            pe.wait_ge(s_R, n - 1)
                        pe.matmul(plk[k % 2][0:EP, 0:NB], lT[k % 2][:, :], hs[:, :], start=True, stop=False)
                        pe.matmul(pcn[:, 0:NB], lo[h][:, j, :], hi[h][:, j, :], start=False, stop=True,
                                  skip_group_check=True).then_inc(s_U, 1)
                        pe.wait_ge(s_M, n + 1)
                        pe.matmul(plk[k % 2][0:EP, 0:NB], eq[k % 2][:, :], hi[h][:, j, :], start=False,
                                  stop=True).then_inc(s_L, 1)
                    for k in range(2 * SK):
                        column(0, k // SK, k % SK, False)
                    with pe.Fori(1, SI - 1) as i:
                        for k in range(2 * SK):
                            column(i, k // SK, k % SK, False)
                    for k in range(2 * SK):
                        column(SI - 1, k // SK, k % SK, k == 2 * SK - 1)

                @block.scalar
                def _(act):
                    with act.Fori(0, SI) as i:
                        for k in range(2 * SK):
                            n = i * (2 * SK) + k
                            act.wait_ge(s_T, n + 1)
                            act.activation(lT[k % 2][:, :], ptt[k % 2].bitcast(BF16)[:, 0:EP], ACT.Copy).then_inc(s_cT, 1)
                            act.wait_ge(s_U, n + 1)
                            act.activation(hs[:, :], pcn[:, 0:NB], ACT.Copy).then_inc(s_cH, 1)

        X = sb(top, "X", [P, NB, D])
        S = sb(top, "S", [P, NB, 2 * D])

        with Phase() as ph:
            (s_ld, s_v) = sems(ph, "c_load", "c_dve")
            rec = sb(ph, "rec", [P, T, REC_W], I32)
            block = ph.enter_context(nc.Block())

            @block.sync
            def _(sp):
                sp.dma_start(rec[:, :, :].rearrange("p t w -> p (t w)"), rec_d).then_inc(s_ld, 16)

            @block.vector
            def _(dve):
                dve.wait_ge(s_ld, 16)
                dve.tensor_copy(src4[:, :], rec[:, :, 0])
                dve.tensor_copy(srcr[:, :], rec[:, :, 1])
                dve.tensor_copy(dlo[:, :], rec[:, :, 2])

        def gather_pass(tag, table, idx, dots=None, side=None):
            width = D if dots is None else D + 2
            with Phase() as ph:
                s_st = sems(ph, tag + "staged0", tag + "staged1")
                s_got = dma_sems(tag + "rows0", tag + "rows1")
                s_oh = sems(ph, tag + "marks0", tag + "marks1")
                s_use = sems(ph, tag + "used0", tag + "used1")
                (s_tick, s_v, s_z, s_x) = sems(ph, tag + "tick", tag + "dve", tag + "scores", tag + "exp")
                idS = [sb(ph, f"idS{h}", [P, GK], I32) for h in range(2)]
                rows = [sb(ph, f"rows{h}", [P, GK, width]) for h in range(2)]
                mark = [sb(ph, f"mark{h}", [P, GK, P]) for h in range(2)]
                if dots is not None:
                    prod_ = sb(ph, "prod", [P, GK, P])
                    de = sb(ph, "de", [P, GK])
                    sc = sb(ph, "sc", [P, GK])
                acc = pb(ph, [P, 7 * 512])
                block = ph.enter_context(nc.Block())

                def loaded(engine, chunk):
                    return nc.values_load_multi_w_load_instructions(
                        blk64[0:1, bass.ds(chunk, GK)], engines=(engine,), min_val=0, max_val=(NBR - 1) * D)[1]

                @block.scalar
                def _(act):
                    for h in range(2):
                        act.activation(idS[h][:, :], idx[:, h * GK:(h + 1) * GK], ACT.Copy).then_inc(s_st[h], 1)

                    def exps(i, h):
                        if dots is not None:
                            act.wait_ge(s_z, i * 2 + h + 1)
                            act.activation(sc[:, :], sc[:, :], ACT.Exp).then_inc(s_x, 1)
                    exps(0, 0)

                    with act.Fori(0, GI - 1) as i:
                        for h in range(2):
                            act.wait_ge(s_use[h], i + 1)
                            act.activation(idS[h][:, :], idx[:, bass.ds(i * (2 * GK) + (2 + h) * GK, GK)],
                                           ACT.Copy).then_inc(s_st[h], 1)
                            exps(i + h, 1 - h)
                    exps(GI - 1, 1)
                    for h in range(2):
                        act.wait_ge(s_use[h], GI)
                    act.activation(S[:, 0:32, 0:D], acc[:, 0:32 * D].rearrange("p (b f) -> p b f", f=D), ACT.Copy)

                @block.gpsimd
                def _(pool):
                    with pool.Fori(0, GI) as i:
                        for h in range(2):
                            pool.wait_ge(s_st[h], i + 1)
                            pool.sem_inc(s_tick, 1)
                            for j in range(GK):
                                pool.indirect_dma_start(rows[h][:, j, :], None, table,
                                                        bass.IndirectOffsetOnAxis(idS[h][:, j:j + 1], 0)
                                                        ).then_inc(s_got[h], 16)

                @block.vector
                def _(dve):
                    link = Chain(dve, s_v)

                    def make(i, h):
                        at = i * (2 * GK) + h * GK
                        ins = dve.tensor_tensor(mark[h][:, :, :], across(iota[:, :], GK),
                                                along(dlo[:, bass.ds(at, GK)], P), ALU.is_equal)
                        if dots is None:
                            ins.then_inc(s_oh[h], 1)
                            return
                        link(ins)
                        blk = loaded(mybir.EngineType.DVE, at)
                        for j in range(GK):
                            last = dve.scalar_tensor_tensor(prod_[:, j, :], mark[h][:, j, :], 1.0,
                                                            dots[:, bass.ds(blk[j] * 2, P)], ALU.mult, ALU.mult,
                                                            accum_out=de[:, j:j + 1])
                        link(last)
                        dve.wait_ge(s_got[h], (i + 1) * (16 * GK))
                        link(dve.tensor_tensor(de[:, :], de[:, :], rows[h][:, :, D], ALU.add))
                        link(dve.scalar_tensor_tensor(sc[:, :], de[:, :], 0.2, de[:, :], ALU.mult, ALU.max))
                        link(dve.tensor_tensor(sc[:, :], sc[:, :], rows[h][:, :, D + 1], ALU.subtract))
                        dve.tensor_scalar(sc[:, :], sc[:, :], 0.0, None, ALU.min).then_inc(s_z, 1)
                        dve.wait_ge(s_x, i * 2 + h + 1)
                        dve.tensor_tensor(mark[h][:, :, :], mark[h][:, :, :], along(sc[:, :], P),
                                          ALU.mult).then_inc(s_oh[h], 1)
                    per = 0 if dots is None else 5
                    for h in range(2):
                        make(0, h)

                    def turn(i, beside):
                        for h in range(2):
                            dve.wait_ge(s_use[h], i + 1)
                            make(i + 1, h)
                            if beside and h == 0:
                                side.dve(dve, link, i)
                    first = 0
                    if side is not None:
                        side.before(dve, link)
                        turn(0, True)
                        n0 = link.base + link.n
                        with dve.Fori(1, side.turns) as i:
                            link.enter(i - 1, 2 * per + side.per)
                            turn(i, True)
                        link.leave(n0, side.turns - 1)
                        first = side.turns
                    n0 = link.base + link.n
                    with dve.Fori(first, GI - 1) as i:
                        link.enter(i - first, 2 * per)
                        turn(i, False)
                    link.leave(n0, GI - 1 - first)
                    for h in range(2):
                        dve.wait_ge(s_use[h], GI)
                    dve.tensor_copy(S[:, 32:NB, 0:D], acc[:, 32 * D:NB * D].rearrange("p (b f) -> p b f", f=D))

                @block.sync
                def _(sp):
                    if side is not None:
                        side.sp(sp)

                @block.tensor
                def _(pe):
                    for b in range(7):
                        pe.matmul(acc[:, b * 512:(b + 1) * 512], zero[:, 0:P], zero[:, :], start=True, stop=True)

                    with pe.Fori(0, GI) as i:
                        for h in range(2):
                            at = loaded(mybir.EngineType.PE, i * (2 * GK) + h * GK)
                            pe.wait_ge(s_oh[h], i + 1)
                            pe.wait_ge(s_got[h], (i + 1) * (16 * GK))
                            for j in range(GK):
                                last = pe.matmul(acc[:, bass.ds(at[j], D)], mark[h][:, j, :], rows[h][:, j, 0:D],
                                                 start=False, stop=True, skip_group_check=True)
                            last.then_inc(s_use[h], 1)

        def norm_tiles(st, tag):
            return [sb(st, tag + n, s) for n, s in (("t3", [P, NB, D]), ("m1", [P, NB]), ("v1", [P, NB]), ("sd", [P, NB]))]

        def norm_dve(dve, link, tiles, s_var, s_dev):
            t3, m1, v1, sd = tiles
            feat = S[:, :, D:2 * D]
            link(dve.tensor_reduce(m1[:, :], X[:, :, :], AX.X, ALU.add))
            link(dve.tensor_scalar(m1[:, :], m1[:, :], 1.0 / D, None, ALU.mult))
            link(dve.tensor_tensor(feat, X[:, :, :], along(m1[:, :], D), ALU.subtract))
            link(dve.tensor_tensor(t3[:, :, :], feat, feat, ALU.mult))
            link(dve.tensor_reduce(v1[:, :], t3[:, :, :], AX.X, ALU.add))
            dve.tensor_scalar(v1[:, :], v1[:, :], 1.0 / D, 1e-5, ALU.mult, ALU.add).then_inc(s_var, 1)
            dve.wait_ge(s_dev, 1)
            link(dve.reciprocal(sd[:, :], sd[:, :]))
            link(dve.tensor_scalar(feat, feat, 0.0, None, ALU.max))
            link(dve.tensor_tensor(feat, feat, along(sd[:, :], D), ALU.mult))

        def norm_act(act, tiles, s_var, s_dev):
            act.wait_ge(s_var, 1)
            act.activation(tiles[3][:, :], tiles[2][:, :], ACT.Sqrt).then_inc(s_dev, 1)

        dsrt = sb(top, "dsrt", [EP, EC])
        ssrt = sb(top, "ssrt", [EP, EC + 1])
        keep = sb(top, "keep", [EP, EC])
        keepM = sb(top, "keepM", [EP, EC])
        whole = sb(top, "whole", [EP, 1])
        endI = sb(top, "endI", [P, NB], I32)
        state = sb(top, "state", [EP, 2 * FA])

        def carries(bank_, dve, link, width, turned, rows_, back, rowT, contT, carryR, out_ap, sums):
            dve.wait_ge(*turned)
            link(dve.tensor_copy(rowT[:, :], bank_[0:width, 0:EP]))
            link(dve.tensor_copy(contT[:, :], bank_[0:width, 128:128 + EP]))
            if sums < width:
                link(dve.tensor_scalar(contT[sums:width, :], contT[sums:width, :], 2.0, 1.0, ALU.mult, ALU.subtract))
                link(dve.tensor_scalar(contT[sums:width, :], contT[sums:width, :], BIG, None, ALU.mult))
                link(dve.memset(carryR[sums:width, 0:1], -BIG))
                link(dve.tensor_tensor_scan(carryR[sums:width, 1:EP + 1], contT[sums:width, :], rowT[sums:width, :],
                                            -BIG, ALU.min, ALU.max))
            if sums:
                link(dve.memset(carryR[0:sums, 0:1], 0.0))
                link(dve.tensor_tensor_scan(carryR[0:sums, 1:EP + 1], contT[0:sums, :], rowT[0:sums, :],
                                            0.0, ALU.mult, ALU.add))
            dve.sem_inc(rows_[0], 1)
            dve.wait_ge(*back)
            link(dve.tensor_copy(out_ap, bank_[0:EP, 256:256 + width]))

        def carries_pe(pe, bank_, tails, cont, carryR, width, tail, turned, rows_, back):
            pe.wait_ge(*tail)
            pe.transpose(bank_[0:width, 0:EP], tails, ident[0:EP, 0:EP])
            pe.transpose(bank_[0:width, 128:128 + EP], cont, ident[0:EP, 0:EP]).then_inc(turned[0], 1)
            pe.wait_ge(*rows_)
            pe.transpose(bank_[0:EP, 256:256 + width], carryR[:, 0:EP], ident[0:width, 0:width]).then_inc(back[0], 1)

        class Scans:

            turns = EC // SLAB

            def __init__(self, st, rnd):
                self.rnd, self.per = rnd, (7 if rnd == 0 else 2)
                (self.s_in, self.s_us, self.s_wr, self.s_pv) = sems(st, *(f"k{rnd}_" + n for n in (
                    "slab", "used", "stored", "before")))
                self.slab = sb(st, "slab", [EP, SLAB, SRT_W])
                self.res = sb(st, "res", [EP, SLAB, 2 * FA])

            def sp(self, sp):
                sv = srt_d.rearrange("(p c) w -> p c w", p=EP)
                gv = seg_d.rearrange("(p c) w -> p (c w)", p=EP)
                if self.rnd == 0:
                    sp.dma_start(ssrt[1:EP, 0:1], sv[0:EP - 1, EC - 1, FA + 1:FA + 2],
                                 allow_slow_non_contiguous=True).then_inc(self.s_pv, 16)
                with sp.Fori(0, self.turns) as i:
                    sp.wait_ge(self.s_us, i + 1)
                    sp.dma_start(self.slab[:, :, :], sv[:, bass.ds(i * SLAB, SLAB), :]).then_inc(self.s_in, 16)
                    if self.rnd:
                        sp.wait_ge(self.s_us, i + 2)
                        sp.dma_start(gv[:, bass.ds(i * (SLAB * 2 * FA), SLAB * 2 * FA)],
                                     self.res[:, :, :].rearrange("p c w -> p (c w)")).then_inc(self.s_wr, 16)
                if self.rnd:
                    sp.wait_ge(self.s_wr, 16 * self.turns)

            def before(self, dve, link):
                dve.sem_inc(self.s_us, 1)
                if self.rnd == 0:
                    link(dve.memset(state[:, 0:FA], 0.0))
                    link(dve.memset(state[:, FA:2 * FA], -BIG))
                    link(dve.memset(ssrt[0:1, 0:1], -1.0))
                    dve.wait_ge(self.s_pv, 16)

            def dve(self, dve, link, i):
                slab, res = self.slab, self.res
                dve.wait_ge(self.s_in, 16 * (i + 1))
                at = i * SLAB
                now = bass.ds(at, SLAB)
                if self.rnd == 0:
                    link(dve.tensor_copy(dsrt[:, now], slab[:, :, FA]))
                    link(dve.tensor_copy(ssrt[:, bass.ds(at + 1, SLAB)], slab[:, :, FA + 1]))
                    link(dve.tensor_tensor(keep[:, now], ssrt[:, bass.ds(at + 1, SLAB)], ssrt[:, now], ALU.is_equal))
                    link(dve.tensor_scalar(keepM[:, now], keep[:, now], 2.0, 1.0, ALU.mult, ALU.subtract))
                    link(dve.tensor_scalar(keepM[:, now], keepM[:, now], BIG, None, ALU.mult))
                elif not isinstance(i, int):
                    dve.wait_ge(self.s_wr, 16 * i)
                for f in range(FA):
                    dve.tensor_tensor_scan(res[:, :, f], keep[:, now], slab[:, :, f], state[:, f:f + 1],
                                           ALU.mult, ALU.add)
                    last = dve.tensor_tensor_scan(res[:, :, FA + f], keepM[:, now], slab[:, :, f],
                                                  state[:, FA + f:FA + f + 1], ALU.min, ALU.max)
                link(last)
                link(dve.tensor_copy(state[:, :], res[:, SLAB - 1, :]))
                dve.sem_inc(self.s_us, 1)

        def bridge():
            with Phase() as ph:
                (s_v, s_tail, s_turn, s_row, s_back) = sems(ph, "v_dve", "v_tails", "v_turned", "v_rows", "v_back")
                contE = sb(ph, "contE", [EP, 2 * FA])
                rowT = sb(ph, "rowT", [2 * FA, EP])
                contT = sb(ph, "contT", [2 * FA, EP])
                carryR = sb(ph, "carryR", [2 * FA, EP + 1])
                fin = sb(ph, "fin", [P, NB])
                pc = pb(ph, [P, 512])
                block = ph.enter_context(nc.Block())

                @block.vector
                def _(dve):
                    link = Chain(dve, s_v)
                    link(dve.tensor_reduce(whole[:, :], keep[:, :], AX.X, ALU.min))
                    dve.tensor_copy(contE[:, :], whole[:, 0:1].broadcast_to((EP, 2 * FA))).then_inc(s_tail, 1)
                    carries(pc, dve, link, 2 * FA, (s_turn, 1), (s_row, 1), (s_back, 1), rowT, contT, carryR,
                            state[:, :], FA)
                    link(dve.tensor_tensor(fin[:, :], st_src[:, :], cn_src[:, :], ALU.add))
                    dve.tensor_scalar(endI[:, :], fin[:, :], 1.0, 0.0, ALU.subtract, ALU.max)

                @block.tensor
                def _(pe):
                    carries_pe(pe, pc, state[:, :], contE[:, :], carryR, 2 * FA, (s_tail, 1), (s_turn, 1),
                               (s_row, 1), (s_back, 1))

        l0 = ExitStack()
        with l0:
            Wg = sb(l0, "Wg", [P, 4 * D])
            Wt = sb(l0, "Wt", [P, KT * D])
            bg = sb(l0, "bg", [P, 4 * D])
            bt = sb(l0, "bt", [P, KT * D])
            with Phase() as ph:
                (s_ld, s_v, s_var, s_dev, s_z, s_tp, s_g) = sems(
                    ph, "d_load", "d_dve", "d_var", "d_dev", "d_zero", "d_transposed", "d_pool")
                raw = sb(ph, "raw", [P, 4, 2 * D])
                brow = sb(ph, "brow", [1, 3, 4 * D])
                tiles = norm_tiles(ph, "d_")
                psw = pb(ph, [P, 4, P])
                psr = pb(ph, [P, 2, 4 * D])
                block = ph.enter_context(nc.Block())

                @block.gpsimd
                def _(pool):
                    pool.memset(raw[:, :, :], 0.0).then_inc(s_z, 1)
                    pool.memset(brow[:, :, :], 0.0).then_inc(s_z, 1)
                    pool.memset(S[:, :, 0:D], 0.0)

                @block.sync
                def _(sp):
                    sp.wait_ge(s_g, 1)
                    sp.dma_start(X[:, 0:NBR - 1, :], x[0:(NBR - 1) * P, :].rearrange("(b p) f -> p b f", p=P)).then_inc(s_ld, 16)
                    sp.dma_start(X[0:N - (NBR - 1) * P, NBR - 1, :], x[(NBR - 1) * P:N, :]).then_inc(s_ld, 16)
                    sp.wait_ge(s_z, 2)
                    W0v = W0.rearrange("k h d -> (k h) d")
                    for dst_ap, src_ap in (
                            (raw[:, 0, 0:D], wih[0:2 * D, :]), (raw[:, 0, D:2 * D], whh[0:2 * D, :]),
                            (raw[0:D, 1, 0:D], wih[2 * D:3 * D, :]), (raw[D:2 * D, 1, D:2 * D], whh[2 * D:3 * D, :]),
                            (raw[:, 2, D:2 * D], W0v[0:P, :]), (raw[:, 3, D:2 * D], W0v[P:2 * P, :]),
                            (brow[:, 0, 0:3 * D], bih.rearrange("(a n) -> a n", a=1)),
                            (brow[:, 1, 0:2 * D], bhh[0:2 * D].rearrange("(a n) -> a n", a=1)),
                            (brow[:, 1, 3 * D:4 * D], bhh[2 * D:3 * D].rearrange("(a n) -> a n", a=1)),
                            (brow[:, 2, :], b0.rearrange("k h -> (k h)").rearrange("(a n) -> a n", a=1))):
                        sp.dma_start(dst_ap, src_ap).then_inc(s_ld, 16)

                @block.tensor
                def _(pe):
                    pe.wait_ge(s_ld, 12 * 16)
                    for k in range(4):
                        pe.transpose(psw[:, k, :], raw[:, k, :], ident[:, :])
                    pe.matmul(psr[:, 0, :], ones[0:1, :], brow[:, 0, :], start=True, stop=False)
                    pe.matmul(psr[:, 0, :], ones[0:1, :], brow[:, 1, :], start=False, stop=True)
                    pe.matmul(psr[:, 1, :], ones[0:1, :], brow[:, 2, :], start=True, stop=True).then_inc(s_tp, 1)

                @block.scalar
                def _(act):
                    norm_act(act, tiles, s_var, s_dev)

                @block.vector
                def _(dve):
                    link = Chain(dve, s_v)
                    dve.memset(X[:, NBR - 1:NB, :], 0.0).then_inc(s_g, 1)
                    dve.wait_ge(s_ld, 12 * 16)
                    norm_dve(dve, link, tiles, s_var, s_dev)
                    dve.wait_ge(s_tp, 1)
                    dve.tensor_copy(Wg[:, :].rearrange("p (k m) -> p k m", k=2), psw[:, 0:2, :])
                    dve.tensor_copy(Wt[:, :].rearrange("p (k m) -> p k m", k=2), psw[:, 2:4, :])
                    dve.tensor_copy(bg[:, :], psr[:, 0, :])
                    dve.tensor_copy(bt[:, :], psr[:, 1, :])

            def unit(tag, gated, messages):
                with Phase() as ph:
                    (s_in, s_t1, s_c1, s_gt, s_sm, s_sig, s_pre, s_tan, s_new, s_t2, s_c2, s_ms, s_mo, s_out, s_v) = sems(
                        ph, *(tag + n for n in ("staged", "turned", "sbuf", "gates", "biased", "sigmoid", "pretanh", "tanh",
                                                "feat", "turned2", "sbuf2", "msgs", "msgsb", "stored", "dve")))
                    stg = sb(ph, "stg", [P, LOT, 2 * D])
                    stT = sb(ph, "stT", [P, LOT, P])
                    stM = sb(ph, "stM", [P, LOT, P])
                    gb = sb(ph, "gb", [P, LOT, 4 * D])
                    nn = sb(ph, "nn", [P, LOT, D])
                    mo = sb(ph, "mo", [P, LOT, KT * D])
                    pst = pb(ph, [P, 8, P])
                    psg = pb(ph, [P, 6, 4 * D])
                    psm = pb(ph, [P, 6, 4 * D])
                    block = ph.enter_context(nc.Block())
                    mv = msg_d.rearrange("(b p k) f -> p b (k f)", p=P, k=KT)

                    @block.vector
                    def _(dve):
                        link = Chain(dve, s_v)

                        def biased(i):
                            dve.wait_ge(s_ms, i + 1)
                            if not (isinstance(i, int) and i == 0):
                                dve.wait_ge(s_out, i * 16)
                            dve.tensor_tensor(mo[:, :, :], psm[:, 0:LOT, :], across(bt[:, :], LOT),
                                              ALU.add).then_inc(s_mo, 1)

                        def turn(i, kind):
                            lot = bass.ds(i * LOT, LOT)
                            if messages and kind != "first":
                                dve.wait_ge(s_t2, i)
                            dve.tensor_copy(stg[:, :, :], S[:, lot, :]).then_inc(s_in, 1)
                            if gated:
                                dve.wait_ge(s_gt, i + 1)
                                dve.tensor_tensor(gb[:, :, :], psg[:, 0:LOT, :], across(bg[:, :], LOT),
                                                  ALU.add).then_inc(s_sm, 1)
                                dve.wait_ge(s_sig, i + 1)
                                link(dve.tensor_tensor(nn[:, :, :], gb[:, :, 0:D], gb[:, :, 3 * D:4 * D], ALU.mult))
                                dve.tensor_tensor(nn[:, :, :], nn[:, :, :], gb[:, :, 2 * D:3 * D],
                                                  ALU.add).then_inc(s_pre, 1)
                                dve.wait_ge(s_tan, i + 1)
                                link(dve.tensor_tensor(gb[:, :, 0:D], stg[:, :, D:2 * D], nn[:, :, :], ALU.subtract))
                                link(dve.tensor_tensor(gb[:, :, 0:D], gb[:, :, 0:D], gb[:, :, D:2 * D], ALU.mult))
                                link(dve.tensor_tensor(stg[:, :, D:2 * D], gb[:, :, 0:D], nn[:, :, :], ALU.add))
                                dve.tensor_copy(S[:, lot, D:2 * D], stg[:, :, D:2 * D]).then_inc(s_new, 1)
                                dve.wait_ge(s_new, i + 1)
                            if messages and kind != "first":
                                biased(0 if kind == "second" else i - 1)
                        turn(0, "first")
                        turn(1, "second")
                        n0 = link.base + link.n
                        with dve.Fori(2, NL) as i:
                            link.enter(i - 2, 4 if gated else 0)
                            turn(i, "")
                        link.leave(n0, NL - 2)
                        if messages:
                            biased(NL - 1)

                    @block.tensor
                    def _(pe):
                        def formed(i, first):
                            if not first:
                                pe.wait_ge(s_mo, i)
                            for k in range(LOT):
                                last = pe.matmul(psm[:, k, :], stM[:, k, :], Wt[:, :], start=True, stop=True)
                            last.then_inc(s_ms, 1)

                        def turn(i, kind):
                            pe.wait_ge(s_in, i + 1)
                            if messages and kind != "first":
                                pe.wait_ge(s_c2, i)
                            if gated:
                                for k in range(LOT):
                                    last = pe.transpose(pst[:, k, :], stg[:, k, :], ident[:, :])
                                last.then_inc(s_t1, 1)
                                pe.wait_ge(s_c1, i + 1)
                                for k in range(LOT):
                                    last = pe.matmul(psg[:, k, :], stT[:, k, :], Wg[:, :], start=True, stop=True)
                                last.then_inc(s_gt, 1)
                            if messages:
                                if kind != "first":
                                    formed(i - 1, kind == "second")
                                if gated:
                                    pe.wait_ge(s_new, i + 1)
                                for k in range(LOT):
                                    last = pe.transpose(pst[:, k, :], stg[:, k, :], ident[:, :])
                                last.then_inc(s_t2, 1)
                        turn(0, "first")
                        turn(1, "second")
                        with pe.Fori(2, NL) as i:
                            turn(i, "")
                        if messages:
                            pe.wait_ge(s_c2, NL)
                            formed(NL - 1, False)

                    @block.scalar
                    def _(act):
                        def turn(i, first):
                            if gated:
                                act.wait_ge(s_t1, i + 1)
                                act.activation(stT[:, :, :], pst[:, 0:LOT, :], ACT.Copy).then_inc(s_c1, 1)
                                act.wait_ge(s_sm, i + 1)
                                act.activation(gb[:, :, 0:2 * D], gb[:, :, 0:2 * D], ACT.Sigmoid).then_inc(s_sig, 1)
                                act.wait_ge(s_pre, i + 1)
                                act.activation(nn[:, :, :], nn[:, :, :], ACT.Tanh).then_inc(s_tan, 1)
                            if messages:
                                act.wait_ge(s_t2, i + 1)
                                if not first:
                                    act.wait_ge(s_ms, i)
                                act.activation(stM[:, :, :], pst[:, 0:LOT, :], ACT.Copy).then_inc(s_c2, 1)
                        turn(0, True)
                        with act.Fori(1, NL) as i:
                            turn(i, False)

                    @block.sync
                    def _(sp):
                        if messages:
                            with sp.Fori(0, NL) as i:
                                sp.wait_ge(s_mo, i + 1)
                                sp.dma_start(mv[:, bass.ds(i * LOT, LOT), :], mo[:, :, :]).then_inc(s_out, 16)
                            sp.wait_ge(s_out, NL * 16)

            unit("e_", False, True)
            for step in range(STEPS):
                with Phase() as ph:
                    gather_pass(f"f{step}_", msg_d, src4, side=Scans(ph, step) if step < 2 else None)
                if step == 0:
                    bridge()
                unit(f"g{step}_", True, step < STEPS - 1)
        with ExitStack() as late:
            l1 = late.enter_context(ExitStack())
            H = sb(l1, "H", [P, NB, D + 2])
            a_s = sb(l1, "a_s", [P, 2, NB])
            sm = sb(l1, "sm", [P, 2, NB])
            with Phase() as ph:
                (s_ld, s_z, s_v, s_var, s_dev, s_tp, s_w, s_in, s_t, s_c, s_h, s_hc) = sems(
                    ph, *("l_" + n for n in ("load", "zero", "dve", "var", "dev", "turned", "weights", "staged", "turned2",
                                             "sbuf", "products", "copied")))
                raw = sb(ph, "raw", [P, 2 * D])
                ar = sb(ph, "ar", [1, 2 * D])
                ab = sb(ph, "ab", [P, 2 * D])
                Wh = sb(ph, "Wh", [P, D])
                stg = sb(ph, "stg", [P, LOT, 2 * D])
                stT = sb(ph, "stT", [P, LOT, P])
                tiles = norm_tiles(ph, "l_")
                psw = pb(ph, [P, 512])
                pst = pb(ph, [P, 8, P])
                psh = pb(ph, [P, LOT, D])
                block = ph.enter_context(nc.Block())

                @block.gpsimd
                def _(pool):
                    pool.memset(raw[:, :], 0.0).then_inc(s_z, 1)

                @block.sync
                def _(sp):
                    sp.wait_ge(s_z, 1)
                    sp.dma_start(raw[0:D, D:2 * D], W1g).then_inc(s_ld, 16)
                    sp.dma_start(ar[:, :], a1).then_inc(s_ld, 16)

                @block.tensor
                def _(pe):
                    pe.wait_ge(s_ld, 32)
                    pe.transpose(psw[:, 0:P], raw[:, :], ident[:, :])
                    pe.matmul(psw[:, 128:128 + 2 * D], ones[0:1, :], ar[:, :], start=True, stop=True).then_inc(s_tp, 1)
                    pe.wait_ge(s_w, 1)
                    with pe.Fori(0, NL) as i:
                        pe.wait_ge(s_in, i + 1)
                        for k in range(LOT):
                            last = pe.transpose(pst[:, k, :], stg[:, k, :], ident[:, :])
                        last.then_inc(s_t, 1)
                        pe.wait_ge(s_c, i + 1)
                        for k in range(LOT):
                            last = pe.matmul(psh[:, k, :], stT[:, k, :], Wh[:, :], start=True, stop=True)
                        last.then_inc(s_h, 1)

                @block.scalar
                def _(act):
                    norm_act(act, tiles, s_var, s_dev)
                    with act.Fori(0, NL) as i:
                        act.wait_ge(s_t, i + 1)
                        act.activation(stT[:, :, :], pst[:, 0:LOT, :], ACT.Copy).then_inc(s_c, 1)

                @block.vector
                def _(dve):
                    link = Chain(dve, s_v)
                    link(dve.tensor_tensor(X[:, :, :], X[:, :, :], S[:, :, D:2 * D], ALU.add))
                    norm_dve(dve, link, tiles, s_var, s_dev)
                    dve.wait_ge(s_tp, 1)
                    dve.tensor_copy(ab[:, :], psw[:, 128:128 + 2 * D])
                    dve.tensor_copy(Wh[:, :], psw[:, 0:D]).then_inc(s_w, 1)
                    with dve.Fori(0, NL) as i:
                        lot = bass.ds(i * LOT, LOT)
                        dve.tensor_copy(stg[:, :, :], S[:, lot, :]).then_inc(s_in, 1)
                        dve.wait_ge(s_h, i + 1)
                        dve.tensor_copy(H[:, lot, 0:D], psh[:, :, :]).then_inc(s_hc, 1)
                    dve.wait_ge(s_hc, NL)
                    t3 = tiles[0]
                    for k in range(2):
                        link(dve.tensor_tensor(t3[:, :, :], H[:, :, 0:D], across(ab[:, k * D:(k + 1) * D], NB), ALU.mult))
                        link(dve.tensor_reduce(a_s[:, k, :], t3[:, :, :], AX.X, ALU.add))
                    link(dve.tensor_copy(sm[:, 0, :], a_s[:, 0, :]))

            dval = sb(l1, "dval", [EP, EC])
            with Phase() as ph:
                s_lo, s_T, s_C, s_L, s_R = (sems(ph, f"m_{n}0", f"m_{n}1") for n in (
                    "marks", "turned", "sbuf", "looked", "read"))
                (s_v, s_dot, s_key) = sems(ph, "m_dve", "m_products", "m_keys")
                s_gd = dma_sems("m_gathered0", "m_gathered1")
                s_ks = sems(ph, "m_staged0", "m_staged1")
                (s_tick, s_last) = sems(ph, "m_tick", "m_last")
                keyS = [sb(ph, f"keyS{h}", [EP, PK], I32) for h in range(2)]
                valS = [sb(ph, f"valS{h}", [EP, PK]) for h in range(2)]
                kG = sb(ph, "kG", [EP, LP], I32)
                kI = sb(ph, "kI", [EP, EC], I32)
                kJ = sb(ph, "kJ", [EP, EC], I32)
                klo = sb(ph, "klo", [EP, EC])
                khi = sb(ph, "khi", [EP, EC])
                identb = sb(ph, "identb", [P, P], BF16)
                lo = [sb(ph, f"lo{h}", [EP, LK, P], BF16) for h in range(2)]
                hi = [sb(ph, f"hi{h}", [EP, LK, NB], BF16) for h in range(4)]
                lT = [sb(ph, f"lT{h}", [P, LK, EP], BF16) for h in range(2)]
                rest = sb(ph, "rest", [P, NB])
                parts = sb(ph, "parts", [P, 3, NB], BF16)
                pr = sb(ph, "pr", [EP, LK, NB])
                ptt = [pb(ph, [P, 1024]) for h in range(2)]
                plk = [pb(ph, [P, 2, 512]) for h in range(2)]
                ptv = [t.bitcast(BF16).rearrange("p (k e) -> p k e", e=P) for t in ptt]
                block = ph.enter_context(nc.Block())

                @block.sync
                def _(sp):
                    sp.dma_start(dot_d.rearrange("(b p) -> p b", p=P), a_s[:, 1, :],
                                 allow_slow_non_contiguous=True).then_inc(s_dot, 16)
                    sp.wait_ge(s_dot, 16)
                    sp.wait_ge(s_key, 1)
                    for h in range(2):
                        sp.dma_start(keyS[h][:, :], kG[:, h * PK:(h + 1) * PK]).then_inc(s_ks[h], 16)
                    with sp.Fori(1, PI) as i:
                        for h in range(2):
                            at = i * (2 * PK) + h * PK
                            sp.wait_ge(s_gd[h], i * (16 * PK))
                            sp.dma_start(dval[:, bass.ds(at + (EC - LP - 2 * PK), PK)], valS[h][:, :]).then_inc(s_ks[h], 16)
                            sp.dma_start(keyS[h][:, :], kG[:, bass.ds(at, PK)]).then_inc(s_ks[h], 16)
                    for h in range(2):
                        at = EC - 2 * PK + h * PK
                        sp.wait_ge(s_gd[h], PI * (16 * PK))
                        sp.dma_start(dval[:, at:at + PK], valS[h][:, :]).then_inc(s_last, 16)
                    sp.wait_ge(s_last, 32)

                @block.gpsimd
                def _(pool):
                    pool.wait_ge(s_dot, 16)
                    with pool.Fori(0, PI) as i:
                        for h in range(2):
                            pool.wait_ge(s_ks[h], i * 32 + 16)
                            pool.sem_inc(s_tick, 1)
                            for j in range(PK):
                                pool.indirect_dma_start(valS[h][:, j:j + 1], None, dot_d.rearrange("(n a) -> n a", a=1),
                                                        bass.IndirectOffsetOnAxis(keyS[h][:, j:j + 1], 0)
                                                        ).then_inc(s_gd[h], 16)

                def step(i, q):
                    return q % 4, q % 2, i * 2 + (q // 2 + 1)

                @block.vector
                def _(dve):
                    link = Chain(dve, s_v)
                    dve.tensor_copy(kG[:, :], dsrt[:, EC - LP:EC]).then_inc(s_key, 1)
                    link(dve.tensor_copy(kI[:, :], dsrt[:, :]))
                    dve.tensor_scalar(kJ[:, :], kI[:, :], 7, None, ALU.arith_shift_right)
                    link(dve.tensor_scalar(kI[:, :], kI[:, :], P - 1, None, ALU.bitwise_and))
                    dve.tensor_copy(identb[:, :], ident[:, :])
                    dve.tensor_copy(klo[:, :], kI[:, :])
                    link(dve.tensor_copy(khi[:, :], kJ[:, :]))
                    link(dve.tensor_copy(parts[:, 0, :], a_s[:, 1, :]))
                    link(dve.tensor_tensor(rest[:, :], a_s[:, 1, :], parts[:, 0, :], ALU.subtract))
                    link(dve.tensor_copy(parts[:, 1, :], rest[:, :]))
                    link(dve.tensor_tensor(rest[:, :], rest[:, :], parts[:, 1, :], ALU.subtract))
                    link(dve.tensor_copy(parts[:, 2, :], rest[:, :]))

                    def marks(i, q):
                        h, g, n = step(i, q)
                        if not (isinstance(i, int) and i * 4 + q < 2):
                            dve.wait_ge(s_T[g], n - 1)
                        at = i * (4 * LK) + q * LK
                        dve.tensor_tensor(lo[g][:, :, :], across(iota[0:EP, :], LK), along(klo[:, bass.ds(at, LK)], P),
                                          ALU.is_equal).then_inc(s_lo[g], 1)
                        link(dve.tensor_tensor(hi[h][:, :, :], across(iota[0:EP, 0:NB], LK),
                                               along(khi[:, bass.ds(at, LK)], NB), ALU.is_equal))

                    def read(i, q):
                        h, g, n = step(i, q)
                        halves = "p (b k) w -> p b (k w)"
                        dve.wait_ge(s_L[g], n)
                        link(dve.tensor_tensor(pr[:, :, :].rearrange(halves, b=2), plk[g][0:EP, :, 0:LK // 2 * NB],
                                               hi[h][:, :, :].rearrange(halves, b=2), ALU.mult))
                        dve.sem_inc(s_R[g], 1)
                        link(dve.tensor_reduce(dval[:, bass.ds(i * (4 * LK) + q * LK, LK)], pr[:, :, :], AX.X, ALU.add))

                    def quarter(i, q, first=False, last=False):
                        if not last:
                            marks(i, q + 1)
                        if not first:
                            read(i, q - 1)
                    marks(0, 0)
                    for q in range(4):
                        quarter(0, q, first=q == 0)
                    n0 = link.base + link.n
                    with dve.Fori(1, LI - 1) as i:
                        link.enter(i - 1, 12)
                        for q in range(4):
                            quarter(i, q)
                    link.leave(n0, LI - 2)
                    for q in range(4):
                        quarter(LI - 1, q, last=q == 3)
                    read(LI - 1, 3)

                @block.tensor
                def _(pe):
                    def turned(i, q):
                        _, g, n = step(i, q)
                        pe.wait_ge(s_lo[g], n)
                        if not (isinstance(i, int) and i * 4 + q < 2):
                            pe.wait_ge(s_C[g], n - 1)
                        for k in range(LK):
                            last = pe.transpose(ptv[g][:, k, 0:EP], lo[g][:, k, :], identb[0:EP, 0:EP])
                        last.then_inc(s_T[g], 1)

                    def looked(i, q):
                        _, g, n = step(i, q)
                        pe.wait_ge(s_C[g], n)
                        if not (isinstance(i, int) and i * 4 + q < 2):
                            pe.wait_ge(s_R[g], n - 1)
                        for k in range(LK):
                            at = k % (LK // 2) * NB
                            for part in range(3):
                                last = pe.matmul(plk[g][0:EP, k // (LK // 2), at:at + NB], lT[g][:, k, :],
                                                 parts[:, part, :], start=part == 0, stop=part == 2)
                        last.then_inc(s_L[g], 1)
                    for q in range(4):
                        turned(0, q)
                        if q:
                            looked(0, q - 1)
                    with pe.Fori(1, LI) as i:
                        for q in range(4):
                            turned(i, q)
                            looked(i, q - 1)
                    looked(LI - 1, 3)

                @block.scalar
                def _(act):
                    def copied(i, q):
                        _, g, n = step(i, q)
                        if not (isinstance(i, int) and q < 2):
                            act.wait_ge(s_L[g], n - 1)
                        act.wait_ge(s_T[g], n)
                        act.activation(lT[g][:, :, :], ptv[g][:, :, 0:EP], ACT.Copy).then_inc(s_C[g], 1)
                    for q in range(4):
                        copied(0, q)
                    with act.Fori(1, LI) as i:
                        for q in range(4):
                            copied(i, q)

            dots = sb(l1, "dots", [P, NBR * P])
            with Phase() as ph:
                (s_v, s_tail, s_turn, s_row, s_back, s_mx, s_wr, s_z, s_zw, s_pr, s_pl, s_sc, s_ex, s_sm, s_sw, s_rw, s_rs,
                 s_id) = sems(
                    ph, *("n_" + n for n in ("dve", "tails", "turned", "rows", "back", "maxima", "stored", "zero", "zeroed",
                                             "pairs", "loaded", "scores", "exp", "sums", "sumsstored", "table",
                                             "tablestored", "nodes")))
                (s_g, s_p, s_g2) = dma_sems("n_largest", "n_placed", "n_summed")
                mx = sb(ph, "mx", [EP, EC])
                two = sb(ph, "two", [EP, EC, 2])
                se = sb(ph, "se", [EP, EC])
                me = sb(ph, "me", [EP, EC])
                c1 = sb(ph, "c1", [EP, 1])
                rowT = sb(ph, "rowT", [1, EP])
                contT = sb(ph, "contT", [1, EP])
                carryR = sb(ph, "carryR", [1, EP + 1])
                md = sb(ph, "md", [P, NB])
                md2 = sb(ph, "md2", [P, NB])
                has = sb(ph, "has", [P, NB])
                e5 = sb(ph, "e5", [P, NB])
                node = sb(ph, "node", [P, NB])
                pidx = sb(ph, "pidx", [P, NB], I32)
                pair = sb(ph, "pair", [P, NB, 2])
                den = sb(ph, "den", [P, NB])
                pc = pb(ph, [P, 512])
                block = ph.enter_context(nc.Block())

                @block.vector
                def _(dve):
                    link = Chain(dve, s_v)
                    dve.memset(two[:, :, :], 0.0).then_inc(s_z, 1)
                    link(dve.tensor_scalar(has[:, :], cn_src[:, :], 1.0, None, ALU.min))
                    dve.wait_ge(s_id, 1)
                    link(dve.tensor_scalar(node[:, :], node[:, :], float(E), None, ALU.add))
                    link(dve.tensor_tensor(md[:, :], st_src[:, :], node[:, :], ALU.subtract))
                    link(dve.tensor_tensor(md[:, :], md[:, :], has[:, :], ALU.mult))
                    link(dve.tensor_tensor(pidx[:, :], md[:, :], node[:, :], ALU.add))

                    def carried(n, tail_at, sums):
                        carries(pc, dve, link, 1, (s_turn, n), (s_row, n), (s_back, n), rowT, contT, carryR, c1[:, 0:1],
                                sums)
                    dve.tensor_tensor_scan(mx[:, :], keepM[:, :], dval[:, :], -BIG, ALU.min, ALU.max).then_inc(s_tail, 1)
                    carried(1, mx, 0)
                    dve.tensor_tensor_scan(mx[:, :], keepM[:, :], dval[:, :], c1[:, 0:1], ALU.min,
                                           ALU.max).then_inc(s_mx, 1)
                    dve.wait_ge(s_g, 16 * NBR)
                    link(dve.tensor_tensor(e5[:, 0:NBR], md2[:, 0:NBR], a_s[:, 0, 0:NBR], ALU.add))
                    link(dve.scalar_tensor_tensor(e5[:, 0:NBR], e5[:, 0:NBR], 0.2, e5[:, 0:NBR], ALU.mult, ALU.max))
                    link(dve.memset(sm[:, 1, :], 0.0))
                    link(dve.tensor_tensor(sm[:, 1, 0:NBR], e5[:, 0:NBR], has[:, 0:NBR], ALU.mult))
                    link(dve.tensor_copy(pair[:, :, 0], sm[:, 0, :]))
                    dve.tensor_copy(pair[:, :, 1], sm[:, 1, :]).then_inc(s_pr, 1)
                    dve.wait_ge(s_pl, 16)
                    for n, (v, to) in enumerate(((0, se), (1, me))):
                        dve.tensor_tensor_scan(to[:, :], keep[:, :], two[:, :, v], 0.0, ALU.mult, ALU.add).then_inc(s_tail, 1)
                        carried(2 + n, to, 1)
                        link(dve.tensor_tensor_scan(to[:, :], keep[:, :], two[:, :, v], c1[:, 0:1], ALU.mult, ALU.add))
                    link(dve.tensor_tensor(se[:, :], se[:, :], dval[:, :], ALU.add))
                    link(dve.scalar_tensor_tensor(se[:, :], se[:, :], 0.2, se[:, :], ALU.mult, ALU.max))
                    dve.tensor_tensor(se[:, :], se[:, :], me[:, :], ALU.subtract).then_inc(s_sc, 1)
                    dve.wait_ge(s_ex, 1)
                    dve.tensor_tensor_scan(mx[:, :], keep[:, :], se[:, :], 0.0, ALU.mult, ALU.add).then_inc(s_tail, 1)
                    carried(4, mx, 1)
                    dve.tensor_tensor_scan(mx[:, :], keep[:, :], se[:, :], c1[:, 0:1], ALU.mult, ALU.add).then_inc(s_sm, 1)
                    dve.wait_ge(s_g2, 16 * NBR)
                    link(dve.tensor_scalar(den[:, 0:NBR], den[:, 0:NBR], 0.5, None, ALU.max))
                    link(dve.reciprocal(den[:, 0:NBR], den[:, 0:NBR]))
                    link(dve.memset(den[:, NBR:NB], 1.0))
                    dve.tensor_tensor(H[:, :, 0:D], H[:, :, 0:D], along(den[:, :], D), ALU.mult)
                    link(dve.tensor_copy(H[:, :, D], sm[:, 0, :]))
                    link(dve.tensor_copy(H[:, :, D + 1], sm[:, 1, :]))
                    dve.sem_inc(s_rw, 1)

                @block.scalar
                def _(act):
                    act.wait_ge(s_sc, 1)
                    act.activation(se[:, :], se[:, :], ACT.Exp).then_inc(s_ex, 1)

                @block.tensor
                def _(pe):
                    for n, tile in enumerate((mx, se, me, mx)):
                        k = n + 1
                        carries_pe(pe, pc, tile[:, EC - 1:EC], whole[:, :], carryR, 1, (s_tail, k), (s_turn, k), (s_row, k),
                                   (s_back, k))

                @block.sync
                def _(sp):
                    sp.dma_start(dots[:, :], dot_d[0:NBR * P].rearrange("(a n) -> a n", a=1).broadcast_to((P, NBR * P))
                                 ).then_inc(s_rs, 16)
                    sp.wait_ge(s_z, 1)
                    sp.dma_start(two_d[0:E, :].rearrange("(p c) w -> p (c w)", p=EP),
                                 two[:, :, :].rearrange("p c w -> p (c w)")).then_inc(s_zw, 16)
                    sp.wait_ge(s_mx, 1)
                    sp.dma_start(mxd_d.rearrange("(p c) w -> p (c w)", p=EP), mx[:, :]).then_inc(s_wr, 16)
                    sp.wait_ge(s_p, 16 * NBR)
                    sp.dma_start(two[:, :, :].rearrange("p c w -> p (c w)"),
                                 two_d[0:E, :].rearrange("(p c) w -> p (c w)", p=EP)).then_inc(s_pl, 16)
                    sp.wait_ge(s_sm, 1)
                    sp.dma_start(sum_d.rearrange("(p c) w -> p (c w)", p=EP), mx[:, :]).then_inc(s_sw, 16)
                    sp.wait_ge(s_rw, 1)
                    sp.dma_start(att_d.rearrange("(b p) f -> p b f", p=P), H[:, :, :]).then_inc(s_rs, 16)
                    sp.wait_ge(s_rs, 32)

                @block.gpsimd
                def _(pool):
                    pool.iota(node[:, :], [[P, NB]], base=0, channel_multiplier=1,
                              allow_small_or_imprecise_dtypes=True).then_inc(s_id, 1)
                    pool.wait_ge(s_wr, 16)
                    for b in range(NBR):
                        pool.indirect_dma_start(md2[:, b:b + 1], None, mxd_d,
                                                bass.IndirectOffsetOnAxis(endI[:, b:b + 1], 0)).then_inc(s_g, 16)
                    pool.wait_ge(s_pr, 1)
                    pool.wait_ge(s_zw, 16)
                    for b in range(NBR):
                        pool.indirect_dma_start(two_d, bass.IndirectOffsetOnAxis(pidx[:, b:b + 1], 0),
                                                pair[:, b, :], None).then_inc(s_p, 16)
                    pool.wait_ge(s_sw, 16)
                    for b in range(NBR):
                        pool.indirect_dma_start(den[:, b:b + 1], None, sum_d,
                                                bass.IndirectOffsetOnAxis(endI[:, b:b + 1], 0)).then_inc(s_g2, 16)
            gather_pass("r_", att_d, srcr, dots)
            l1.close()

            with Phase() as ph:
                (s_v, s_var, s_dev, s_m, s_x, s_rows, s_wr) = sems(
                    ph, *("s_" + n for n in ("dve", "var", "dev", "below", "exp", "rows", "stored")))
                tiles = norm_tiles(ph, "s_")
                block = ph.enter_context(nc.Block())

                @block.vector
                def _(dve):
                    link = Chain(dve, s_v)
                    t3, left = tiles[0], S[:, :, 0:D]
                    dve.tensor_scalar(t3[:, :, :], left, 0.0, None, ALU.min).then_inc(s_m, 1)
                    link(dve.scalar_tensor_tensor(X[:, :, :], left, 0.0, X[:, :, :], ALU.max, ALU.add))
                    dve.wait_ge(s_x, 1)
                    link(dve.scalar_tensor_tensor(X[:, :, :], t3[:, :, :], -1.0, X[:, :, :], ALU.add, ALU.add))
                    norm_dve(dve, link, tiles, s_var, s_dev)
                    dve.sem_inc(s_rows, 1)

                @block.scalar
                def _(act):
                    act.wait_ge(s_m, 1)
                    act.activation(tiles[0][:, :, :], tiles[0][:, :, :], ACT.Exp).then_inc(s_x, 1)
                    norm_act(act, tiles, s_var, s_dev)

                @block.sync
                def _(sp):
                    sp.wait_ge(s_rows, 1)
                    sp.dma_start(row_d.rearrange("(b p) f -> p b f", p=P), S[:, :, D:2 * D]).then_inc(s_wr, 16)
                    sp.wait_ge(s_wr, 16)
            gather_pass("t_", row_d, srcr)

            with Phase() as ph:
                (s_ld, s_v, s_bt, s_f, s_t, s_c, s_h, s_r, s_o, s_g2, s_b) = sems(
                    ph, *("u_" + n for n in ("load", "dve", "bias", "features", "turned", "sbuf", "hidden", "relu", "out",
                                             "added", "biases")))
                (s_g,) = dma_sems("u_gathered")
                K3 = 3 * FA
                sg = sb(ph, "sg", [P, NB, 2 * FA])
                f3 = sb(ph, "f3", [P, NB, K3])
                has = sb(ph, "has", [P, NB])
                rc = sb(ph, "rc", [P, NB])
                w1 = sb(ph, "w1", [K3, HID])
                ur = sb(ph, "ur", [1, 1])
                wu = sb(ph, "wu", [1, HID])
                br = sb(ph, "br", [1, HID])
                w2 = sb(ph, "w2", [HID, D])
                b2r = sb(ph, "b2r", [1, D])
                b2b = sb(ph, "b2b", [P, D])
                b1c = sb(ph, "b1c", [HID, 1])
                stg = sb(ph, "stg", [P, LOT, K3])
                stT = sb(ph, "stT", [K3, LOT, P])
                hd = sb(ph, "hd", [P, LOT, P])
                psb = pb(ph, [P, 512])
                pst = pb(ph, [P, 8, P])
                psh = pb(ph, [P, 8, P])
                pso = pb(ph, [P, LOT, D])
                block = ph.enter_context(nc.Block())

                @block.gpsimd
                def _(pool):
                    for b in range(NBR):
                        pool.indirect_dma_start(sg[:, b, :], None, seg_d,
                                                bass.IndirectOffsetOnAxis(endI[:, b:b + 1], 0)).then_inc(s_g, 16)

                @block.sync
                def _(sp):
                    for dst_ap, src_ap in ((w1[:, :], W13[0:K3, :]), (wu[:, :], W13[K3:K3 + 1, :]), (w2[:, :], W23),
                                           (br[:, :], b13.rearrange("(a n) -> a n", a=1)), (ur[:, :], u3[0:1, :]),
                                           (b2r[:, :], b23.rearrange("(a n) -> a n", a=1))):
                        sp.dma_start(dst_ap, src_ap).then_inc(s_ld, 16)

                @block.vector
                def _(dve):
                    link = Chain(dve, s_v)
                    link(dve.tensor_tensor(X[:, :, :], X[:, :, :], S[:, :, 0:D], ALU.add))
                    dve.tensor_scalar(has[:, :], cn_src[:, :], 1.0, None, ALU.min)
                    link(dve.tensor_scalar(rc[:, :], cn_src[:, :], 1.0, None, ALU.max))
                    link(dve.reciprocal(rc[:, :], rc[:, :]))
                    link(dve.memset(f3[:, NBR:NB, :], 0.0))
                    dve.wait_ge(s_g, 16 * NBR)
                    link(dve.tensor_tensor(f3[:, 0:NBR, 0:2 * FA], sg[:, 0:NBR, :], along(has[:, 0:NBR], 2 * FA), ALU.mult))
                    link(dve.tensor_tensor(f3[:, 0:NBR, 2 * FA:K3], f3[:, 0:NBR, 0:FA], along(rc[:, 0:NBR], FA), ALU.mult))
                    dve.wait_ge(s_bt, 1)
                    dve.tensor_copy(b1c[:, :], psb[:, 0:1])
                    dve.tensor_copy(b2b[:, :], psb[:, 8:8 + D]).then_inc(s_b, 1)
                    dve.wait_ge(s_b, 1)
                    n0 = link.base + link.n
                    with dve.Fori(0, NL) as i:
                        link.enter(i, 1)
                        lot = bass.ds(i * LOT, LOT)
                        dve.tensor_copy(stg[:, :, :], f3[:, lot, :]).then_inc(s_f, 1)
                        link(dve.tensor_tensor(X[:, lot, :], X[:, lot, :], across(b2b[:, :], LOT), ALU.add))
                        dve.wait_ge(s_o, i + 1)
                        dve.tensor_tensor(X[:, lot, :], X[:, lot, :], pso[:, :, :], ALU.add).then_inc(s_g2, 1)
                    link.leave(n0, NL)

                @block.tensor
                def _(pe):
                    pe.wait_ge(s_ld, 6 * 16)
                    pe.matmul(psb[:, 0:1], br[:, :], ones[0:1, 0:1], start=True, stop=False)
                    pe.matmul(psb[:, 0:1], wu[:, :], ur[:, :], start=False, stop=True)
                    pe.matmul(psb[:, 8:8 + D], ones[0:1, :], b2r[:, :], start=True, stop=True).then_inc(s_bt, 1)
                    with pe.Fori(0, NL) as i:
                        pe.wait_ge(s_f, i + 1)
                        for k in range(LOT):
                            last = pe.transpose(pst[0:K3, k, :], stg[:, k, :], ident[:, :])
                        last.then_inc(s_t, 1)
                        pe.wait_ge(s_c, i + 1)
                        for k in range(LOT):
                            last = pe.matmul(psh[:, k, :], w1[:, :], stT[:, k, :], start=True, stop=True)
                        last.then_inc(s_h, 1)
                        pe.wait_ge(s_r, i + 1)
                        for k in range(LOT):
                            last = pe.matmul(pso[:, k, :], hd[:, k, :], w2[:, :], start=True, stop=True)
                        last.then_inc(s_o, 1)

                @block.scalar
                def _(act):
                    act.wait_ge(s_b, 1)
                    with act.Fori(0, NL) as i:
                        act.wait_ge(s_t, i + 1)
                        act.activation(stT[:, :, :], pst[0:K3, 0:LOT, :], ACT.Copy).then_inc(s_c, 1)
                        act.wait_ge(s_h, i + 1)
                        act.activation(hd[:, :, :], psh[:, 0:LOT, :], ACT.Relu, bias=b1c[:, 0:1]).then_inc(s_r, 1)

        with Phase() as ph:
            (s_out,) = sems(ph, "z_out")
            block = ph.enter_context(nc.Block())

            @block.sync
            def _(sp):
                sp.dma_start(out[0:(NBR - 1) * P, :].rearrange("(b p) f -> p b f", p=P), X[:, 0:NBR - 1, :]).then_inc(s_out, 16)
                sp.dma_start(out[(NBR - 1) * P:N, :], X[0:N - (NBR - 1) * P, NBR - 1, :]).then_inc(s_out, 16)
                sp.wait_ge(s_out, 32)


_INS = ["x", "src", "dst", "edge_attr_32", "edge_type_4", "L0_gnn_W", "L0_gnn_b", "L0_gnn_w_ih", "L0_gnn_w_hh",
        "L0_gnn_b_ih", "L0_gnn_b_hh", "L1_gnn_W", "L1_gnn_a", "L3_gnn_u", "L3_gnn_W1", "L3_gnn_b1", "L3_gnn_W2",
        "L3_gnn_b2"]


def kernel(**inputs):
    import numpy as np
    import concourse.bacc as bacc
    from concourse.bass_utils import run_bass_kernel_spmd

    nc = bacc.Bacc("TRN2", target_bir_lowering=False, num_devices=1)
    arrays, args = {}, []
    for name in _INS:
        a = np.ascontiguousarray(inputs[name])
        arrays[f"in_{name}"] = a
        args.append(nc.dram_tensor(f"in_{name}", a.shape, mybir.dt.from_np(a.dtype), kind="ExternalInput").ap())
    args.append(nc.dram_tensor("out_x", (N, D), F32, kind="ExternalOutput").ap())
    build(nc, *args)
    r = run_bass_kernel_spmd(nc, [arrays], core_ids=[0])
    return r.results[0]["out_x"]
```
